# Optimizing a Trainium2 kernel written in Bass

```python
import numpy as np
import jax
import jax.numpy as jnp

def _softmax(x, axis=-1):
    return jax.nn.softmax(x, axis=axis)

def _gelu(x):
    return jax.nn.gelu(x, approximate=True)

def _silu(x):
    return jax.nn.silu(x)

def _sigmoid(x):
    return jax.nn.sigmoid(x)

def _layernorm(x, axis=-1, eps=1e-05):
    m = jnp.mean(x, axis=axis, keepdims=True)
    v = jnp.var(x, axis=axis, keepdims=True)
    return (x - m) / jnp.sqrt(v + eps)

def _scatter_add(tgt, idx, src, axis=0):
    return tgt.at[idx].add(src)

def _segment_sum(src, seg, n):
    return jax.ops.segment_sum(src, seg, n)
kernel_name = 'mk_adaln_ffn_d2_seqx_r8_e13ecf'

def setup_inputs(seed: int=0):
    np.random.seed(seed)
    _w = jnp.asarray

    def _rec_inputs():
        import jax
        import jax.numpy as jnp
        _rk = jax.random.key(seed)
        x = -0.000125 + 0.9999 * jax.random.normal(jax.random.fold_in(_rk, 1), (128, 32, 512), jnp.float32)
        _lenS = 32 - jax.random.randint(jax.random.fold_in(_rk, 7), (128,), 0, max(1, 32 // 4) + 1, jnp.int32)
        _lenS2 = 32 - jax.random.randint(jax.random.fold_in(_rk, 8), (128,), 0, max(1, 32 // 4) + 1, jnp.int32)
        cond_128 = 0.0061147 + 1.02565 * jax.random.normal(jax.random.fold_in(_rk, 11), (128, 128), jnp.float32)
        fside_S_0 = -0.022604 + 0.987366 * jax.random.normal(jax.random.fold_in(_rk, 12), (32,), jnp.float32)
        return (x, cond_128, fside_S_0)
    x, cond_128, fside_S_0 = _rec_inputs()

    def _L0_cond_setup():
        import jax, jax.numpy as jnp
        import numpy as np
        K = 8
        T = 1.0
        D_EMBD = 128
        IN_C = 32
        OUT_C = 32
        BS = 32
        H = 512
        HID = 128
        key = jax.random.key(seed)
        ks = jax.random.split(key, 10)
        s = lambda fan_in: 1.0 / np.sqrt(fan_in)
        return {'x': jax.random.normal(ks[0], (BS, IN_C, H), dtype=jnp.float32), 'embedding': jax.random.normal(ks[1], (BS, D_EMBD), dtype=jnp.float32), 'W0': jax.random.normal(ks[2], (D_EMBD, HID), dtype=jnp.float32) * s(D_EMBD), 'b0': jnp.zeros((HID,), dtype=jnp.float32), 'W1': jax.random.normal(ks[3], (HID, HID), dtype=jnp.float32) * s(HID), 'b1': jnp.zeros((HID,), dtype=jnp.float32), 'W2': jax.random.normal(ks[4], (HID, K), dtype=jnp.float32) * s(HID), 'b2': jnp.zeros((K,), dtype=jnp.float32), 'weight': jax.random.normal(ks[5], (K, OUT_C, IN_C, 1), dtype=jnp.float32) * s(IN_C), 'bias_k': jax.random.normal(ks[6], (K, OUT_C), dtype=jnp.float32) * 0.1}
    _L0_cond_all = _L0_cond_setup()
    _L0_cond_in = {k: v for k, v in _L0_cond_all.items() if k in ('W0', 'b0', 'W1', 'b1', 'W2', 'b2', 'weight', 'bias_k')}
    del _L0_cond_all

    def _L0_ffn_setup():
        import jax, jax.numpy as jnp
        import numpy as np
        LORA_R = 16
        SCALE = 16.0 / np.sqrt(16.0)
        NUM_EXPERTS = 4
        TOP_K = 2
        IN_F = 512
        OUT_F = 512
        key = jax.random.key(seed)
        k_x, k_a, k_b, k_r = jax.random.split(key, 4)
        x = jax.random.normal(k_x, (2, 256, IN_F), dtype=jnp.float32)
        A = jax.random.normal(k_a, (NUM_EXPERTS, LORA_R, IN_F), dtype=jnp.float32) * (1.0 / np.sqrt(IN_F))
        B = jax.random.normal(k_b, (NUM_EXPERTS, OUT_F, LORA_R), dtype=jnp.float32) * 0.02
        Wr = jax.random.normal(k_r, (NUM_EXPERTS, IN_F), dtype=jnp.float32) * 0.02
        return {'x': x, 'A': A, 'B': B, 'Wr': Wr}
    _L0_ffn_all = _L0_ffn_setup()
    _L0_ffn_in = {k: v for k, v in _L0_ffn_all.items() if k in ('A', 'B', 'Wr')}
    del _L0_ffn_all

    def _L1_cond_setup():
        import jax, jax.numpy as jnp
        import numpy as np
        from jax import lax
        N, C_IN, L = (32, 32, 512)
        C_OUT, K, GROUPS = (32, 9, 4)
        C_DIM, PAD, STRIDE = (128, 4, 1)
        key = jax.random.key(seed)
        k1, k2, k3, k4, k5 = jax.random.split(key, 5)
        x = jax.random.normal(k1, (N, C_IN, L), dtype=jnp.float32)
        c = jax.random.normal(k2, (N, C_DIM), dtype=jnp.float32)
        weight = jax.random.normal(k3, (C_OUT, C_IN // GROUPS, K), dtype=jnp.float32)
        c_weight = jax.random.normal(k4, (C_OUT, C_DIM), dtype=jnp.float32)
        bias = jax.random.normal(k5, (C_OUT,), dtype=jnp.float32)
        return {'x': x, 'c': c, 'weight': weight, 'c_weight': c_weight, 'bias': bias}
    _L1_cond_all = _L1_cond_setup()
    _L1_cond_in = {k: v for k, v in _L1_cond_all.items() if k in ('weight', 'c_weight')}
    del _L1_cond_all

    def _L1_ffn_setup():
        import jax, jax.numpy as jnp
        import numpy as np
        BLOCK = 32
        WBITS = 4
        ABITS = 16

        def _ste(x, dq):
            return x + jax.lax.stop_gradient(dq - x)

        def block_qdq_weight(w, block=BLOCK, bits=WBITS):
            out_f, in_f = w.shape
            wb = w.reshape(out_f, in_f // block, block)
            qmax = 2 ** (bits - 1) - 1
            scale = jnp.maximum(jnp.max(jnp.abs(wb), axis=-1, keepdims=True) / qmax, 1e-12)
            wq = jnp.clip(jnp.round(wb / scale), -qmax - 1, qmax) * scale
            return _ste(w, wq.reshape(out_f, in_f))

        def act_qdq(x, bits=ABITS):
            qmax = 2 ** bits - 1
            mn = jnp.minimum(jnp.min(x), 0.0)
            mx = jnp.maximum(jnp.max(x), 0.0)
            scale = jnp.maximum((mx - mn) / qmax, 1e-12)
            zp = jnp.clip(jnp.round(-mn / scale), 0, qmax)
            q = jnp.clip(jnp.round(x / scale) + zp, 0, qmax)
            return _ste(x, (q - zp) * scale)

        def fixed_qdq(x, scale, zp=0.0, bits=ABITS):
            qmax = 2 ** bits - 1
            q = jnp.clip(jnp.round(x / scale) + zp, 0, qmax)
            return _ste(x, (q - zp) * scale)
        key = jax.random.key(seed)
        k1, k2, k3, k4 = jax.random.split(key, 4)
        H, I = (512, 1376)
        x = jax.random.normal(k1, (2, 256, H), dtype=jnp.float32)
        w_gate = jax.random.normal(k2, (I, H), dtype=jnp.float32) * H ** (-0.5)
        w_up = jax.random.normal(k3, (I, H), dtype=jnp.float32) * H ** (-0.5)
        w_down = jax.random.normal(k4, (H, I), dtype=jnp.float32) * I ** (-0.5)
        return {'x': x, 'w_gate': w_gate, 'w_up': w_up, 'w_down': w_down}
    _L1_ffn_all = _L1_ffn_setup()
    _L1_ffn_in = {k: v for k, v in _L1_ffn_all.items() if k in ('w_gate', 'w_up', 'w_down')}
    del _L1_ffn_all
    return {'x': x, 'cond_128': cond_128, 'fside_S_0': fside_S_0, 'L0_cond_W0': _L0_cond_in['W0'], 'L0_cond_b0': _L0_cond_in['b0'], 'L0_cond_W1': _L0_cond_in['W1'], 'L0_cond_b1': _L0_cond_in['b1'], 'L0_cond_W2': _L0_cond_in['W2'], 'L0_cond_b2': _L0_cond_in['b2'], 'L0_cond_weight': _L0_cond_in['weight'], 'L0_cond_bias_k': _L0_cond_in['bias_k'], 'L0_ffn_A': _L0_ffn_in['A'], 'L0_ffn_B': _L0_ffn_in['B'], 'L0_ffn_Wr': _L0_ffn_in['Wr'], 'L1_cond_weight': _L1_cond_in['weight'], 'L1_cond_c_weight': _L1_cond_in['c_weight'], 'L1_ffn_w_gate': _L1_ffn_in['w_gate'], 'L1_ffn_w_up': _L1_ffn_in['w_up'], 'L1_ffn_w_down': _L1_ffn_in['w_down']}

def reference(x, cond_128, fside_S_0, L0_cond_W0, L0_cond_b0, L0_cond_W1, L0_cond_b1, L0_cond_W2, L0_cond_b2, L0_cond_weight, L0_cond_bias_k, L0_ffn_A, L0_ffn_B, L0_ffn_Wr, L1_cond_weight, L1_cond_c_weight, L1_ffn_w_gate, L1_ffn_w_up, L1_ffn_w_down):
    import jax
    import jax.numpy as jnp

    def _L0_cond_ref(x, embedding, W0, b0, W1, b1, W2, b2, weight, bias_k):
        import jax, jax.numpy as jnp
        import numpy as np
        K = 8
        T = 1.0
        D_EMBD = 128
        IN_C = 32
        OUT_C = 32
        BS = 32
        H = 512
        HID = 128
        h = jax.nn.gelu(embedding @ W0 + b0, approximate=False)
        h = jax.nn.gelu(h @ W1 + b1, approximate=False)
        att = jax.nn.softmax((h @ W2 + b2) / T, axis=-1)
        agg_w = jnp.einsum('bk,koi->boi', att, weight[..., 0])
        agg_b = att @ bias_k
        out = jnp.einsum('boi,bih->boh', agg_w, x) + agg_b[:, :, None]
        return out

    def _L0_ffn_ref(x, A, B, Wr):
        import jax, jax.numpy as jnp
        import numpy as np
        LORA_R = 16
        SCALE = 16.0 / np.sqrt(16.0)
        NUM_EXPERTS = 4
        TOP_K = 2
        IN_F = 512
        OUT_F = 512
        orig_shape = x.shape
        flat = x.reshape(-1, orig_shape[-1])
        logits = flat @ Wr.T
        topk_vals, topk_idx = jax.lax.top_k(logits, TOP_K)
        T = flat.shape[0]
        neg_inf = jnp.finfo(logits.dtype).min
        sparse = jnp.full_like(logits, neg_inf)
        rows = jnp.arange(T)[:, None]
        sparse = sparse.at[rows, topk_idx].set(topk_vals)
        gates = jax.nn.softmax(sparse, axis=-1)
        mid = jnp.einsum('tf,erf->ter', flat, A)
        all_deltas = jnp.einsum('ter,eor->teo', mid, B) * SCALE
        delta = jnp.sum(gates[:, :, None] * all_deltas, axis=1)
        return delta.reshape(*orig_shape[:-1], -1)

    def _L1_cond_ref(x, c, weight, c_weight, bias):
        import jax, jax.numpy as jnp
        import numpy as np
        from jax import lax
        N, C_IN, L = (32, 32, 512)
        C_OUT, K, GROUPS = (32, 9, 4)
        C_DIM, PAD, STRIDE = (128, 4, 1)
        out = lax.conv_general_dilated(x, weight, window_strides=(STRIDE,), padding=[(PAD, PAD)], dimension_numbers=('NCH', 'OIH', 'NCH'), feature_group_count=GROUPS)
        ctx = jnp.einsum('nd,od->no', c, c_weight)
        out = out + ctx[:, :, None] + bias[None, :, None]
        return out

    def _L1_ffn_ref(x, w_gate, w_up, w_down):
        import jax, jax.numpy as jnp
        import numpy as np
        BLOCK = 32
        WBITS = 4
        ABITS = 16

        def _ste(x, dq):
            return x + jax.lax.stop_gradient(dq - x)

        def block_qdq_weight(w, block=BLOCK, bits=WBITS):
            out_f, in_f = w.shape
            wb = w.reshape(out_f, in_f // block, block)
            qmax = 2 ** (bits - 1) - 1
            scale = jnp.maximum(jnp.max(jnp.abs(wb), axis=-1, keepdims=True) / qmax, 1e-12)
            wq = jnp.clip(jnp.round(wb / scale), -qmax - 1, qmax) * scale
            return _ste(w, wq.reshape(out_f, in_f))

        def act_qdq(x, bits=ABITS):
            qmax = 2 ** bits - 1
            mn = jnp.minimum(jnp.min(x), 0.0)
            mx = jnp.maximum(jnp.max(x), 0.0)
            scale = jnp.maximum((mx - mn) / qmax, 1e-12)
            zp = jnp.clip(jnp.round(-mn / scale), 0, qmax)
            q = jnp.clip(jnp.round(x / scale) + zp, 0, qmax)
            return _ste(x, (q - zp) * scale)

        def fixed_qdq(x, scale, zp=0.0, bits=ABITS):
            qmax = 2 ** bits - 1
            q = jnp.clip(jnp.round(x / scale) + zp, 0, qmax)
            return _ste(x, (q - zp) * scale)
        sigmoid_scale = 1.0 / 65536.0
        wg = block_qdq_weight(w_gate)
        wu = block_qdq_weight(w_up)
        wd = block_qdq_weight(w_down)
        xq = act_qdq(x)
        up = act_qdq(jnp.einsum('bsh,ih->bsi', xq, wu))
        gate = act_qdq(jnp.einsum('bsh,ih->bsi', xq, wg))
        sig = fixed_qdq(jax.nn.sigmoid(gate), sigmoid_scale)
        gate = act_qdq(gate * sig)
        o = act_qdq(gate * up)
        return jnp.einsum('bsi,hi->bsh', o, wd)
    x = x + _L0_ffn_ref(_L0_cond_ref(x, cond_128, L0_cond_W0, L0_cond_b0, L0_cond_W1, L0_cond_b1, L0_cond_W2, L0_cond_b2, L0_cond_weight, L0_cond_bias_k), L0_ffn_A, L0_ffn_B, L0_ffn_Wr)
    x = x + _L1_ffn_ref(_L1_cond_ref(x, cond_128, L1_cond_weight, L1_cond_c_weight, fside_S_0), L1_ffn_w_gate, L1_ffn_w_up, L1_ffn_w_down)
    return x

_drawn_inputs = setup_inputs


def setup_inputs(seed=0):
    import zlib

    import numpy as np

    out = dict(_drawn_inputs(seed))
    spreads = {'L0_cond_b0': (0.0, 2.0), 'L0_cond_b1': (0.0, 0.639), 'L0_cond_b2': (0.0, 0.73)}
    factors = {'L0_cond_bias_k': 5.676}
    for name, (base, spread) in spreads.items():
        noise = np.random.default_rng([zlib.crc32(name.encode()), seed]).standard_normal(out[name].shape)
        drawn = base * np.exp(spread * noise) if base else spread * noise
        out[name] = jnp.asarray(drawn.astype(out[name].dtype))
    for name, factor in factors.items():
        out[name] = (out[name] * factor).astype(out[name].dtype)
    return out
```

```python
from contextlib import ExitStack

import numpy as np

import concourse.bass as bass
from concourse import mybir

ALU = mybir.AluOpType
ACT = mybir.ActivationFunctionType
AX = mybir.AxisListType
F32 = mybir.dt.float32
F16 = mybir.dt.float16
I32 = mybir.dt.int32
U16 = mybir.dt.uint16
RMAX = bass.bass_isa.ReduceOp.max
ds = bass.ds

P = 128
BATCH, CHAN, H = 128, 32, 512
TOK = BATCH * CHAN
TILES = TOK // P
BPT = P // CHAN
GT = 8
GROUPS = TILES // GT
SUP = 4
KTAP, PAD = 9, 4
KT = H // P
EXP_N, TOPK, RANK, MIX_K = 4, 2, 16, 8
ER = EXP_N * RANK
AWN = ER + EXP_N
SCALE = 16.0 / 4.0
INNER = 1376
MT = -(-INNER // P)
INNER_P = MT * P
LAST = INNER - (MT - 1) * P
NC = 512
CHUNKS = TOK // NC
HALF = TOK // 2
BLK = 32
NB = H // BLK
MAGIC = 1.5 * 2.0 ** 23
QMAX = 65535.0
WMAX = 7.0
TINY = 1e-12
WUP = 1024.0
VDN = 1.0 / 16.0
SIG_ONE = 65536.0


def constants():
    ident = np.eye(P, dtype=np.float32)
    b = np.arange(P)
    pick = (b[:, None] % BPT == b[None, :] // CHAN).astype(np.float32)
    tile_of = (b[:, None] // BPT == np.arange(TILES)[None, :]).astype(np.float32)
    e, j = np.meshgrid(np.arange(EXP_N), np.arange(EXP_N), indexing="ij")
    before = np.broadcast_to((j < e).astype(np.float32).reshape(1, -1), (P, EXP_N * EXP_N))
    after = np.broadcast_to((j > e).astype(np.float32).reshape(1, -1), (P, EXP_N * EXP_N))
    return np.ascontiguousarray(np.concatenate([ident, pick, tile_of, before, after], axis=1))


C_ID, C_PICK, C_TILE, C_BEF, C_AFT, C_END = 0, P, 2 * P, 2 * P + TILES, 2 * P + TILES + 16, 2 * P + TILES + 32

PE_SETUP = ["condT", "awT", "bT", "mixT", "cwT", "h1", "h2", "logits", "attT", "aggb", "ctx", "attrep", "sumaw"]
EV_SETUP = ["id16", "condT", "awT", "bT", "mixT", "cwT", "negmax", "att", "attT", "aggb", "ctx", "attexp", "attrep",
            "sumaw"]
PE_AT = {n: i + 1 for i, n in enumerate(PE_SETUP)}
EV_AT = {n: i + 1 for i, n in enumerate(EV_SETUP)}


def pick1(ap, i):
    if isinstance(i, int):
        return ap[:, i]
    one = ap[:, ds(i, 1)]
    return one.rearrange("p a b -> p (a b)") if len(one.shape) == 3 else one.rearrange("p a b c -> p (a b) c")


class Chain:

    def __init__(self, eng, sem):
        self.eng, self.sem, self.base, self.n = eng, sem, 0, 0

    def __call__(self, ins):
        ins.then_inc(self.sem, 1)
        self.n += 1
        return ins

    def settle(self):
        self.eng.wait_ge(self.sem, self.base + self.n)

    def then(self, ins):
        self(ins)
        self.settle()

    def start(self):
        self.base, self.n = self.base + self.n, 0
        return self.base

    def iteration(self, start, i, per):
        self.base, self.n = start + i * per, 0

    def end(self, start, count, per):
        assert self.n == per, (self.n, per)
        self.base, self.n = start + count * per, 0


def build(nc, a, out):
    with ExitStack() as ctx:
        def sb(name, shape, dt):
            return ctx.enter_context(nc.sbuf_tensor("sb_" + name, shape, dt))

        def sem(name):
            return ctx.enter_context(nc.semaphore(name))

        def dram(name, shape):
            return nc.dram_tensor(name, shape, F32, kind="Internal").ap()

        KB = 1024
        WT = 8 * INNER_P * 2
        O_A, O_B, O_WG, O_WU = 0, 64 * KB, 128 * KB, 128 * KB + WT
        arena = sb("arena", [P, (O_WU + WT) // 4], F32)
        wd_region = sb("wd_region", [P, WT // 4], F32)

        def view(region, off, shape, dt):
            size = int(np.prod(shape)) * (2 if dt in (F16, U16) else 4)
            assert off % 4 == 0 and size % 4 == 0
            v = region[:, off // 4:(off + size) // 4]
            if dt != F32:
                v = v.bitcast(dt)
            if len(shape) == 2:
                v = v.rearrange("p (a b) -> p a b", a=shape[0])
            if len(shape) == 3:
                v = v.rearrange("p (a b c) -> p a b c", a=shape[0], b=shape[1])
            return v

        at = lambda off, shape, dt: view(arena, off, shape, dt)

        wgT = at(O_WG, [8, INNER_P], F16)
        wuT = at(O_WU, [8, INNER_P], F16)
        wdT = view(wd_region, 0, [MT, 2, H], F16)
        wdT8 = view(wd_region, 0, [MT, 8, P], F16)
        xT = at(O_B, [8, TOK], F16)
        y1 = at(O_A, [TILES, H], F32)
        xin = at(O_B, [GT, H], F32)
        xres = at(O_B + 16 * KB, [GT, H], F32)
        PW = H + 2 * PAD
        xc = at(O_B + 32 * KB, [GT, PW], F32)
        o = O_B + 32 * KB + GT * PW * 4
        mixbd = at(o, [GT, P], F32)
        o += GT * P * 4
        y0T = at(o, [2, H], F32)
        o += 2 * H * 4
        zbuf = at(o, [GT, AWN], F32)
        o += GT * AWN * 4
        zbias = at(o, [SUP, AWN], F32)
        o += SUP * AWN * 4
        gmid = at(o, [GT, ER], F32)
        assert o + GT * ER * 4 <= O_WG
        o = O_WU
        gmidT = at(o, [GT, P], F32)
        o += GT * P * 4
        mixtmp = at(o, [2, GT * CHAN], F32)
        o += 2 * GT * CHAN * 4
        mixacc = at(o, [1, GT * CHAN], F32)
        o += GT * CHAN * 4
        gate_t = at(o, [8, GT * 16], F32)
        o += 8 * GT * 16 * 4
        wk = at(o, [CHAN, KTAP], F32)
        o += CHAN * KTAP * 4
        mixT = at(o, [MIX_K, CHAN], F32)
        o += MIX_K * CHAN * 4
        attrep = at(o, [TILES, MIX_K], F32)
        o += TILES * MIX_K * 4
        awT = at(o, [KT, AWN], F32)
        o += KT * AWN * 4
        sumaw = at(o, [1, AWN], F32)
        o += AWN * 4
        bT = at(o, [1, H], F32)
        o += H * 4
        aggb = at(o, [1, TILES], F32)
        o += TILES * 4
        assert o <= O_WU + WT
        o = O_A
        cond = at(o, [1, P], F32)[:, 0]
        condT = at(o + 512, [1, P], F32)[:, 0]
        w0 = at(o + 1024, [1, P], F32)[:, 0]
        w1 = at(o + 1536, [1, P], F32)[:, 0]
        h1T = at(o + 2048, [1, P], F32)[:, 0]
        h2T = at(o + 2560, [1, P], F32)[:, 0]
        w2 = at(o + 3072, [1, MIX_K], F32)[:, 0]
        b2 = at(o + 3104, [1, MIX_K], F32)[:, 0]
        b01 = at(o + 3136, [1, 2], F32)[:, 0]
        side = at(o + 3144, [1, 1], F32)[:, 0]
        smx = at(o + 3148, [1, 4], F32)[:, 0]
        expv = at(o + 3164, [1, MIX_K], F32)[:, 0]
        att = at(o + 3196, [1, MIX_K], F32)[:, 0]
        biask = at(o + 3228, [1, CHAN], F32)[:, 0]
        attT = at(o + 3356, [1, P], F32)[:, 0]
        cw = at(o + 3868, [1, P], F32)[:, 0]
        cwT = at(o + 4380, [1, CHAN], F32)[:, 0]
        attexp = at(o + 4508, [TILES, MIX_K], F32)
        aw = at(o + 6144, [1, H], F32)[:, 0]
        bnat = at(o + 8192, [4, ER], F32)
        mixnat = at(o + 9216, [2, P], F32)
        o = O_A + 48 * KB
        wn = at(o, [2, H], F32)
        wint = at(o + 4 * KB, [2, H], F32)
        wsp = at(o + 8 * KB, [2, 8 * P], F16)
        wsc = at(o + 12 * KB, [8, NB], F32)
        wdnat = at(O_A + 16 * KB, [KT, INNER], F32)
        xq = at(O_WU, [1, SUP * H], U16)[:, 0]
        xv = at(O_WU + 4 * KB, [2, SUP * H], F32)
        xhl = view(wd_region, 0, [2, 2, SUP * H], F16)
        gbuf = at(O_A, [2, TOK], F32)
        ubuf = at(O_A, [2, TOK], F32)
        graw = at(O_A + 32 * KB, [2, HALF], F32)
        gq = at(O_A + 48 * KB, [1, HALF], U16)[:, 0]
        sq = at(O_A + 52 * KB, [1, HALF], U16)[:, 0]
        sig = at(O_A + 56 * KB, [1, HALF], F32)[:, 0]
        nv = at(O_WG, [2, HALF], F32)
        pin = at(O_A, [2, HALF], F32)
        uin = at(O_A + 16 * KB, [2, HALF], F32)
        qg = at(O_A + 32 * KB, [2, HALF], U16)
        qu = at(O_A + 40 * KB, [2, HALF], U16)
        vg = at(O_A + 48 * KB, [1, HALF], F32)[:, 0]
        vu = at(O_A + 56 * KB, [1, HALF], F32)[:, 0]
        prod = at(O_B, [2, HALF], F32)
        CH = MT * NC
        o = O_A
        pd = at(o, [2, CH], F32)
        o += 2 * CH * 4
        qd = at(o, [1, CH], U16)[:, 0]
        o += CH * 2
        vd = at(o, [1, CH], F32)[:, 0]
        o += CH * 4
        hd = at(o, [2, 2 * CH], F16)
        o += 2 * CH * 4
        x1b = at(o, [2, SUP * H], F32)
        o += 2 * SUP * H * 4
        ob = at(o, [2, SUP * H], F32)
        o += 2 * SUP * H * 4
        otmp = at(o, [2, H], F32)
        o += 2 * H * 4
        assert o <= O_WU + WT

        cst = sb("cst", [P, C_END], F32)
        id16 = sb("id16", [P, P], F16)
        ones = sb("ones", [P, P], F32)
        ctxcol = sb("ctxcol", [P, TILES], F32)
        gS = sb("gS", [P, MT], F32)
        uS = sb("uS", [P, MT], F32)
        dS = sb("dS", [P, KT], F32)
        dR = sb("dR", [P, KT], F32)
        rS = sb("rS", [P, 2, 1], F32)
        rowv = sb("rowv", [P, H], F32)
        dgS = sb("dgS", [P, P], F32)
        st_hi = sb("st_hi", [P, 2 * MT], F32)
        st_lo = sb("st_lo", [P, 2 * MT], F32)
        st = sb("st", [P, 5, 2], F32)
        red = sb("red", [P, 5, 2], F32)
        rg = sb("rg", [P, 5, 16], F32)
        vm = sb("vm", [P, 4], F32)
        vmq = sb("vmq", [P, 2], U16)
        st2 = sb("st2", [P, 2], F32)
        ident = cst[:, C_ID:C_ID + P]
        bank = [ctx.enter_context(nc.psum_tensor(f"bank{i}", [P, 512], F32)) for i in range(8)]

        X, G, S, U, O = range(5)
        SC, INV, ZP, NSC, NINV = 0, 1, 2, 3, 4

        def par(which, col):
            return rg[:, which, col:col + 1]

        x1d = dram("x1_rows", (TOK, H))
        gd = dram("gate_raw", (MT, P, TOK))
        ud = dram("up_raw", (MT, P, TOK))
        sd = dram("gated_raw", (MT, P, TOK))
        od = dram("product_raw", (MT, P, TOK))

        s_load = sem("setup_loaded")
        s_wk = sem("conv_weights_loaded")
        s_wdn = sem("down_rows_loaded")
        s_pe = sem("setup_pe")
        s_ev = sem("setup_evacuated")
        s_act = sem("setup_act")
        s_zero = sem("zeroed")
        s_none = sem("carries_waits")
        dch = sem("vector_steps")
        pch = sem("pool_steps")
        s_xin = sem("xin_loaded")
        s_xres = sem("xres_loaded")
        s_bd = sem("mix_ready")
        s_y0 = sem("y0_done")
        s_y0e = sem("y0_evacuated")
        s_ze = sem("z_evacuated")
        s_d4 = sem("logits_shifted")
        s_exp = sem("gates_exp")
        s_gm = sem("gated_mid")
        s_gt = sem("gated_mid_turned")
        s_gte = sem("gated_mid_copied")
        s_dl = sem("delta_done")
        s_x1 = sem("x1_ready")
        s_x1o = sem("x1_stored")
        s_cv = sem("conv_done")
        s_cve = sem("conv_evacuated")
        wn_in = [sem(f"wn_loaded{i}") for i in range(2)]
        wn_used = [sem(f"wn_used{i}") for i in range(2)]
        hl_ready = [sem(f"w_split{i}") for i in range(2)]
        hl_turned = [sem(f"w_turned{i}") for i in range(2)]
        wt_copied = [sem(f"w_copied{i}") for i in range(2)]
        s_mixn = sem("setup_loaded_pool")
        s_z1 = sem("z_tile_done")
        s_dg = sem("diagonal_ready")
        s_row = sem("row_scales_done")
        s_ob = sem("out_ready")
        s_st = sem("stats_ready")
        s_red = sem("range_reduced")
        s_par = sem("range_known")
        s_vm = sem("largest_gate")
        s_vma = sem("largest_gate_act")
        xq_q = sem("x_quantised")
        xq_v = sem("x_integer")
        xq_hi = sem("x_high")
        xq_lo = sem("x_low")
        xq_t = sem("x_turned")
        xq_ed = sem("x_turned_copied_dve")
        xq_ea = sem("x_turned_copied_act")
        g_mm = sem("gate_mm")
        g_ev = sem("gate_evacuated")
        g_st = [sem(f"gate_stored{i}") for i in range(2)]
        g_rd = sem("gate_reduced")
        u_mm = sem("up_mm")
        u_ev = sem("up_evacuated")
        u_st = [sem(f"up_stored{i}") for i in range(2)]
        u_rd = sem("up_reduced")
        s_gin = [sem(f"gate_loaded{i}") for i in range(2)]
        s_gq = sem("gate_quantised")
        s_nv = sem("gate_integer")
        s_sig = sem("sigmoid_done")
        s_sq = sem("sigmoid_quantised")
        s_pr = sem("gated_ready")
        s_pst = [sem(f"gated_stored{i}") for i in range(2)]
        s_pin = [sem(f"product_inputs_loaded{i}") for i in range(2)]
        s_q2 = sem("product_inputs_quantised")
        s_v2 = sem("product_inputs_read")
        s_po = sem("product_ready")
        s_pos = [sem(f"product_stored{i}") for i in range(2)]
        s_din = [sem(f"down_input_loaded{i}") for i in range(2)]
        s_dq = sem("down_quantised")
        s_dv = sem("down_integer")
        s_dhi = sem("down_high")
        s_dlo = sem("down_low")
        s_dmm = sem("down_mm")
        s_dev = sem("down_evacuated")
        s_x1i = [sem(f"x1_loaded{i}") for i in range(2)]
        s_out = [sem(f"out_stored{i}") for i in range(2)]

        N_SMALL = 15
        N_SLOT = ((MT + 1) // 2, MT // 2)
        U0, U1 = N_SLOT

        def settle_wait(eng, *waits):
            for s, v in waits:
                eng.wait_ge(s, v)
            eng.sem_inc(s_none, 1)

        block = ctx.enter_context(nc.Block())

        @block.sync
        def _(sp):
            def small(dst, src):
                sp.dma_start(dst, src).then_inc(s_load, 16)

            small(cst[:, :], a["consts"])
            small(cond, a["cond_128"])
            small(w0, a["L0_cond_W0"])
            small(w1, a["L0_cond_W1"])
            small(w2, a["L0_cond_W2"])
            small(b01[:, 0:1], a["L0_cond_b0"].rearrange("(p a) -> p a", a=1))
            small(b01[:, 1:2], a["L0_cond_b1"].rearrange("(p a) -> p a", a=1))
            small(b2[0:1, :], a["L0_cond_b2"].rearrange("(a k) -> a k", a=1))
            small(biask[0:MIX_K, :], a["L0_cond_bias_k"])
            small(aw[0:ER, :], a["L0_ffn_A"].rearrange("e r f -> (e r) f"))
            small(aw[ER:AWN, :], a["L0_ffn_Wr"])
            for e in range(EXP_N):
                small(bnat.rearrange("p t (e r) -> p t e r", e=EXP_N)[:, :, e, :],
                      a["L0_ffn_B"][e].rearrange("(t p) r -> p t r", p=P))
            for s in range(2):
                sp.dma_start(wn[:, s], a["L1_ffn_w_gate"][s * P:(s + 1) * P, :]).then_inc(wn_in[s], 16)
            x_v = a["x"].rearrange("(t b) c h -> (b c) t h", b=BPT)
            sp.dma_start(xin, x_v[:, 0:GT, :]).then_inc(s_xin, 16)
            sp.dma_start(xres, x_v[:, 0:GT, :]).then_inc(s_xres, 16)
            sp.dma_start(wdnat, a["L1_ffn_w_down"].rearrange("(t p) i -> p t i", p=P)).then_inc(s_wdn, 16)
            wg_v, wu_v = a["L1_ffn_w_gate"], a["L1_ffn_w_up"]
            wd_v = a["L1_ffn_w_down"].rearrange("(t p) i -> p t i", p=P)
            wn3 = wn.rearrange("p s (t i) -> p s t i", t=KT)
            with sp.Fori(0, (MT - 3) // 2) as i:
                for s in range(2):
                    settle_wait(sp, (wn_used[s], i + 2))
                    sp.dma_start(wn[:, s], wg_v[ds(i * 2 * P + (2 + s) * P, P), :]).then_inc(wn_in[s], 16)
            sp.wait_ge(wn_used[0], (MT - 1) // 2 + 1)
            sp.dma_start(wn[0:LAST, 0], wg_v[(MT - 1) * P:INNER, :]).then_inc(wn_in[0], 16)

            sp.sem_inc(s_x1o, 16)
            rows = x1d.rearrange("(t p) h -> p t h", p=P)
            with sp.Fori(0, GROUPS - 1) as g:
                sp.wait_ge(s_y0, (g + 1) * GT)
                sp.dma_start(xin, x_v[:, ds((g + 1) * GT, GT), :]).then_inc(s_xin, 16)
                sp.wait_ge(s_x1, (g + 1) * GT + 2)
                sp.dma_start(rows[:, ds(g * GT, GT), :], xc[:, :, PAD:PAD + H]).then_inc(s_x1o, 16)
                sp.dma_start(xres, x_v[:, ds((g + 1) * GT, GT), :]).then_inc(s_xres, 16)
            sp.wait_ge(s_x1, GROUPS * GT + 2)
            sp.dma_start(rows[:, (GROUPS - 1) * GT:, :], xc[:, :, PAD:PAD + H]).then_inc(s_x1o, 16)

            sp.wait_ge(xq_q, CHUNKS)
            for s in range(2):
                sp.sem_inc(g_st[s], 16)

            def load_units(m):
                settle_wait(sp, (wn_used[0], m + U0 + 1))
                sp.dma_start(wn[:, 0], wu_v[ds(m * P, P), :]).then_inc(wn_in[0], 16)
                settle_wait(sp, (wn_used[1], m + U1 + 1))
                sp.dma_start(wn3[:, 1], wd_v[:, :, ds(m * P, P)]).then_inc(wn_in[1], 16)

            def load_last_units():
                sp.wait_ge(wn_used[0], MT - 1 + U0 + 1)
                sp.dma_start(wn[0:LAST, 0], wu_v[(MT - 1) * P:INNER, :]).then_inc(wn_in[0], 16)
                sp.wait_ge(wn_used[1], MT - 1 + U1 + 1)
                sp.dma_start(wn3[:, 1, :, 0:LAST], wd_v[:, :, (MT - 1) * P:INNER]).then_inc(wn_in[1], 16)

            gd_v, ud_v, sd_v, od_v = (t.rearrange("m p t -> p m t") for t in (gd, ud, sd, od))

            def store_gate(m, slot):
                sp.wait_ge(g_ev, (m + 1) * CHUNKS + 4)
                sp.dma_start(pick1(gd_v, m), gbuf[:, slot]).then_inc(g_st[slot], 16)

            load_units(0)
            with sp.Fori(0, (MT - 3) // 2) as i:
                for s in range(2):
                    load_units(i * 2 + s + 1)
                    store_gate(i * 2 + s, s)
            load_units(MT - 2)
            store_gate(MT - 3, 0)
            load_last_units()
            store_gate(MT - 2, 1)
            store_gate(MT - 1, 0)

            def load_gate(m, half):
                sp.wait_ge(s_gq, m * 2 + half - 1)
                sp.dma_start(graw[:, half], pick1(gd_v, m)[:, half * HALF:(half + 1) * HALF])\
                    .then_inc(s_gin[half], 16)

            def store_up(m, slot):
                sp.wait_ge(u_ev, (m + 1) * CHUNKS + 4)
                sp.dma_start(pick1(ud_v, m), ubuf[:, slot]).then_inc(u_st[slot], 16)
                for half in range(2):
                    sp.wait_ge(s_pr, m * 2 + half + 1)
                    sp.dma_start(pick1(sd_v, m)[:, half * HALF:(half + 1) * HALF], nv[:, half])\
                        .then_inc(s_pst[half], 16)

            for s in range(2):
                sp.wait_ge(g_st[s], 16 + 16 * N_SLOT[s])
                sp.sem_inc(u_st[s], 16)
            sp.sem_inc(s_pst[0], 16)
            sp.sem_inc(s_pst[1], 16)
            for half in range(2):
                sp.dma_start(graw[:, half], gd_v[:, 0, half * HALF:(half + 1) * HALF]).then_inc(s_gin[half], 16)
            with sp.Fori(0, (MT - 1) // 2) as i:
                for s in range(2):
                    for half in range(2):
                        load_gate(i * 2 + s + 1, half)
                    store_up(i * 2 + s, s)
            store_up(MT - 1, 0)

            for s in range(2):
                sp.wait_ge(u_st[s], 16 + 16 * N_SLOT[s])
            sp.wait_ge(s_pst[0], 16 + 16 * MT)
            sp.wait_ge(s_pst[1], 16 + 16 * MT)
            sp.wait_ge(u_rd, 2 + MT)
            sp.sem_inc(s_pos[0], 16)
            sp.sem_inc(s_pos[1], 16)

            def load_factors(m, half):
                sp.dma_start(pin[:, half], pick1(sd_v, m)[:, half * HALF:(half + 1) * HALF])\
                    .then_inc(s_pin[half], 16)
                sp.dma_start(uin[:, half], pick1(ud_v, m)[:, half * HALF:(half + 1) * HALF])\
                    .then_inc(s_pin[half], 16)

            def store_product(m, half):
                sp.wait_ge(s_po, m * 2 + half + 1)
                sp.dma_start(pick1(od_v, m)[:, half * HALF:(half + 1) * HALF], prod[:, half])\
                    .then_inc(s_pos[half], 16)

            for half in range(2):
                load_factors(0, half)
            with sp.Fori(0, MT - 1) as m:
                for half in range(2):
                    sp.wait_ge(s_q2, m * 4 + half * 2 + 2)
                    load_factors(m + 1, half)
                for half in range(2):
                    store_product(m, half)
            for half in range(2):
                store_product(MT - 1, half)

            x1_v = x1d.rearrange("(s j i o) h -> s j o i h", s=CHUNKS, j=BPT, i=SUP)
            out_v = out.rearrange("(s j i) o h -> s j o i h", s=CHUNKS, j=BPT, i=SUP)

            def rows_of(v, c, j):
                return v[c, j] if isinstance(c, int) else v[ds(c, 1), j].rearrange("a o i h -> (a o) i h")

            def load_chunk(c, slot):
                src = od_v[:, :, c * NC:(c + 1) * NC] if isinstance(c, int) else od_v[:, :, ds(c * NC, NC)]
                sp.dma_start(pd[:, slot].rearrange("p (m t) -> p m t", m=MT), src).then_inc(s_din[slot], 16)

            def load_x1(c, slot):
                for j in range(BPT):
                    sp.dma_start(x1b[CHAN * j:CHAN * (j + 1), slot].rearrange("p (i h) -> p i h", i=SUP),
                                 rows_of(x1_v, c, j)).then_inc(s_x1i[slot], 16)

            def store_out(c, slot):
                sp.wait_ge(s_ob, c * SUP + SUP)
                for j in range(BPT):
                    sp.dma_start(rows_of(out_v, c, j),
                                 ob[CHAN * j:CHAN * (j + 1), slot].rearrange("p (i h) -> p i h", i=SUP))\
                        .then_inc(s_out[slot], 16)

            sp.wait_ge(s_pos[0], 16 + 16 * MT)
            sp.wait_ge(s_pos[1], 16 + 16 * MT)
            sp.wait_ge(s_par, 5)
            sp.sem_inc(s_out[0], 64)
            sp.sem_inc(s_out[1], 64)
            for c in range(2):
                load_chunk(c, c)
                load_x1(c, c)
            with sp.Fori(0, (CHUNKS - 2) // 2) as i:
                for s in range(2):
                    sp.wait_ge(s_dq, i * 2 + s + 1)
                    load_chunk(i * 2 + s + 2, s)
                    store_out(i * 2 + s, s)
                    load_x1(i * 2 + s + 2, s)
            for c in (CHUNKS - 2, CHUNKS - 1):
                store_out(c, c % 2)
            for s in range(2):
                sp.wait_ge(s_out[s], 64 + 64 * (CHUNKS // 2))

        @block.vector
        def _(dve):
            ch = Chain(dve, dch)
            V = nc.vector

            ch(V.memset(wk.rearrange("p a b -> p (a b)"), 0.0))
            ch(V.memset(mixbd.rearrange("p a b -> p (a b)"), 0.0))
            ch(V.memset(xc[:, :, 0:PAD], 0.0))
            ch(V.memset(xc[:, :, PAD + H:PW], 0.0))
            ch(V.memset(st2[:, :], -3.0e38))
            V.memset(ones[:, :], 1.0).then_inc(s_zero, 1)
            ch.settle()
            dve.sem_inc(s_zero, 1)
            for s in range(2):
                dve.sem_inc(wn_used[s], 1)
            dve.sem_inc(s_x1, 2)
            dve.sem_inc(xq_v, 1)
            dve.sem_inc(xq_ed, 2)
            dve.sem_inc(g_rd, 2)
            dve.sem_inc(u_rd, 2)
            dve.sem_inc(s_nv, 1)
            dve.sem_inc(s_sq, 1)
            dve.sem_inc(s_v2, 4)
            dve.sem_inc(s_dv, 1)
            dve.sem_inc(s_dev, 4)

            dve.wait_ge(s_load, 16 * N_SMALL)
            V.tensor_copy(id16[:, :], ident).then_inc(s_ev, 1)
            dve.wait_ge(s_pe, PE_AT["condT"])
            V.tensor_copy(condT, bank[0][:, 0:P]).then_inc(s_ev, 1)
            dve.wait_ge(s_pe, PE_AT["awT"])
            V.tensor_copy(awT.rearrange("p a b -> p (a b)"), bank[1][:, 0:KT * AWN]).then_inc(s_ev, 1)
            dve.wait_ge(s_pe, PE_AT["bT"])
            V.tensor_scalar(bT[0:ER, 0], bank[2][0:ER, :], SCALE, None, ALU.mult).then_inc(s_ev, 1)
            dve.wait_ge(s_pe, PE_AT["mixT"])
            V.tensor_copy(mixT.rearrange("p a b -> p (a b)"), bank[3][:, 0:MIX_K * CHAN]).then_inc(s_ev, 1)
            dve.wait_ge(s_pe, PE_AT["cwT"])
            V.tensor_copy(cwT, bank[4][:, 0:CHAN]).then_inc(s_ev, 1)
            dve.wait_ge(s_pe, PE_AT["logits"])
            V.tensor_reduce(smx[:, 0:1], bank[7][:, 0:MIX_K], AX.X, ALU.max, negate=True).then_inc(s_ev, 1)
            dve.wait_ge(s_act, 3)
            ch.then(V.reciprocal(smx[:, 2:3], smx[:, 1:2]))
            V.tensor_scalar(att, expv, smx[:, 2:3], None, ALU.mult).then_inc(s_ev, 1)
            dve.wait_ge(s_pe, PE_AT["attT"])
            V.tensor_copy(attT[0:MIX_K, :], bank[0][0:MIX_K, 0:P]).then_inc(s_ev, 1)
            dve.wait_ge(s_pe, PE_AT["aggb"])
            V.tensor_copy(aggb[:, 0], bank[1][:, 0:TILES]).then_inc(s_ev, 1)
            dve.wait_ge(s_pe, PE_AT["ctx"])
            V.tensor_scalar(ctxcol[:, :], bank[2][:, 0:TILES], side, None, ALU.add).then_inc(s_ev, 1)
            dve.wait_ge(s_ev, EV_AT["att"])
            V.tensor_tensor(attexp, att.unsqueeze(1).broadcast_to([P, TILES, MIX_K]),
                            cst[:, C_TILE:C_TILE + TILES].unsqueeze(2).broadcast_to([P, TILES, MIX_K]), ALU.mult)\
                .then_inc(s_ev, 1)
            dve.wait_ge(s_pe, PE_AT["attrep"])
            V.tensor_copy(attrep.rearrange("p a b -> p (a b)"), bank[3][:, 0:TILES * MIX_K]).then_inc(s_ev, 1)
            dve.wait_ge(s_pe, PE_AT["sumaw"])
            V.tensor_copy(sumaw[:, 0], bank[4][:, 0:AWN]).then_inc(s_ev, 1)

            def power_of_two(dst, src):
                V_i = src.bitcast(I32)
                ch.then(V.tensor_scalar(dst.bitcast(I32), V_i, 0x7F800000, None, ALU.bitwise_and))

            dve.wait_ge(s_wdn, 16)
            ch.then(V.tensor_reduce(dR[:, :], wdnat, AX.X, ALU.max, apply_absolute_value=True))
            ch.then(V.tensor_scalar(dR[:, :], dR[:, :], 1.0 / WMAX, TINY, ALU.mult, ALU.max))
            power_of_two(dS[:, :], dR[:, :])
            ch.then(V.reciprocal(dR[:, :], dS[:, :]))
            ch.then(V.tensor_scalar(dR[:, :], dR[:, :], WUP, None, ALU.mult))

            PREP_G, PREP_D = 11, 7

            def prep(u, slot, norm, clear):
                w = wn[:, slot]
                wi = wint[:, slot]
                blocks = [NB, BLK]

                def b(v):
                    return v.unsqueeze(2).broadcast_to([P] + blocks)

                dve.wait_ge(wn_in[slot], (u + 1) * 16)
                ch.then(V.tensor_reduce(wsc[:, 0], w.rearrange("p (b k) -> p b k", k=BLK), AX.X, ALU.max,
                                        apply_absolute_value=True))
                ch.then(V.tensor_scalar(wsc[:, 1], wsc[:, 0], 1.0 / WMAX, TINY, ALU.mult, ALU.max))
                ch.then(V.reciprocal(wsc[:, 2], wsc[:, 1]))
                last = V.tensor_tensor(wi.rearrange("p (b k) -> p b k", k=BLK),
                                       w.rearrange("p (b k) -> p b k", k=BLK), b(wsc[:, 2]), ALU.mult)
                if clear:
                    ch.then(last)
                    pad = wn[LAST:P, 0] if slot == 0 else wn[:, 1].rearrange("p (t i) -> p t i", t=KT)[:, :, LAST:P]
                    last = V.memset(pad, 0.0)
                last.then_inc(wn_used[slot], 1)
                dve.wait_ge(wn_used[slot], u + 2)
                ch(V.tensor_scalar(wi, wi, MAGIC, MAGIC, ALU.add, ALU.subtract))
                if norm is not None:
                    ch.then(V.tensor_reduce(wsc[:, 4, 0:1], wsc[:, 1], AX.X, ALU.max))
                    power_of_two(wsc[:, 4, 1:2], wsc[:, 4, 0:1])
                    ch(V.tensor_scalar(norm, wsc[:, 4, 1:2], 1.0, None, ALU.mult))
                    ch.then(V.reciprocal(rS[:, slot], wsc[:, 4, 1:2]))
                    ch.then(V.tensor_scalar(wsc[:, 3], wsc[:, 1], rS[:, slot], WUP, ALU.mult, ALU.mult))
                else:
                    ch.then(V.tensor_tensor(wsc[:, 3].rearrange("p (t b) -> p t b", t=KT),
                                            wsc[:, 1].rearrange("p (t b) -> p t b", t=KT),
                                            dR[:, :].unsqueeze(2).broadcast_to([P, KT, NB // KT]), ALU.mult))
                ch.then(V.tensor_tensor(wi.rearrange("p (b k) -> p b k", k=BLK),
                                        wi.rearrange("p (b k) -> p b k", k=BLK), b(wsc[:, 3]), ALU.mult))
                dve.wait_ge(hl_turned[slot], u + 1)
                ch.then(V.tensor_copy(wsp[:, slot, 0:H], wi))
                V.tensor_tensor(wsp[:, slot, H:2 * H], wi, wsp[:, slot, 0:H], ALU.subtract)\
                    .then_inc(hl_ready[slot], 1)

            start = ch.start()
            with dve.Fori(0, (MT - 3) // 2) as i:
                ch.iteration(start, i, 2 * PREP_G)
                for s in range(2):
                    prep(i, s, gS[:, ds(i * 2 + s, 1)], False)
            ch.end(start, (MT - 3) // 2, 2 * PREP_G)
            prep((MT - 3) // 2, 0, gS[:, MT - 3:MT - 2], True)
            prep((MT - 3) // 2, 1, gS[:, MT - 2:MT - 1], False)
            prep((MT - 1) // 2, 0, gS[:, MT - 1:MT], False)

            def z_out(g):
                for h in range(2):
                    rows = aggb[:, 0, h * SUP + g * GT:h * SUP + g * GT + SUP] if isinstance(g, int) else \
                        aggb[:, 0, ds(g * GT + h * SUP, SUP)]
                    ch.then(V.tensor_tensor(zbias, sumaw[:, 0].unsqueeze(1).broadcast_to([P, SUP, AWN]),
                                            rows.unsqueeze(2).broadcast_to([P, SUP, AWN]), ALU.mult))
                    dve.wait_ge(s_z1, g * GT + (h + 1) * SUP)
                    V.tensor_tensor(zbuf[:, h * SUP:(h + 1) * SUP],
                                    bank[2 + h][:, 0:SUP * AWN].rearrange("p (t n) -> p t n", t=SUP),
                                    zbias, ALU.add).then_inc(s_ze, 1)
                    dve.wait_ge(s_ze, g * 2 + h + 1)

            Z_STEPS, G_STEPS = 2, 12

            def gates(g):
                v = zbuf[:, :, ER:AWN]
                four = [P, GT, EXP_N, EXP_N]
                vj, ve = v.unsqueeze(2).broadcast_to(four), v.unsqueeze(3).broadcast_to(four)
                t4 = [gate_t[:, k, :].rearrange("p (t e j) -> p t e j", t=GT, e=EXP_N) for k in range(2)]
                flat = [gate_t[:, k, :].rearrange("p (t q) -> p t q", t=GT) for k in range(2)]
                masks = [cst[:, c:c + 16].unsqueeze(1).broadcast_to([P, GT, 16]) for c in (C_BEF, C_AFT)]
                small = [gate_t[:, k, 0:GT * EXP_N].rearrange("p (t e) -> p t e", t=GT) for k in range(2, 6)]
                rank, sel, d, ex = small
                m1, total = gate_t[:, 6, 0:GT], gate_t[:, 6, GT:2 * GT]
                inv = gate_t[:, 6, 2 * GT:3 * GT]
                by_e = lambda x: x.unsqueeze(2).broadcast_to([P, GT, EXP_N])
                ch(V.tensor_tensor(t4[0], vj, ve, ALU.is_ge))
                ch(V.tensor_tensor(t4[1], vj, ve, ALU.is_gt))
                ch.then(V.tensor_reduce(m1, v, AX.X, ALU.max))
                ch(V.tensor_tensor(flat[0], flat[0], masks[0], ALU.mult))
                ch(V.tensor_tensor(flat[1], flat[1], masks[1], ALU.mult))
                V.tensor_tensor(d, v, by_e(m1), ALU.subtract).then_inc(s_d4, 1)
                ch.settle()
                ch.then(V.tensor_tensor(flat[0], flat[0], flat[1], ALU.add))
                ch.then(V.tensor_reduce(rank, t4[0], AX.X, ALU.add))
                ch.then(V.tensor_scalar(sel, rank, TOPK - 0.5, None, ALU.is_lt))
                dve.wait_ge(s_exp, g + 1)
                ch.then(V.tensor_tensor(ex, ex, sel, ALU.mult))
                ch.then(V.tensor_reduce(total, ex, AX.X, ALU.add))
                ch.then(V.reciprocal(inv, total))
                ch.then(V.tensor_tensor(ex, ex, by_e(inv), ALU.mult))
                V.tensor_tensor(gmid.rearrange("p t (e r) -> p t e r", e=EXP_N),
                                zbuf[:, :, 0:ER].rearrange("p t (e r) -> p t e r", e=EXP_N),
                                ex.unsqueeze(3).broadcast_to([P, GT, EXP_N, RANK]), ALU.mult).then_inc(s_gm, 1)

            def add_delta(g):
                dve.wait_ge(s_xres, g * 16 + 16)
                dve.wait_ge(s_x1o, g * 16 + 16)
                dve.wait_ge(s_cv, g * 2 + 1)
                for t in range(GT):
                    dve.wait_ge(s_dl, g * GT + t + 1)
                    V.tensor_tensor(xc[:, t, PAD:PAD + H], bank[6 + t % 2][:, :], xres[:, t], ALU.add)\
                        .then_inc(s_x1, 1)

            def y_range(g):
                for s in range(2):
                    dve.wait_ge(s_cve, g * GT + s * SUP + SUP + GT)
                    at_ = g * GT + s * SUP
                    v = y1[:, at_:at_ + SUP] if isinstance(g, int) else y1[:, ds(at_, SUP)]
                    col = slice(g * 2 + s, g * 2 + s + 1) if isinstance(g, int) else ds(g * 2 + s, 1)
                    v = v.rearrange("p a b -> p (a b)")
                    ch(V.tensor_reduce(st_hi[:, col], v, AX.X, ALU.max))
                    ch(V.tensor_reduce(st_lo[:, col], v, AX.X, ALU.min))

            dve.wait_ge(s_ev, EV_AT["sumaw"])
            z_out(0)
            gates(0)
            start = ch.start()
            with dve.Fori(0, GROUPS - 1) as g:
                ch.iteration(start, g, Z_STEPS + G_STEPS + 4)
                add_delta(g)
                z_out(g + 1)
                gates(g + 1)
                y_range(g)
            ch.end(start, GROUPS - 1, Z_STEPS + G_STEPS + 4)
            add_delta(GROUPS - 1)
            y_range(GROUPS - 1)

            def known_range(which, n, k=None):
                ch.settle()
                if n:
                    ch(V.tensor_reduce(st[:, which, 0:1], st_hi[:, 0:n], AX.X, ALU.max))
                    ch(V.tensor_reduce(st[:, which, 1:2], st_lo[:, 0:n], AX.X, ALU.min, negate=True))
                ch.settle()
                dve.sem_inc(s_st, 1)
                dve.wait_ge(s_red, which + 1)
                r = rg[:, which, 5:7]
                d, q, e, f, n_ = (rg[:, which, 7 + j:8 + j] for j in range(5))
                ch.then(V.tensor_scalar(r, red[:, which, :], 0.0, 1.0 if k is None else k, ALU.max, ALU.mult))
                ch.then(V.tensor_tensor(d, r[:, 0:1], r[:, 1:2], ALU.add))
                ch.then(V.tensor_scalar(q, d, 1.0 / QMAX, None, ALU.mult))
                ch.then(V.scalar_tensor_tensor(e, q, -65536.0, d, ALU.mult, ALU.add))
                ch.then(V.tensor_tensor(f, e, q, ALU.add))
                ch.then(V.scalar_tensor_tensor(n_, f, 1.0 / QMAX, q, ALU.mult, ALU.add))
                ch.then(V.tensor_scalar(par(which, SC), n_, TINY, None, ALU.max))
                ch.then(V.reciprocal(par(which, INV), par(which, SC)))
                ch.then(V.tensor_scalar(par(which, ZP), r[:, 1:2], par(which, INV), MAGIC, ALU.mult, ALU.add))
                ch.then(V.tensor_scalar(par(which, ZP), par(which, ZP), MAGIC, None, ALU.subtract))
                if k is not None:
                    ch.then(V.tensor_scalar(par(which, INV), par(which, INV), k, None, ALU.mult))
                ch.then(V.tensor_scalar(par(which, NSC), par(which, SC), -1.0, None, ALU.mult))
                ch.then(V.tensor_scalar(par(which, NINV), par(which, INV), -1.0, None, ALU.mult))

            known_range(X, 2 * GROUPS)
            dve.sem_inc(s_par, 1)
            ch.then(V.tensor_scalar(gS[:, :], gS[:, :], par(X, SC), 1.0 / (WUP * VDN), ALU.mult, ALU.mult))

            def x_integer(c, s):
                dve.wait_ge(xq_q, c + 1)
                dve.wait_ge(xq_hi, c + 1)
                V.tensor_scalar(xv[:, s], xq, par(X, ZP), VDN, ALU.subtract, ALU.mult).then_inc(xq_v, 1)

            def x_low(c, s):
                dve.wait_ge(xq_hi, c + 3)
                dve.wait_ge(xq_t, c * SUP + SUP)
                V.tensor_tensor(xhl[:, s, 1], xv[:, s], xhl[:, s, 0], ALU.subtract).then_inc(xq_lo, 1)

            def x_copy(eng, c, ts, copied):
                for t in ts:
                    eng.wait_ge(xq_t, c * SUP + t + 1 + 2 * SUP)
                    tile = c * SUP + t
                    dst = xT[:, :, tile * P:(tile + 1) * P] if isinstance(c, int) else xT[:, :, ds(tile * P, P)]
                    src = bank[4 + t][:, :].bitcast(F16).rearrange("p (a b) -> p a b", a=8)
                    if eng is dve:
                        V.tensor_copy(dst, src).then_inc(copied, 1)
                    else:
                        nc.scalar.activation(dst, src, ACT.Copy).then_inc(copied, 1)

            dve.wait_ge(s_x1o, 16 + 16 * GROUPS)
            dve.wait_ge(s_par, 1)
            x_integer(0, 0)
            with dve.Fori(0, (CHUNKS - 2) // 2) as i:
                for s in range(2):
                    c = i * 2 + s
                    x_low(c, s)
                    x_integer(c + 1, 1 - s)
                    x_copy(dve, c, (0, 1), xq_ed)
            x_low(CHUNKS - 2, 0)
            x_integer(CHUNKS - 1, 1)
            x_copy(dve, CHUNKS - 2, (0, 1), xq_ed)
            x_low(CHUNKS - 1, 1)
            x_copy(dve, CHUNKS - 1, (0, 1), xq_ed)

            def raw_range(m, buf, slot, ev, rd):
                dve.wait_ge(ev, m * CHUNKS + CHUNKS + 4)
                col = slice(m, m + 1) if isinstance(m, int) else ds(m, 1)
                ch(V.tensor_reduce(st_hi[:, col], buf[:, slot], AX.X, ALU.max))
                V.tensor_reduce(st_lo[:, col], buf[:, slot], AX.X, ALU.min).then_inc(rd, 1)

            def gate_step(m, slot, clear=False):
                prep(m + U0, 0, uS[:, m:m + 1] if isinstance(m, int) else uS[:, ds(m, 1)], clear)
                prep(m + U1, 1, None, clear)
                raw_range(m, gbuf, slot, g_ev, g_rd)

            start = ch.start()
            with dve.Fori(0, (MT - 3) // 2) as i:
                ch.iteration(start, i, 2 * (PREP_G + PREP_D + 1))
                for s in range(2):
                    gate_step(i * 2 + s, s)
            ch.end(start, (MT - 3) // 2, 2 * (PREP_G + PREP_D + 1))
            gate_step(MT - 3, 0)
            gate_step(MT - 2, 1, clear=True)
            gate_step(MT - 1, 0)
            dve.wait_ge(g_rd, 2 + MT)
            ch.then(V.tensor_scalar(uS[:, :], uS[:, :], par(X, SC), 1.0 / (WUP * VDN), ALU.mult, ALU.mult))
            known_range(G, MT)
            dve.sem_inc(s_par, 1)

            dve.wait_ge(s_vma, 1)
            V.tensor_scalar(vm[:, 0:1], vmq[:, 0:1], -1.0, par(G, ZP), ALU.mult, ALU.add).then_inc(s_vm, 1)
            dve.wait_ge(s_vma, 2)
            ch.then(V.tensor_scalar(vmq[:, 1:2], vm[:, 1:2], SIG_ONE, None, ALU.mult))
            ch.then(V.tensor_tensor(vm[:, 2:3], vm[:, 0:1], vmq[:, 1:2], ALU.mult))
            ch.then(V.tensor_scalar(st[:, S, 0:1], vm[:, 2:3], -1.0, None, ALU.mult))

            def gated(m, half):
                n = m * 2 + half
                dve.wait_ge(s_gq, n + 1)
                dve.wait_ge(s_pst[half], m * 16 + 16)
                V.tensor_scalar(nv[:, half], gq, -1.0, par(G, ZP), ALU.mult, ALU.add).then_inc(s_nv, 1)
                dve.wait_ge(s_sig, n + 1)
                V.tensor_scalar(sq, sig, SIG_ONE, None, ALU.mult).then_inc(s_sq, 1)
                settle_wait(dve, (s_sq, n + 2))
                V.tensor_tensor_reduce(nv[:, half], nv[:, half], sq, 1.0, st2[:, 0:1], ALU.mult, ALU.max,
                                       st2[:, 0:1]).then_inc(s_pr, 1)

            def up_step(m, slot):
                for half in range(2):
                    gated(m, half)
                raw_range(m, ubuf, slot, u_ev, u_rd)

            start = ch.start()
            with dve.Fori(0, (MT - 1) // 2) as i:
                ch.iteration(start, i, 2)
                for s in range(2):
                    up_step(i * 2 + s, s)
            ch.end(start, (MT - 1) // 2, 2)
            up_step(MT - 1, 0)
            dve.wait_ge(s_pr, 2 * MT)
            ch(V.tensor_scalar(st[:, S, 1:2], st2[:, 0:1], 1.0, None, ALU.mult))
            ch.then(V.tensor_scalar(vm[:, 3:4], par(G, SC), 1.0 / SIG_ONE, None, ALU.mult))
            known_range(S, 0, k=vm[:, 3:4])
            dve.wait_ge(u_rd, 2 + MT)
            known_range(U, MT)
            dve.sem_inc(s_par, 2)

            def product(m, half):
                n = m * 2 + half
                dve.wait_ge(s_q2, n * 2 + 1)
                V.tensor_scalar(vg, qg[:, half], par(S, ZP), None, ALU.subtract).then_inc(s_v2, 1)
                dve.wait_ge(s_q2, n * 2 + 2)
                V.tensor_scalar(vu, qu[:, half], par(U, ZP), None, ALU.subtract).then_inc(s_v2, 1)
                settle_wait(dve, (s_v2, n * 2 + 2 + 4), (s_pos[half], m * 16 + 16))
                col = slice(n, n + 1) if isinstance(n, int) else ds(n, 1)
                V.tensor_tensor_reduce(prod[:, half], vg, vu, 1.0, st2[:, 1:2], ALU.mult, ALU.max,
                                       st2[:, 1:2]).then_inc(s_po, 1)
                dve.wait_ge(s_po, n + 1)
                ch(V.tensor_reduce(st_lo[:, col], prod[:, half], AX.X, ALU.min))

            start = ch.start()
            with dve.Fori(0, MT) as m:
                ch.iteration(start, m, 2)
                for half in range(2):
                    product(m, half)
            ch.end(start, MT, 2)
            ch.then(V.tensor_tensor(vm[:, 3:4], par(S, SC), par(U, SC), ALU.mult))
            ch(V.tensor_reduce(st[:, O, 1:2], st_lo[:, 0:2 * MT], AX.X, ALU.min, negate=True))
            ch(V.tensor_scalar(st[:, O, 0:1], st2[:, 1:2], 1.0, None, ALU.mult))
            known_range(O, 0, k=vm[:, 3:4])
            dve.sem_inc(s_par, 1)

            def d_integer(c, s):
                dve.wait_ge(s_dq, c + 1)
                dve.wait_ge(s_dhi, c + 1)
                V.tensor_scalar(vd, qd, par(O, ZP), VDN, ALU.subtract, ALU.mult).then_inc(s_dv, 1)
                dve.wait_ge(s_dhi, c + 2)
                dve.wait_ge(s_dmm, c * SUP + SUP)
                V.tensor_tensor(hd[:, s, CH:2 * CH], vd, hd[:, s, 0:CH], ALU.subtract).then_inc(s_dlo, 1)

            def d_out(c, s):
                for t in range(SUP):
                    dve.wait_ge(s_dmm, c * SUP + t + 1 + 2 * SUP)
                    V.tensor_tensor(otmp[:, t % 2], bank[t][:, :], rowv[:, :], ALU.mult).then_inc(s_dev, 1)
                    dve.wait_ge(s_dev, c * SUP + t + 1 + SUP)
                    V.tensor_tensor(ob[:, s, t * H:(t + 1) * H], otmp[:, t % 2], x1b[:, s, t * H:(t + 1) * H],
                                    ALU.add).then_inc(s_ob, 1)

            def d_room(pair, s):
                dve.wait_ge(s_x1i[s], pair * 64 + 64)
                dve.wait_ge(s_out[s], pair * 64 + 64)

            dve.wait_ge(s_par, 5)
            d_integer(0, 0)
            for t in range(KT):
                ch.then(V.tensor_scalar(dgS[:, :], ident, dS[:, t:t + 1], None, ALU.mult))
                dve.sem_inc(s_dg, 1)
                dve.wait_ge(s_row, t + 1)
            ch.then(V.tensor_scalar(rowv[:, :], bank[7][:, :], par(O, SC), 1.0 / (WUP * VDN), ALU.mult, ALU.mult))
            with dve.Fori(0, (CHUNKS - 2) // 2) as i:
                for s in range(2):
                    c = i * 2 + s
                    d_integer(c + 1, 1 - s)
                    d_room(i, s)
                    d_out(c, s)
            d_integer(CHUNKS - 1, 1)
            for s in range(2):
                d_room((CHUNKS - 2) // 2, s)
                d_out(CHUNKS - 2 + s, s)

        @block.scalar
        def _(act):
            A = nc.scalar
            act.wait_ge(s_zero, 2)
            for j in range(BPT):
                for g in range(4):
                    r = 8 * g
                    act.dma_start(wk[CHAN * j + r:CHAN * j + r + 8, r:r + 8, :],
                                  a["L1_cond_weight"][r:r + 8].rearrange("o i k -> i o k")).then_inc(s_wk, 16)
            act.sem_inc(xq_hi, 2)
            act.sem_inc(xq_ea, 2)
            act.sem_inc(s_y0e, 2)
            act.sem_inc(s_cve, GT)
            act.sem_inc(g_ev, 4)
            act.sem_inc(u_ev, 4)
            act.sem_inc(s_dhi, 1)
            for s in range(2):
                act.sem_inc(wt_copied[s], 1)
            act.wait_ge(s_pe, PE_AT["h1"])
            A.activation(h1T, bank[5][:, 0:P], ACT.Gelu, bias=b01[:, 0:1]).then_inc(s_act, 1)
            act.wait_ge(s_pe, PE_AT["h2"])
            A.activation(h2T, bank[6][:, 0:P], ACT.Gelu, bias=b01[:, 1:2]).then_inc(s_act, 1)
            act.wait_ge(s_ev, EV_AT["negmax"])
            A.activation(expv, bank[7][:, 0:MIX_K], ACT.Exp, bias=smx[:, 0:1], accum_out=smx[:, 1:2])\
                .then_inc(s_act, 1)

            def copy_weights(u, slot, dst):
                settle_wait(act, (hl_turned[slot], u + 2))
                A.activation(dst, bank[4 + slot][:, :].bitcast(F16).rearrange("p (a b) -> p a b", a=8), ACT.Copy)\
                    .then_inc(wt_copied[slot], 1)

            with act.Fori(0, (MT - 1) // 2) as i:
                for s in range(2):
                    copy_weights(i, s, wgT[:, :, ds(i * 2 * P + s * P, P)])
            copy_weights((MT - 1) // 2, 0, wgT[:, :, (MT - 1) * P:MT * P])

            def y0_out(g):
                for t in range(GT):
                    act.wait_ge(s_y0, g * GT + t + 1)
                    if t >= 2:
                        act.wait_ge(s_z1, g * GT + t - 1)
                    A.activation(y0T[:, t % 2], bank[t % 2][:, :], ACT.Copy).then_inc(s_y0e, 1)

            def gates_exp(g):
                act.wait_ge(s_d4, g + 1)
                A.activation(gate_t[:, 5, 0:GT * EXP_N], gate_t[:, 4, 0:GT * EXP_N], ACT.Exp).then_inc(s_exp, 1)

            def gmid_out(g):
                for h in range(2):
                    act.wait_ge(s_gt, g * 2 + h + 1)
                    A.activation(gmidT[0:ER, h * SUP:(h + 1) * SUP].rearrange("p a b -> p (a b)"),
                                 bank[4 + h][0:ER, :], ACT.Copy).then_inc(s_gte, 1)

            def conv_out(g):
                for t in range(GT):
                    if t % SUP == 0:
                        settle_wait(act, (s_cv, g * 2 + t // SUP + 2))
                    tile = g * GT + t
                    bias = ctxcol[:, tile:tile + 1] if isinstance(g, int) else ctxcol[:, ds(tile, 1)]
                    A.activation(pick1(y1, tile), bank[t][:, :], ACT.Identity, bias=bias).then_inc(s_cve, 1)

            act.wait_ge(s_ev, EV_AT["ctx"])
            y0_out(0)
            gates_exp(0)
            with act.Fori(0, GROUPS - 1) as g:
                gmid_out(g)
                y0_out(g + 1)
                gates_exp(g + 1)
                conv_out(g)
            gmid_out(GROUPS - 1)
            conv_out(GROUPS - 1)

            def x_quant(c):
                settle_wait(act, (xq_v, c + 1))
                v = y1[:, c * SUP:(c + 1) * SUP] if isinstance(c, int) else y1[:, ds(c * SUP, SUP)]
                A.activation(xq, v.rearrange("p a b -> p (a b)"), ACT.Identity, bias=par(X, ZP), scale=par(X, INV))\
                    .then_inc(xq_q, 1)

            def x_high(c, s):
                act.wait_ge(xq_v, c + 2)
                act.wait_ge(xq_t, c * SUP + SUP)
                A.activation(xhl[:, s, 0], xv[:, s], ACT.Copy).then_inc(xq_hi, 1)

            def x_copy(c):
                for t in (2, 3):
                    settle_wait(act, (xq_t, c * SUP + t + 1 + 2 * SUP))
                    tile = c * SUP + t
                    dst = xT[:, :, tile * P:(tile + 1) * P] if isinstance(c, int) else xT[:, :, ds(tile * P, P)]
                    A.activation(dst, bank[4 + t][:, :].bitcast(F16).rearrange("p (a b) -> p a b", a=8), ACT.Copy)\
                        .then_inc(xq_ea, 1)

            act.wait_ge(s_par, 1)
            act.wait_ge(s_x1o, 16 + 16 * GROUPS)
            x_quant(0)
            with act.Fori(0, (CHUNKS - 2) // 2) as i:
                for s in range(2):
                    x_high(i * 2 + s, s)
                    x_quant(i * 2 + s + 1)
                    x_copy(i * 2 + s)
            x_high(CHUNKS - 2, 0)
            x_quant(CHUNKS - 1)
            x_copy(CHUNKS - 2)
            x_high(CHUNKS - 1, 1)
            x_copy(CHUNKS - 1)

            def raw_out(pair, m, slot, c, buf, mm, ev, rd, stored, scale):
                if c == 0:
                    act.wait_ge(stored[slot], pair * 16 + 16)
                    act.wait_ge(rd, m + 1)
                settle_wait(act, (mm, m * CHUNKS + c + 1))
                col = scale[:, m:m + 1] if isinstance(m, int) else scale[:, ds(m, 1)]
                A.activation(buf[:, slot, c * NC:(c + 1) * NC], bank[c % 4][:, :], ACT.Copy, scale=col)\
                    .then_inc(ev, 1)

            def gate_step(pair, slot):
                m = pair * 2 + slot
                for c in range(CHUNKS):
                    raw_out(pair, m, slot, c, gbuf, g_mm, g_ev, g_rd, g_st, gS)
                    if c == 3:
                        dst = wuT[:, :, m * P:(m + 1) * P] if isinstance(m, int) else wuT[:, :, ds(m * P, P)]
                        copy_weights(m + U0, 0, dst)
                    if c == 7:
                        dst = wdT8[:, m] if isinstance(m, int) else \
                            wdT8[:, ds(m, 1)].rearrange("p a b c -> p (a b) c")
                        copy_weights(m + U1, 1, dst)

            with act.Fori(0, (MT - 1) // 2) as i:
                for s in range(2):
                    gate_step(i, s)
            gate_step((MT - 1) // 2, 0)

            act.wait_ge(s_par, 2)
            A.activation(vmq[:, 0:1], par(G, 5), ACT.Identity, bias=par(G, ZP), scale=par(G, INV)).then_inc(s_vma, 1)
            act.wait_ge(s_vm, 1)
            A.activation(vm[:, 1:2], vm[:, 0:1], ACT.Sigmoid, scale=par(G, NSC)).then_inc(s_vma, 1)

            def gate_quant(m, half):
                n = m * 2 + half
                act.wait_ge(s_gin[half], m * 16 + 16)
                act.wait_ge(s_nv, n + 1)
                A.activation(gq, graw[:, half], ACT.Identity, bias=par(G, ZP), scale=par(G, INV)).then_inc(s_gq, 1)

            def gate_sigmoid(m, half):
                n = m * 2 + half
                act.wait_ge(s_nv, n + 2)
                act.wait_ge(s_sq, n + 1)
                A.activation(sig, nv[:, half], ACT.Sigmoid, scale=par(G, NSC)).then_inc(s_sig, 1)

            def up_step(pair, slot):
                m = pair * 2 + slot
                for c in range(CHUNKS):
                    raw_out(pair, m, slot, c, ubuf, u_mm, u_ev, u_rd, u_st, uS)
                    if c == 1 or c == 5:
                        gate_quant(m, c // 4)
                    if c == 3 or c == 7:
                        gate_sigmoid(m, c // 4)

            for s in range(2):
                act.wait_ge(g_st[s], 16 + 16 * N_SLOT[s])
            with act.Fori(0, (MT - 1) // 2) as i:
                for s in range(2):
                    up_step(i, s)
            up_step((MT - 1) // 2, 0)

            act.wait_ge(s_par, 4)
            with act.Fori(0, MT) as m:
                for half in range(2):
                    act.wait_ge(s_pin[half], m * 32 + 32)
                    act.wait_ge(s_v2, m * 4 + half * 2 + 2)
                    A.activation(qg[:, half], pin[:, half], ACT.Identity, bias=par(S, ZP), scale=par(S, NINV))\
                        .then_inc(s_q2, 1)
                    A.activation(qu[:, half], uin[:, half], ACT.Identity, bias=par(U, ZP), scale=par(U, INV))\
                        .then_inc(s_q2, 1)

            act.wait_ge(s_par, 5)
            with act.Fori(0, CHUNKS // 2) as i:
                for s in range(2):
                    c = i * 2 + s
                    act.wait_ge(s_din[s], i * 16 + 16)
                    act.wait_ge(s_dv, c + 1)
                    A.activation(qd, pd[:, s], ACT.Identity, bias=par(O, ZP), scale=par(O, INV)).then_inc(s_dq, 1)
                    act.wait_ge(s_dv, c + 2)
                    act.wait_ge(s_dmm, c * SUP + SUP)
                    A.activation(hd[:, s, 0:CH], vd, ACT.Copy).then_inc(s_dhi, 1)

        @block.gpsimd
        def _(pool):
            G_ = nc.gpsimd
            pc = Chain(pool, pch)

            def load(dst, src, signal):
                pool.dma_start(dst, src).then_inc(signal, 16)

            load(cw[0:CHAN, :], a["L1_cond_c_weight"], s_mixn)
            mix_v = a["L0_cond_weight"].rearrange("k o i a -> (k o) (i a)").rearrange("(t p) i -> p t i", p=P)
            for j in range(BPT):
                load(mixnat[:, :, CHAN * j:CHAN * (j + 1)], mix_v, s_mixn)
                load(side[CHAN * j:CHAN * (j + 1), :], a["fside_S_0"].rearrange("(p a) -> p a", a=1), s_mixn)

            MIX_STEPS = 14

            def mix(g):

                def part(k, dst, lo=0, n=P):
                    rep = attrep[lo:lo + n, g * GT:(g + 1) * GT, k] if isinstance(g, int) else \
                        attrep[lo:lo + n, ds(g * GT, GT), k]
                    s_ = [n, GT, CHAN]
                    return G_.tensor_tensor(dst, mixT[lo:lo + n, k].unsqueeze(1).broadcast_to(s_),
                                            rep.unsqueeze(2).broadcast_to(s_), ALU.mult)

                acc = mixacc[:, 0].rearrange("p (t o) -> p t o", t=GT)
                tmp = [mixtmp[:, j].rearrange("p (t o) -> p t o", t=GT) for j in range(2)]
                pc(part(0, acc))
                for k in range(1, MIX_K):
                    pc.then(part(k, tmp[k % 2]))
                    if k < MIX_K - 1:
                        pc(G_.tensor_tensor(acc, acc, tmp[k % 2], ALU.add))
                pc.settle()
                if not isinstance(g, int):
                    pool.wait_ge(s_y0, g * GT)
                for b in range(BPT):
                    r = slice(CHAN * b, CHAN * (b + 1))
                    G_.tensor_tensor(mixbd[r, :, r], acc[r], tmp[(MIX_K - 1) % 2][r], ALU.add).then_inc(s_bd, 1)
                pool.wait_ge(s_bd, g * BPT + BPT)

            pool.wait_ge(s_ev, EV_AT["attrep"])
            mix(0)
            start = pc.start()
            with pool.Fori(0, GROUPS - 1) as i:
                pc.iteration(start, i, MIX_STEPS)
                mix(i + 1)
            pc.end(start, GROUPS - 1, MIX_STEPS)
            for which in (X, G, S, U, O):
                pool.wait_ge(s_st, which + 1)
                G_.partition_all_reduce(red[:, which, :], st[:, which, :], P, RMAX).then_inc(s_red, 1)

        @block.tensor
        def _(pe):
            T = nc.tensor
            for s in range(2):
                pe.sem_inc(hl_turned[s], 1)
            pe.sem_inc(s_cv, 1)
            pe.sem_inc(xq_t, 2 * SUP)
            pe.sem_inc(s_dmm, 2 * SUP)

            def b16(i):
                return bank[i][:, :].bitcast(F16)

            pe.wait_ge(s_load, 16 * N_SMALL)
            pe.wait_ge(s_mixn, 16 * 9)
            pe.wait_ge(s_zero, 2)
            T.transpose(bank[0][:, 0:P], cond, ident).then_inc(s_pe, 1)
            for t in range(KT):
                last = T.transpose(bank[1][:, t * AWN:(t + 1) * AWN], aw[0:AWN, t * P:(t + 1) * P],
                                   cst[0:AWN, C_ID:C_ID + AWN])
            last.then_inc(s_pe, 1)
            for t in range(4):
                last = T.transpose(bank[2][0:ER, t * P:(t + 1) * P], bnat[:, t], ident)
            last.then_inc(s_pe, 1)
            for t in range(2):
                last = T.transpose(bank[3][:, t * P:(t + 1) * P], mixnat[:, t], ident)
            last.then_inc(s_pe, 1)
            T.transpose(bank[4][:, 0:CHAN], cw[0:CHAN, :], cst[0:CHAN, C_ID:C_ID + CHAN]).then_inc(s_pe, 1)
            pe.wait_ge(s_ev, EV_AT["condT"])
            T.matmul(bank[5][:, 0:P], w0, condT, start=True, stop=True).then_inc(s_pe, 1)
            pe.wait_ge(s_act, 1)
            T.matmul(bank[6][:, 0:P], w1, h1T, start=True, stop=True).then_inc(s_pe, 1)
            pe.wait_ge(s_act, 2)
            T.matmul(bank[7][:, 0:MIX_K], h2T, w2, start=True, stop=False)
            T.matmul(bank[7][:, 0:MIX_K], ones[0:1, :], b2[0:1, :], start=False, stop=True).then_inc(s_pe, 1)
            pe.wait_ge(s_ev, EV_AT["att"])
            T.transpose(bank[0][0:MIX_K, 0:P], att, ident).then_inc(s_pe, 1)
            pe.wait_ge(s_ev, EV_AT["attT"])
            attT_v = attT[0:MIX_K, :].rearrange("k (q b) -> k b q", b=BPT)
            for b in range(BPT):
                last = T.matmul(bank[1][CHAN * b:CHAN * (b + 1), 0:TILES], biask[0:MIX_K, :], attT_v[:, b],
                                start=True, stop=True)
            last.then_inc(s_pe, 1)
            condT_v = condT.rearrange("d (s j i) -> d j s i", j=BPT, i=SUP)
            for j in range(BPT):
                last = T.matmul(bank[2][CHAN * j:CHAN * (j + 1), 0:TILES].rearrange("p (s i) -> p s i", i=SUP),
                                cwT, condT_v[:, j], start=True, stop=True)
            last.then_inc(s_pe, 1)
            pe.wait_ge(s_ev, EV_AT["attexp"])
            T.matmul(bank[3][:, 0:TILES * MIX_K], cst[:, C_PICK:C_PICK + P], attexp.rearrange("p a b -> p (a b)"),
                     start=True, stop=True).then_inc(s_pe, 1)
            for t in range(KT):
                last = T.matmul(bank[4][:, 0:AWN], ones[:, :], awT[:, t], start=(t == 0), stop=(t == KT - 1))
            last.then_inc(s_pe, 1)

            def turn(u, slot):
                pe.wait_ge(hl_ready[slot], u + 1)
                pe.wait_ge(wt_copied[slot], u + 1)
                for b in range(8):
                    last = T.transpose(b16(4 + slot)[:, b * P:(b + 1) * P], wsp[:, slot, b * P:(b + 1) * P], id16[:, :])
                last.then_inc(hl_turned[slot], 1)

            pe.wait_ge(s_ev, EV_AT["sumaw"])
            with pe.Fori(0, (MT - 1) // 2) as i:
                for s in range(2):
                    turn(i, s)
            turn((MT - 1) // 2, 0)

            def y0(g, t):
                pe.wait_ge(s_y0e, g * GT + t + 1)
                for k in range(KT):
                    last = T.matmul(bank[t % 2][:, k * P:(k + 1) * P], xin[:, t, k * P:(k + 1) * P], mixbd[:, t],
                                    start=True, stop=True)
                last.then_inc(s_y0, 1)

            def z(g, t):
                pe.wait_ge(s_y0e, g * GT + t + 3)
                for k in range(KT):
                    last = T.matmul(bank[2 + t // SUP][:, (t % SUP) * AWN:(t % SUP + 1) * AWN],
                                    y0T[:, t % 2, k * P:(k + 1) * P], awT[:, k], start=(k == 0), stop=(k == KT - 1))
                last.then_inc(s_z1, 1)

            def mixed(g):
                pe.wait_ge(s_bd, g * BPT + BPT)
                pe.wait_ge(s_xin, g * 16 + 16)
                if not isinstance(g, int):
                    pe.wait_ge(s_cve, g * GT - SUP)
                y0(g, 0)
                for t in range(GT):
                    if t + 1 < GT:
                        y0(g, t + 1)
                    z(g, t)

            def delta(g):
                settle_wait(pe, (s_gm, g + 1), (s_cve, g * GT + GT))
                for h in range(2):
                    for t in range(SUP):
                        last = T.transpose(bank[4 + h][0:ER, t * P:(t + 1) * P], gmid[:, h * SUP + t], ident)
                    last.then_inc(s_gt, 1)
                for t in range(GT):
                    if t % SUP == 0:
                        pe.wait_ge(s_gte, g * 2 + t // SUP + 1)
                    pe.wait_ge(s_x1, g * GT + t + 1)
                    T.matmul(bank[6 + t % 2][:, :], gmidT[0:ER, t], bT[0:ER, 0], start=True, stop=True)\
                        .then_inc(s_dl, 1)

            def convolve(g):
                for s in range(2):
                    settle_wait(pe, (s_x1, g * GT + s * SUP + SUP + 2))
                    for k in range(KTAP):
                        for j in range(BPT):
                            for i in range(BPT):
                                r = slice(CHAN * i, CHAN * (i + 1))
                                last = T.matmul(bank[s * SUP + i][CHAN * j:CHAN * (j + 1), :], wk[r, :, k],
                                                xc[r, s * SUP + j, k:k + H], start=(k == 0), stop=(k == KTAP - 1))
                    last.then_inc(s_cv, 1)

            mixed(0)
            pe.wait_ge(s_wk, 16 * 16)
            with pe.Fori(0, GROUPS - 1) as g:
                delta(g)
                mixed(g + 1)
                pe.wait_ge(s_y0e, g * GT + 2 * GT + 2)
                pe.wait_ge(s_ze, g * 2 + 4)
                convolve(g)
            delta(GROUPS - 1)
            convolve(GROUPS - 1)

            def x_turn(c, s):
                pe.wait_ge(xq_lo, c + 1)
                for t in range(SUP):
                    copied = xq_ed if t < 2 else xq_ea
                    pe.wait_ge(copied, c * 2 + t % 2 + 1)
                    for b in range(8):
                        src = xhl[:, s, b // KT, t * H + (b % KT) * P:t * H + (b % KT + 1) * P]
                        last = T.transpose(b16(4 + t)[:, b * P:(b + 1) * P], src, id16[:, :])
                    last.then_inc(xq_t, 1)

            pe.wait_ge(s_cve, GROUPS * GT + GT)
            with pe.Fori(0, CHUNKS // 2) as i:
                for s in range(2):
                    x_turn(i * 2 + s, s)

            def project(m, w, mm, ev, units):
                for c in range(CHUNKS):
                    pe.wait_ge(xq_ed, c * 2 + 4)
                    pe.wait_ge(xq_ea, c * 2 + 4)
                    pe.wait_ge(ev, m * CHUNKS + c + 1)
                    n = 0
                    for k in range(KT):
                        for wh, xh in ((0, 0), (0, 1), (1, 0)):
                            blk = wh * KT + k
                            lhs = w[:, blk, m * P:(m + 1) * P] if isinstance(m, int) else w[:, blk, ds(m * P, P)]
                            last = T.matmul(bank[c % 4][:, :], lhs, xT[:, xh * KT + k, c * NC:(c + 1) * NC],
                                            start=(n == 0), stop=(n == 3 * KT - 1))
                            n += 1
                    last.then_inc(mm, 1)
                    if units and c == 3:
                        turn(m + U0, 0)
                    if units and c == 7:
                        turn(m + U1, 1)

            pe.wait_ge(wt_copied[0], U0 + 1)
            pe.wait_ge(wt_copied[1], U1 + 1)
            with pe.Fori(0, MT) as m:
                project(m, wgT, g_mm, g_ev, True)
            pe.wait_ge(wt_copied[0], U0 + MT + 1)
            pe.wait_ge(wt_copied[1], U1 + MT + 1)
            pe.wait_ge(g_ev, MT * CHUNKS + 4)
            with pe.Fori(0, MT) as m:
                project(m, wuT, u_mm, u_ev, False)

            for t in range(KT):
                pe.wait_ge(s_dg, t + 1)
                T.matmul(bank[7][:, t * P:(t + 1) * P], ones[:, :], dgS[:, :], start=True, stop=True)\
                    .then_inc(s_row, 1)

            def down(c, s):
                pe.wait_ge(s_dlo, c + 1)
                for t in range(SUP):
                    pe.wait_ge(s_dev, c * SUP + t + 1)
                    n = 0
                    for m in range(MT):
                        for vh, wh in ((0, 0), (0, 1), (1, 0)):
                            o_ = vh * CH + m * NC + t * P
                            last = T.matmul(bank[t][:, :], hd[:, s, o_:o_ + P], wdT[:, m, wh], start=(n == 0),
                                            stop=(n == 3 * MT - 1))
                            n += 1
                    last.then_inc(s_dmm, 1)

            pe.wait_ge(u_ev, MT * CHUNKS + 4)
            with pe.Fori(0, CHUNKS // 2) as i:
                for s in range(2):
                    down(i * 2 + s, s)


_INS = ["x", "cond_128", "fside_S_0", "L0_cond_W0", "L0_cond_b0", "L0_cond_W1", "L0_cond_b1", "L0_cond_W2",
        "L0_cond_b2", "L0_cond_weight", "L0_cond_bias_k", "L0_ffn_A", "L0_ffn_B", "L0_ffn_Wr", "L1_cond_weight",
        "L1_cond_c_weight", "L1_ffn_w_gate", "L1_ffn_w_up", "L1_ffn_w_down"]


def kernel(**inputs):
    import concourse.bacc as bacc
    from concourse.bass_utils import run_bass_kernel_spmd

    nc = bacc.Bacc("TRN2", target_bir_lowering=False, num_devices=1)
    arrays, args = {}, {}
    for name in _INS + ["consts"]:
        v = constants() if name == "consts" else np.ascontiguousarray(inputs[name])
        arrays[f"in_{name}"] = v
        args[name] = nc.dram_tensor(f"in_{name}", v.shape, mybir.dt.from_np(v.dtype), kind="ExternalInput").ap()
    result = nc.dram_tensor("out", (BATCH, CHAN, H), F32, kind="ExternalOutput").ap()
    build(nc, args, result)
    r = run_bass_kernel_spmd(nc, [arrays], core_ids=[0])
    return r.results[0]["out"]
```

```python
from contextlib import ExitStack

import numpy as np

import concourse.bass as bass
from concourse import mybir

ALU = mybir.AluOpType
ACT = mybir.ActivationFunctionType
AX = mybir.AxisListType
F32 = mybir.dt.float32
F16 = mybir.dt.float16
I32 = mybir.dt.int32
U16 = mybir.dt.uint16
RMAX = bass.bass_isa.ReduceOp.max
ds = bass.ds

P = 128
BATCH, CHAN, H = 128, 32, 512
TOK = BATCH * CHAN
TILES = TOK // P
BPT = P // CHAN
GT = 8
GROUPS = TILES // GT
SUP = 4
KTAP, PAD = 9, 4
KUP = 64.0
KT = H // P
EXP_N, TOPK, RANK, MIX_K = 4, 2, 16, 8
ER = EXP_N * RANK
AWN = ER + EXP_N
SCALE = 16.0 / 4.0
INNER = 1376
MT = -(-INNER // P)
INNER_P = MT * P
LAST = INNER - (MT - 1) * P
NC = 512
CHUNKS = TOK // NC
HALF = TOK // 2
BLK = 32
NB = H // BLK
MAGIC = 1.5 * 2.0 ** 23
QMAX = 65535.0
WMAX = 7.0
TINY = 1e-12
WUP = 1024.0
VDN = 1.0 / 16.0
SIG_ONE = 65536.0


def constants():
    ident = np.eye(P, dtype=np.float32)
    b = np.arange(P)
    pick = (b[:, None] % BPT == b[None, :] // CHAN).astype(np.float32)
    tile_of = (b[:, None] // BPT == np.arange(TILES)[None, :]).astype(np.float32)
    e, j = np.meshgrid(np.arange(EXP_N), np.arange(EXP_N), indexing="ij")
    before = np.broadcast_to((j < e).astype(np.float32).reshape(1, -1), (P, EXP_N * EXP_N))
    after = np.broadcast_to((j > e).astype(np.float32).reshape(1, -1), (P, EXP_N * EXP_N))
    return np.ascontiguousarray(np.concatenate([ident, pick, tile_of, before, after], axis=1))


C_ID, C_PICK, C_TILE, C_BEF, C_AFT, C_END = 0, P, 2 * P, 2 * P + TILES, 2 * P + TILES + 16, 2 * P + TILES + 32

PE_SETUP = ["condT", "awT", "bT", "mixT", "cwT", "h1", "h2", "logits", "attT", "aggb", "ctx", "attrep", "sumaw"]
EV_SETUP = ["id16", "condT", "awT", "bT", "mixT", "cwT", "negmax", "att", "attT", "aggb", "ctx", "attexp", "attrep",
            "sumaw"]
PE_AT = {n: i + 1 for i, n in enumerate(PE_SETUP)}
EV_AT = {n: i + 1 for i, n in enumerate(EV_SETUP)}


def pick1(ap, i):
    if isinstance(i, int):
        return ap[:, i]
    one = ap[:, ds(i, 1)]
    return one.rearrange("p a b -> p (a b)") if len(one.shape) == 3 else one.rearrange("p a b c -> p (a b) c")


class Chain:

    def __init__(self, eng, sem):
        self.eng, self.sem, self.base, self.n = eng, sem, 0, 0

    def __call__(self, ins):
        ins.then_inc(self.sem, 1)
        self.n += 1
        return ins

    def settle(self):
        self.eng.wait_ge(self.sem, self.base + self.n)

    def then(self, ins):
        self(ins)
        self.settle()

    def start(self):
        self.base, self.n = self.base + self.n, 0
        return self.base

    def iteration(self, start, i, per):
        self.base, self.n = start + i * per, 0

    def end(self, start, count, per):
        assert self.n == per, (self.n, per)
        self.base, self.n = start + count * per, 0


def build(nc, a, out):
    with ExitStack() as ctx:
        def sb(name, shape, dt):
            return ctx.enter_context(nc.sbuf_tensor("sb_" + name, shape, dt))

        def sem(name):
            return ctx.enter_context(nc.semaphore(name))

        def dram(name, shape):
            return nc.dram_tensor(name, shape, F32, kind="Internal").ap()

        KB = 1024
        WT = 8 * INNER_P * 2
        O_A, O_B, O_WG, O_WU = 0, 64 * KB, 128 * KB, 128 * KB + WT
        arena = sb("arena", [P, (O_WU + WT) // 4], F32)
        wd_region = sb("wd_region", [P, WT // 4], F32)

        def view(region, off, shape, dt):
            size = int(np.prod(shape)) * (2 if dt in (F16, U16) else 4)
            assert off % 4 == 0 and size % 4 == 0
            v = region[:, off // 4:(off + size) // 4]
            if dt != F32:
                v = v.bitcast(dt)
            if len(shape) == 2:
                v = v.rearrange("p (a b) -> p a b", a=shape[0])
            if len(shape) == 3:
                v = v.rearrange("p (a b c) -> p a b c", a=shape[0], b=shape[1])
            return v

        at = lambda off, shape, dt: view(arena, off, shape, dt)

        wgT = at(O_WG, [8, INNER_P], F16)
        wuT = at(O_WU, [8, INNER_P], F16)
        wdT = view(wd_region, 0, [MT, 2, H], F16)
        wdT8 = view(wd_region, 0, [MT, 8, P], F16)
        xT = at(O_B, [8, TOK], F16)
        y1 = at(O_A, [TILES, H], F32)
        xin = at(O_B, [GT, H], F32)
        xres = at(O_B + 16 * KB, [GT, H], F32)
        PW = H + 2 * PAD
        xh0 = at(O_B + 32 * KB, [GT, PW], F16)
        xl0 = at(O_B + 32 * KB + GT * PW * 2, [GT, PW], F16)
        o = O_B + 32 * KB + GT * PW * 4
        mixbd = at(o, [GT, P], F32)
        o += GT * P * 4
        y0T = at(o, [2, H], F32)
        o += 2 * H * 4
        zbuf = at(o, [GT, AWN], F32)
        o += GT * AWN * 4
        zbias = at(o, [SUP, AWN], F32)
        o += SUP * AWN * 4
        gmid = at(o, [GT, ER], F32)
        assert o + GT * ER * 4 <= O_WG
        o = O_WU
        gmidT = at(o, [GT, P], F32)
        o += GT * P * 4
        mixtmp = at(o, [2, GT * CHAN], F32)
        o += 2 * GT * CHAN * 4
        mixacc = at(o, [1, GT * CHAN], F32)
        o += GT * CHAN * 4
        gate_t = at(o, [8, GT * 16], F32)
        o += 8 * GT * 16 * 4
        wk = at(o, [CHAN, KTAP], F32)
        o += CHAN * KTAP * 4
        mixT = at(o, [MIX_K, CHAN], F32)
        o += MIX_K * CHAN * 4
        attrep = at(o, [TILES, MIX_K], F32)
        o += TILES * MIX_K * 4
        awT = at(o, [KT, AWN], F32)
        o += KT * AWN * 4
        sumaw = at(o, [1, AWN], F32)
        o += AWN * 4
        bT = at(o, [1, H], F32)
        o += H * 4
        aggb = at(o, [1, TILES], F32)
        o += TILES * 4
        assert o <= O_WU + WT
        o = O_A
        cond = at(o, [1, P], F32)[:, 0]
        condT = at(o + 512, [1, P], F32)[:, 0]
        w0 = at(o + 1024, [1, P], F32)[:, 0]
        w1 = at(o + 1536, [1, P], F32)[:, 0]
        h1T = at(o + 2048, [1, P], F32)[:, 0]
        h2T = at(o + 2560, [1, P], F32)[:, 0]
        w2 = at(o + 3072, [1, MIX_K], F32)[:, 0]
        b2 = at(o + 3104, [1, MIX_K], F32)[:, 0]
        b01 = at(o + 3136, [1, 2], F32)[:, 0]
        side = at(o + 3144, [1, 1], F32)[:, 0]
        smx = at(o + 3148, [1, 4], F32)[:, 0]
        expv = at(o + 3164, [1, MIX_K], F32)[:, 0]
        att = at(o + 3196, [1, MIX_K], F32)[:, 0]
        biask = at(o + 3228, [1, CHAN], F32)[:, 0]
        attT = at(o + 3356, [1, P], F32)[:, 0]
        cw = at(o + 3868, [1, P], F32)[:, 0]
        cwT = at(o + 4380, [1, CHAN], F32)[:, 0]
        attexp = at(o + 4508, [TILES, MIX_K], F32)
        aw = at(o + 6144, [1, H], F32)[:, 0]
        bnat = at(o + 8192, [4, ER], F32)
        mixnat = at(o + 9216, [2, P], F32)
        def prep_buffers(region, o):
            return (view(region, o, [2, H], F32), view(region, o + 4 * KB, [2, H], F32),
                    view(region, o + 8 * KB, [2, 8 * P], F16), view(region, o + 12 * KB, [8, NB], F32))

        prep_a, prep_b = prep_buffers(wd_region, 0), prep_buffers(arena, O_A + 48 * KB)
        wbd = view(wd_region, 13 * KB, [2, KTAP, P], F16)
        wdnat = at(O_A + 16 * KB, [KT, INNER], F32)
        xq = at(O_WU, [1, SUP * H], U16)[:, 0]
        xv = at(O_WU + 4 * KB, [2, SUP * H], F32)
        xhl = view(wd_region, 0, [2, 2, SUP * H], F16)
        gbuf = at(O_A, [2, TOK], F32)
        ubuf = at(O_A, [2, TOK], F32)
        graw = at(O_A + 32 * KB, [2, HALF], F32)
        gq = at(O_A + 48 * KB, [1, HALF], U16)[:, 0]
        sq = at(O_A + 52 * KB, [1, HALF], U16)[:, 0]
        sig = at(O_A + 56 * KB, [1, HALF], F32)[:, 0]
        nv = at(O_WG, [2, HALF], F32)
        pin = at(O_A, [2, HALF], F32)
        uin = at(O_A + 16 * KB, [2, HALF], F32)
        qg = at(O_A + 32 * KB, [2, HALF], U16)
        qu = at(O_A + 40 * KB, [2, HALF], U16)
        vg = at(O_A + 48 * KB, [1, HALF], F32)[:, 0]
        vu = at(O_A + 56 * KB, [1, HALF], F32)[:, 0]
        prod = at(O_B, [2, HALF], F32)
        CH = MT * NC
        o = O_A
        pd = at(o, [2, CH], F32)
        o += 2 * CH * 4
        qd = at(o, [1, CH], U16)[:, 0]
        o += CH * 2
        vd = at(o, [1, CH], F32)[:, 0]
        o += CH * 4
        hd = at(o, [2, 2 * CH], F16)
        o += 2 * CH * 4
        x1b = at(o, [2, SUP * H], F32)
        o += 2 * SUP * H * 4
        ob = at(o, [2, SUP * H], F32)
        o += 2 * SUP * H * 4
        otmp = at(o, [2, H], F32)
        o += 2 * H * 4
        assert o <= O_WU + WT

        cst = sb("cst", [P, C_END], F32)
        id16 = sb("id16", [P, P], F16)
        ones = sb("ones", [P, P], F32)
        ctxcol = sb("ctxcol", [P, TILES], F32)
        gS = sb("gS", [P, MT], F32)
        uS = sb("uS", [P, MT], F32)
        dS = sb("dS", [P, KT], F32)
        dR = sb("dR", [P, KT], F32)
        rS = sb("rS", [P, 2, 1], F32)
        rowv = sb("rowv", [P, H], F32)
        dgS = sb("dgS", [P, P], F32)
        st_hi = sb("st_hi", [P, 2 * MT], F32)
        st_lo = sb("st_lo", [P, 2 * MT], F32)
        st = sb("st", [P, 5, 2], F32)
        red = sb("red", [P, 5, 2], F32)
        rg = sb("rg", [P, 5, 16], F32)
        vm = sb("vm", [P, 4], F32)
        vmq = sb("vmq", [P, 2], U16)
        st2 = sb("st2", [P, 2], F32)
        ident = cst[:, C_ID:C_ID + P]
        bank = [ctx.enter_context(nc.psum_tensor(f"bank{i}", [P, 512], F32)) for i in range(8)]

        X, G, S, U, O = range(5)
        SC, INV, ZP, NSC, NINV = 0, 1, 2, 3, 4

        def par(which, col):
            return rg[:, which, col:col + 1]

        x1d = dram("x1_rows", (TOK, H))
        gd = dram("gate_raw", (MT, P, TOK))
        ud = dram("up_raw", (MT, P, TOK))
        sd = dram("gated_raw", (MT, P, TOK))
        od = dram("product_raw", (MT, P, TOK))

        s_load = sem("setup_loaded")
        s_wk = sem("conv_weights_loaded")
        s_wdn = sem("down_rows_loaded")
        s_pe = sem("setup_pe")
        s_ev = sem("setup_evacuated")
        s_act = sem("setup_act")
        s_wbd = sem("conv_weights_split")
        s_hi0 = sem("x1_high")
        s_lo0 = sem("x1_low")
        s_zero = sem("zeroed")
        s_none = sem("carries_waits")
        dch = sem("vector_steps")
        pch = sem("pool_steps")
        s_xin = sem("xin_loaded")
        s_xres = sem("xres_loaded")
        s_bd = sem("mix_ready")
        s_y0 = sem("y0_done")
        s_y0e = sem("y0_evacuated")
        s_ze = sem("z_evacuated")
        s_d4 = sem("logits_shifted")
        s_exp = sem("gates_exp")
        s_gm = sem("gated_mid")
        s_gt = sem("gated_mid_turned")
        s_gte = sem("gated_mid_copied")
        s_dl = sem("delta_done")
        s_x1 = sem("x1_ready")
        s_x1o = sem("x1_stored")
        s_cv = sem("conv_done")
        s_cve = sem("conv_evacuated")
        wn_in = [sem(f"wn_loaded{i}") for i in range(2)]
        wn_used = [sem(f"wn_used{i}") for i in range(2)]
        hl_ready = [sem(f"w_split{i}") for i in range(2)]
        hl_turned = [sem(f"w_turned{i}") for i in range(2)]
        wt_copied = [sem(f"w_copied{i}") for i in range(2)]
        s_mixn = sem("setup_loaded_pool")
        s_z1 = sem("z_tile_done")
        s_dg = sem("diagonal_ready")
        s_row = sem("row_scales_done")
        s_ob = sem("out_ready")
        s_st = sem("stats_ready")
        s_red = sem("range_reduced")
        s_par = sem("range_known")
        s_vm = sem("largest_gate")
        s_vma = sem("largest_gate_act")
        xq_q = sem("x_quantised")
        xq_v = sem("x_integer")
        xq_hi = sem("x_high")
        xq_lo = sem("x_low")
        xq_t = sem("x_turned")
        xq_ed = sem("x_turned_copied_dve")
        xq_ea = sem("x_turned_copied_act")
        g_mm = sem("gate_mm")
        g_ev = sem("gate_evacuated")
        g_st = [sem(f"gate_stored{i}") for i in range(2)]
        g_rd = sem("gate_reduced")
        u_mm = sem("up_mm")
        u_ev = sem("up_evacuated")
        u_st = [sem(f"up_stored{i}") for i in range(2)]
        u_rd = sem("up_reduced")
        s_gin = [sem(f"gate_loaded{i}") for i in range(2)]
        s_gq = sem("gate_quantised")
        s_nv = sem("gate_integer")
        s_sig = sem("sigmoid_done")
        s_sq = sem("sigmoid_quantised")
        s_pr = sem("gated_ready")
        s_pst = [sem(f"gated_stored{i}") for i in range(2)]
        s_pin = [sem(f"product_inputs_loaded{i}") for i in range(2)]
        s_q2 = sem("product_inputs_quantised")
        s_v2 = sem("product_inputs_read")
        s_po = sem("product_ready")
        s_pos = [sem(f"product_stored{i}") for i in range(2)]
        s_din = [sem(f"down_input_loaded{i}") for i in range(2)]
        s_dq = sem("down_quantised")
        s_dv = sem("down_integer")
        s_dhi = sem("down_high")
        s_dlo = sem("down_low")
        s_dmm = sem("down_mm")
        s_dev = sem("down_evacuated")
        s_x1i = [sem(f"x1_loaded{i}") for i in range(2)]
        s_out = [sem(f"out_stored{i}") for i in range(2)]

        N_SMALL = 15
        N_SLOT = ((MT + 1) // 2, MT // 2)
        U0, U1 = N_SLOT

        TURN_AFTER = {t: 2 * (GROUPS - 1) + k for k, t in enumerate((2, 3, 5, 6, 7))}
        assert max(TURN_AFTER.values()) == MT - 1

        UNIT_AFTER = {5: 0, 7: 1}
        LAST_UNIT_AFTER = {2: 0, 4: 1}

        def settle_wait(eng, *waits):
            for s, v in waits:
                eng.wait_ge(s, v)
            eng.sem_inc(s_none, 1)

        block = ctx.enter_context(nc.Block())

        @block.sync
        def _(sp):
            def small(dst, src):
                sp.dma_start(dst, src).then_inc(s_load, 16)

            small(cst[:, :], a["consts"])
            small(cond, a["cond_128"])
            small(w0, a["L0_cond_W0"])
            small(w1, a["L0_cond_W1"])
            small(w2, a["L0_cond_W2"])
            small(b01[:, 0:1], a["L0_cond_b0"].rearrange("(p a) -> p a", a=1))
            small(b01[:, 1:2], a["L0_cond_b1"].rearrange("(p a) -> p a", a=1))
            small(b2[0:1, :], a["L0_cond_b2"].rearrange("(a k) -> a k", a=1))
            small(biask[0:MIX_K, :], a["L0_cond_bias_k"])
            small(aw[0:ER, :], a["L0_ffn_A"].rearrange("e r f -> (e r) f"))
            small(aw[ER:AWN, :], a["L0_ffn_Wr"])
            for e in range(EXP_N):
                small(bnat.rearrange("p t (e r) -> p t e r", e=EXP_N)[:, :, e, :],
                      a["L0_ffn_B"][e].rearrange("(t p) r -> p t r", p=P))
            x_v = a["x"].rearrange("(t b) c h -> (b c) t h", b=BPT)
            sp.dma_start(xin, x_v[:, 0:GT, :]).then_inc(s_xin, 16)
            sp.dma_start(xres, x_v[:, 0:GT, :]).then_inc(s_xres, 16)
            wn, wg_v, wu_v = prep_a[0], a["L1_ffn_w_gate"], a["L1_ffn_w_up"]
            for s in range(2):
                sp.dma_start(wn[:, s], wg_v[s * P:(s + 1) * P, :]).then_inc(wn_in[s], 16)
            sp.dma_start(wdnat, a["L1_ffn_w_down"].rearrange("(t p) i -> p t i", p=P)).then_inc(s_wdn, 16)
            wd_v = a["L1_ffn_w_down"].rearrange("(t p) i -> p t i", p=P)

            rows = x1d.rearrange("(t p) h -> p t h", p=P)
            with sp.Fori(0, GROUPS - 1) as g:
                sp.wait_ge(s_y0, (g + 1) * GT)
                sp.dma_start(xin, x_v[:, ds((g + 1) * GT, GT), :]).then_inc(s_xin, 16)
                sp.wait_ge(s_x1, (g + 1) * GT + 2)
                sp.dma_start(rows[:, ds(g * GT, GT), :], xres).then_inc(s_x1o, 16)
                sp.wait_ge(s_lo0, g * 2 + 2)
                sp.wait_ge(s_x1o, g * 16 + 16)
                sp.dma_start(xres, x_v[:, ds((g + 1) * GT, GT), :]).then_inc(s_xres, 16)
                for s in range(2):
                    settle_wait(sp, (wn_used[s], g + 2))
                    sp.dma_start(wn[:, s], wg_v[ds(g * 2 * P + (2 + s) * P, P), :]).then_inc(wn_in[s], 16)
            sp.wait_ge(s_x1, GROUPS * GT + 2)
            sp.dma_start(rows[:, (GROUPS - 1) * GT:, :], xres).then_inc(s_x1o, 16)
            for m in range(2 * GROUPS, MT - 1):
                sp.wait_ge(wn_used[m % 2], m // 2 + 1)
                sp.dma_start(wn[:, m % 2], wg_v[m * P:(m + 1) * P, :]).then_inc(wn_in[m % 2], 16)
            sp.wait_ge(wn_used[0], (MT - 1) // 2 + 1)
            sp.dma_start(wn[0:LAST, 0], wg_v[(MT - 1) * P:INNER, :]).then_inc(wn_in[0], 16)
            wn = prep_b[0]
            wn3 = wn.rearrange("p s (t i) -> p s t i", t=KT)

            sp.wait_ge(xq_q, CHUNKS)
            for s in range(2):
                sp.sem_inc(g_st[s], 16)

            def load_units(m):
                settle_wait(sp, (wn_used[0], m + U0 + 1))
                sp.dma_start(wn[:, 0], wu_v[ds(m * P, P), :]).then_inc(wn_in[0], 16)
                settle_wait(sp, (wn_used[1], m + U1 + 1))
                sp.dma_start(wn3[:, 1], wd_v[:, :, ds(m * P, P)]).then_inc(wn_in[1], 16)

            def load_last_units():
                sp.wait_ge(wn_used[0], MT - 1 + U0 + 1)
                sp.dma_start(wn[0:LAST, 0], wu_v[(MT - 1) * P:INNER, :]).then_inc(wn_in[0], 16)
                sp.wait_ge(wn_used[1], MT - 1 + U1 + 1)
                sp.dma_start(wn3[:, 1, :, 0:LAST], wd_v[:, :, (MT - 1) * P:INNER]).then_inc(wn_in[1], 16)

            gd_v, ud_v, sd_v, od_v = (t.rearrange("m p t -> p m t") for t in (gd, ud, sd, od))

            def store_gate(m, slot):
                sp.wait_ge(g_ev, (m + 1) * CHUNKS + 4)
                sp.dma_start(pick1(gd_v, m), gbuf[:, slot]).then_inc(g_st[slot], 16)

            load_units(0)
            store_gate(0, 0)
            with sp.Fori(0, (MT - 3) // 2) as i:
                for s in range(2):
                    load_units(i * 2 + s + 1)
                    store_gate(i * 2 + s + 1, 1 - s)
            load_units(MT - 2)
            store_gate(MT - 2, 1)
            load_last_units()
            store_gate(MT - 1, 0)

            def load_gate(m, half):
                sp.wait_ge(s_gq, m * 2 + half - 1)
                sp.dma_start(graw[:, half], pick1(gd_v, m)[:, half * HALF:(half + 1) * HALF])\
                    .then_inc(s_gin[half], 16)

            def store_gated(m, half):
                settle_wait(sp, (s_pr, m * 2 + half + 1))
                sp.dma_start(pick1(sd_v, m)[:, half * HALF:(half + 1) * HALF], nv[:, half]).then_inc(s_pst[half], 16)

            def store_up(m, slot):
                sp.wait_ge(u_ev, (m + 1) * CHUNKS + 4)
                sp.dma_start(pick1(ud_v, m), ubuf[:, 1 - slot]).then_inc(u_st[slot], 16)

            def up_step(m, slot, last=False):
                load_gate(m, 1)
                store_gated(m - 1, 1)
                if not last:
                    load_gate(m + 1, 0)
                store_gated(m, 0)
                store_up(m, slot)

            for s in (1, 0):
                sp.wait_ge(g_st[s], 16 + 16 * N_SLOT[s])
                sp.sem_inc(u_st[1 - s], 16)
                sp.sem_inc(s_pst[s], 16)
            for half in range(2):
                sp.dma_start(graw[:, half], gd_v[:, 0, half * HALF:(half + 1) * HALF]).then_inc(s_gin[half], 16)
            load_gate(1, 0)
            store_gated(0, 0)
            store_up(0, 0)
            with sp.Fori(0, (MT - 3) // 2) as i:
                for s in range(2):
                    up_step(i * 2 + s + 1, 1 - s)
            up_step(MT - 2, 1)
            up_step(MT - 1, 0, last=True)
            store_gated(MT - 1, 1)

            for s in range(2):
                sp.wait_ge(u_st[s], 16 + 16 * N_SLOT[s])
            sp.wait_ge(s_pst[0], 16 + 16 * MT)
            sp.wait_ge(s_pst[1], 16 + 16 * MT)
            sp.wait_ge(u_rd, 2 + MT)
            sp.sem_inc(s_pos[0], 16)
            sp.sem_inc(s_pos[1], 16)

            def load_factors(m, half):
                sp.dma_start(pin[:, half], pick1(sd_v, m)[:, half * HALF:(half + 1) * HALF])\
                    .then_inc(s_pin[half], 16)
                sp.dma_start(uin[:, half], pick1(ud_v, m)[:, half * HALF:(half + 1) * HALF])\
                    .then_inc(s_pin[half], 16)

            def store_product(m, half):
                sp.wait_ge(s_po, m * 2 + half + 1)
                sp.dma_start(pick1(od_v, m)[:, half * HALF:(half + 1) * HALF], prod[:, half])\
                    .then_inc(s_pos[half], 16)

            for half in range(2):
                load_factors(0, half)
            with sp.Fori(0, MT - 1) as m:
                for half in range(2):
                    sp.wait_ge(s_q2, m * 4 + half * 2 + 2)
                    load_factors(m + 1, half)
                for half in range(2):
                    store_product(m, half)
            for half in range(2):
                store_product(MT - 1, half)

            out_v = out.rearrange("(t b) o h -> (b o) t h", b=BPT)

            def rows_of(v, c):
                return v[:, c * SUP:(c + 1) * SUP] if isinstance(c, int) else v[:, ds(c * SUP, SUP)]

            def load_chunk(c, slot):
                src = od_v[:, :, c * NC:(c + 1) * NC] if isinstance(c, int) else od_v[:, :, ds(c * NC, NC)]
                sp.dma_start(pd[:, slot].rearrange("p (m t) -> p m t", m=MT), src).then_inc(s_din[slot], 16)

            def load_x1(c, slot):
                sp.dma_start(x1b[:, slot].rearrange("p (i h) -> p i h", i=SUP), rows_of(rows, c))\
                    .then_inc(s_x1i[slot], 16)

            def store_out(c, slot):
                sp.wait_ge(s_ob, c * SUP + SUP)
                sp.dma_start(rows_of(out_v, c), ob[:, slot].rearrange("p (i h) -> p i h", i=SUP))\
                    .then_inc(s_out[slot], 16)

            sp.wait_ge(s_pos[0], 16 + 16 * MT)
            sp.wait_ge(s_pos[1], 16 + 16 * MT)
            sp.wait_ge(s_par, 5)
            sp.sem_inc(s_out[0], 16)
            sp.sem_inc(s_out[1], 16)
            for c in range(2):
                load_chunk(c, c)
                load_x1(c, c)
            with sp.Fori(0, (CHUNKS - 2) // 2) as i:
                for s in range(2):
                    sp.wait_ge(s_dq, i * 2 + s + 1)
                    load_chunk(i * 2 + s + 2, s)
                    store_out(i * 2 + s, s)
                    load_x1(i * 2 + s + 2, s)
            for c in (CHUNKS - 2, CHUNKS - 1):
                store_out(c, c % 2)
            for s in range(2):
                sp.wait_ge(s_out[s], 16 + 16 * (CHUNKS // 2))

        @block.vector
        def _(dve):
            ch = Chain(dve, dch)
            V = nc.vector

            ch(V.memset(wk.rearrange("p a b -> p (a b)"), 0.0))
            ch(V.memset(mixbd.rearrange("p a b -> p (a b)"), 0.0))
            for half in (xh0, xl0):
                ch(V.memset(half[:, :, 0:PAD], 0.0))
                ch(V.memset(half[:, :, PAD + H:PW], 0.0))
            ch(V.memset(wbd.rearrange("p a b c -> p (a b c)"), 0.0))
            ch(V.memset(st2[:, :], -3.0e38))
            V.memset(ones[:, :], 1.0).then_inc(s_zero, 1)
            ch.settle()
            dve.sem_inc(s_zero, 1)
            for s in range(2):
                dve.sem_inc(wn_used[s], 1)
            dve.sem_inc(s_x1, 2)
            dve.sem_inc(xq_v, 1)
            dve.sem_inc(xq_ed, 3)
            dve.sem_inc(g_rd, 2)
            dve.sem_inc(u_rd, 2)
            dve.sem_inc(s_nv, 1)
            dve.sem_inc(s_sq, 1)
            dve.sem_inc(s_v2, 4)
            dve.sem_inc(s_dv, 1)
            dve.sem_inc(s_dev, 4)

            dve.wait_ge(s_load, 16 * N_SMALL)
            V.tensor_copy(id16[:, :], ident).then_inc(s_ev, 1)
            dve.wait_ge(s_pe, PE_AT["condT"])
            V.tensor_copy(condT, bank[0][:, 0:P]).then_inc(s_ev, 1)
            dve.wait_ge(s_pe, PE_AT["awT"])
            V.tensor_copy(awT.rearrange("p a b -> p (a b)"), bank[1][:, 0:KT * AWN]).then_inc(s_ev, 1)
            dve.wait_ge(s_pe, PE_AT["bT"])
            V.tensor_scalar(bT[0:ER, 0], bank[2][0:ER, :], SCALE, None, ALU.mult).then_inc(s_ev, 1)
            dve.wait_ge(s_pe, PE_AT["mixT"])
            V.tensor_copy(mixT.rearrange("p a b -> p (a b)"), bank[3][:, 0:MIX_K * CHAN]).then_inc(s_ev, 1)
            dve.wait_ge(s_pe, PE_AT["cwT"])
            V.tensor_copy(cwT, bank[4][:, 0:CHAN]).then_inc(s_ev, 1)
            dve.wait_ge(s_pe, PE_AT["logits"])
            V.tensor_reduce(smx[:, 0:1], bank[7][:, 0:MIX_K], AX.X, ALU.max, negate=True).then_inc(s_ev, 1)
            dve.wait_ge(s_act, 3)
            ch.then(V.reciprocal(smx[:, 2:3], smx[:, 1:2]))
            V.tensor_scalar(att, expv, smx[:, 2:3], None, ALU.mult).then_inc(s_ev, 1)
            dve.wait_ge(s_pe, PE_AT["attT"])
            V.tensor_copy(attT[0:MIX_K, :], bank[0][0:MIX_K, 0:P]).then_inc(s_ev, 1)
            dve.wait_ge(s_pe, PE_AT["aggb"])
            V.tensor_copy(aggb[:, 0], bank[1][:, 0:TILES]).then_inc(s_ev, 1)
            dve.wait_ge(s_pe, PE_AT["ctx"])
            V.tensor_scalar(ctxcol[:, :], bank[2][:, 0:TILES], side, None, ALU.add).then_inc(s_ev, 1)
            dve.wait_ge(s_ev, EV_AT["att"])
            V.tensor_tensor(attexp, att.unsqueeze(1).broadcast_to([P, TILES, MIX_K]),
                            cst[:, C_TILE:C_TILE + TILES].unsqueeze(2).broadcast_to([P, TILES, MIX_K]), ALU.mult)\
                .then_inc(s_ev, 1)
            dve.wait_ge(s_pe, PE_AT["attrep"])
            V.tensor_copy(attrep.rearrange("p a b -> p (a b)"), bank[3][:, 0:TILES * MIX_K]).then_inc(s_ev, 1)
            dve.wait_ge(s_pe, PE_AT["sumaw"])
            V.tensor_copy(sumaw[:, 0], bank[4][:, 0:AWN]).then_inc(s_ev, 1)

            def power_of_two(dst, src):
                V_i = src.bitcast(I32)
                ch.then(V.tensor_scalar(dst.bitcast(I32), V_i, 0x7F800000, None, ALU.bitwise_and))

            dve.wait_ge(s_wdn, 16)
            ch.then(V.tensor_reduce(dR[:, :], wdnat, AX.X, ALU.max, apply_absolute_value=True))
            ch.then(V.tensor_scalar(dR[:, :], dR[:, :], 1.0 / WMAX, TINY, ALU.mult, ALU.max))
            power_of_two(dS[:, :], dR[:, :])
            ch.then(V.reciprocal(dR[:, :], dS[:, :]))
            ch.then(V.tensor_scalar(dR[:, :], dR[:, :], WUP, None, ALU.mult))

            PREP_G, PREP_D = 11, 7

            def prep(buffers, u, slot, norm, clear=False, factor=None):
                wn, wint, wsp, wsc = buffers
                w = wn[:, slot]
                wi = wint[:, slot]
                blocks = [NB, BLK]

                def b(v):
                    return v.unsqueeze(2).broadcast_to([P] + blocks)

                dve.wait_ge(wn_in[slot], (u + 1) * 16)
                ch.then(V.tensor_reduce(wsc[:, 0], w.rearrange("p (b k) -> p b k", k=BLK), AX.X, ALU.max,
                                        apply_absolute_value=True))
                ch.then(V.tensor_scalar(wsc[:, 1], wsc[:, 0], 1.0 / WMAX, TINY, ALU.mult, ALU.max))
                ch.then(V.reciprocal(wsc[:, 2], wsc[:, 1]))
                last = V.tensor_tensor(wi.rearrange("p (b k) -> p b k", k=BLK),
                                       w.rearrange("p (b k) -> p b k", k=BLK), b(wsc[:, 2]), ALU.mult)
                if clear:
                    ch.then(last)
                    pad = wn[LAST:P, 0] if slot == 0 else wn[:, 1].rearrange("p (t i) -> p t i", t=KT)[:, :, LAST:P]
                    last = V.memset(pad, 0.0)
                last.then_inc(wn_used[slot], 1)
                dve.wait_ge(wn_used[slot], u + 2)
                ch(V.tensor_scalar(wi, wi, MAGIC, MAGIC, ALU.add, ALU.subtract))
                if norm is not None:
                    ch.then(V.tensor_reduce(wsc[:, 4, 0:1], wsc[:, 1], AX.X, ALU.max))
                    power_of_two(wsc[:, 4, 1:2], wsc[:, 4, 0:1])
                    if factor is None:
                        ch(V.tensor_scalar(norm, wsc[:, 4, 1:2], 1.0, None, ALU.mult))
                    else:
                        ch(V.tensor_scalar(norm, wsc[:, 4, 1:2], factor, 1.0 / (WUP * VDN), ALU.mult, ALU.mult))
                    ch.then(V.reciprocal(rS[:, slot], wsc[:, 4, 1:2]))
                    ch.then(V.tensor_scalar(wsc[:, 3], wsc[:, 1], rS[:, slot], WUP, ALU.mult, ALU.mult))
                else:
                    ch.then(V.tensor_tensor(wsc[:, 3].rearrange("p (t b) -> p t b", t=KT),
                                            wsc[:, 1].rearrange("p (t b) -> p t b", t=KT),
                                            dR[:, :].unsqueeze(2).broadcast_to([P, KT, NB // KT]), ALU.mult))
                ch.then(V.tensor_tensor(wi.rearrange("p (b k) -> p b k", k=BLK),
                                        wi.rearrange("p (b k) -> p b k", k=BLK), b(wsc[:, 3]), ALU.mult))
                dve.wait_ge(hl_turned[slot], u + 1)
                ch.then(V.tensor_copy(wsp[:, slot, 0:H], wi))
                V.tensor_tensor(wsp[:, slot, H:2 * H], wi, wsp[:, slot, 0:H], ALU.subtract)\
                    .then_inc(hl_ready[slot], 1)

            dve.wait_ge(s_wk, 16 * 16)
            for half in range(2):
                for j in range(BPT):
                    r = slice(CHAN * j, CHAN * (j + 1))
                    src = wk[r].rearrange("p o k -> p k o")
                    if half == 0:
                        ch(V.tensor_scalar(wbd[r, 0, :, r], src, KUP, None, ALU.mult))
                    else:
                        V.scalar_tensor_tensor(wbd[r, 1, :, r], src, KUP, wbd[r, 0, :, r], ALU.mult, ALU.subtract)\
                            .then_inc(s_wbd, 1)
                ch.settle()

            def z_out(g):
                for h in range(2):
                    rows = aggb[:, 0, h * SUP + g * GT:h * SUP + g * GT + SUP] if isinstance(g, int) else \
                        aggb[:, 0, ds(g * GT + h * SUP, SUP)]
                    ch.then(V.tensor_tensor(zbias, sumaw[:, 0].unsqueeze(1).broadcast_to([P, SUP, AWN]),
                                            rows.unsqueeze(2).broadcast_to([P, SUP, AWN]), ALU.mult))
                    dve.wait_ge(s_z1, g * GT + (h + 1) * SUP)
                    V.tensor_tensor(zbuf[:, h * SUP:(h + 1) * SUP],
                                    bank[2 + h][:, 0:SUP * AWN].rearrange("p (t n) -> p t n", t=SUP),
                                    zbias, ALU.add).then_inc(s_ze, 1)
                    dve.wait_ge(s_ze, g * 2 + h + 1)

            Z_STEPS, G_STEPS = 2, 12

            def gates(g):
                v = zbuf[:, :, ER:AWN]
                four = [P, GT, EXP_N, EXP_N]
                vj, ve = v.unsqueeze(2).broadcast_to(four), v.unsqueeze(3).broadcast_to(four)
                t4 = [gate_t[:, k, :].rearrange("p (t e j) -> p t e j", t=GT, e=EXP_N) for k in range(2)]
                flat = [gate_t[:, k, :].rearrange("p (t q) -> p t q", t=GT) for k in range(2)]
                masks = [cst[:, c:c + 16].unsqueeze(1).broadcast_to([P, GT, 16]) for c in (C_BEF, C_AFT)]
                small = [gate_t[:, k, 0:GT * EXP_N].rearrange("p (t e) -> p t e", t=GT) for k in range(2, 6)]
                rank, sel, d, ex = small
                m1, total = gate_t[:, 6, 0:GT], gate_t[:, 6, GT:2 * GT]
                inv = gate_t[:, 6, 2 * GT:3 * GT]
                by_e = lambda x: x.unsqueeze(2).broadcast_to([P, GT, EXP_N])
                ch(V.tensor_tensor(t4[0], vj, ve, ALU.is_ge))
                ch(V.tensor_tensor(t4[1], vj, ve, ALU.is_gt))
                ch.then(V.tensor_reduce(m1, v, AX.X, ALU.max))
                ch(V.tensor_tensor(flat[0], flat[0], masks[0], ALU.mult))
                ch(V.tensor_tensor(flat[1], flat[1], masks[1], ALU.mult))
                V.tensor_tensor(d, v, by_e(m1), ALU.subtract).then_inc(s_d4, 1)
                ch.settle()
                ch.then(V.tensor_tensor(flat[0], flat[0], flat[1], ALU.add))
                ch.then(V.tensor_reduce(rank, t4[0], AX.X, ALU.add))
                ch.then(V.tensor_scalar(sel, rank, TOPK - 0.5, None, ALU.is_lt))
                dve.wait_ge(s_exp, g + 1)
                ch.then(V.tensor_tensor(ex, ex, sel, ALU.mult))
                ch.then(V.tensor_reduce(total, ex, AX.X, ALU.add))
                ch.then(V.reciprocal(inv, total))
                ch.then(V.tensor_tensor(ex, ex, by_e(inv), ALU.mult))
                V.tensor_tensor(gmid.rearrange("p t (e r) -> p t e r", e=EXP_N),
                                zbuf[:, :, 0:ER].rearrange("p t (e r) -> p t e r", e=EXP_N),
                                ex.unsqueeze(3).broadcast_to([P, GT, EXP_N, RANK]), ALU.mult).then_inc(s_gm, 1)

            def add_delta(g):
                dve.wait_ge(s_xres, g * 16 + 16)
                for t in range(GT):
                    dve.wait_ge(s_dl, g * GT + t + 1)
                    V.tensor_tensor(xres[:, t], bank[6 + t % 2][:, :], xres[:, t], ALU.add).then_inc(s_x1, 1)
                for s in range(2):
                    settle_wait(dve, (s_hi0, g * 2 + s + 1))
                    ts = slice(s * SUP, (s + 1) * SUP)
                    V.tensor_tensor(xl0[:, ts, PAD:PAD + H], xres[:, ts], xh0[:, ts, PAD:PAD + H], ALU.subtract)\
                        .then_inc(s_lo0, 1)

            def y_range(g, s):
                dve.wait_ge(s_cve, g * GT + s * SUP + SUP + 2)
                at_ = g * GT + s * SUP
                v = y1[:, at_:at_ + SUP] if isinstance(g, int) else y1[:, ds(at_, SUP)]
                col = slice(g * 2 + s, g * 2 + s + 1) if isinstance(g, int) else ds(g * 2 + s, 1)
                v = v.rearrange("p a b -> p (a b)")
                ch(V.tensor_reduce(st_hi[:, col], v, AX.X, ALU.max))
                ch(V.tensor_reduce(st_lo[:, col], v, AX.X, ALU.min))

            dve.wait_ge(s_ev, EV_AT["sumaw"])
            z_out(0)
            gates(0)
            start = ch.start()
            PER = Z_STEPS + G_STEPS + 4 + 2 * PREP_G
            with dve.Fori(0, GROUPS - 1) as g:
                ch.iteration(start, g, PER)
                add_delta(g)
                z_out(g + 1)
                gates(g + 1)
                for s in range(2):
                    prep(prep_a, g, s, gS[:, ds(g * 2 + s, 1)])
                for s in range(2):
                    y_range(g, s)
            ch.end(start, GROUPS - 1, PER)
            add_delta(GROUPS - 1)
            for m in range(2 * (GROUPS - 1), MT):
                prep(prep_a, m // 2, m % 2, gS[:, m:m + 1], clear=(m == MT - 3))
            for s in range(2):
                y_range(GROUPS - 1, s)

            def known_range(which, n, k=None):
                ch.settle()
                if n:
                    ch(V.tensor_reduce(st[:, which, 0:1], st_hi[:, 0:n], AX.X, ALU.max))
                    ch(V.tensor_reduce(st[:, which, 1:2], st_lo[:, 0:n], AX.X, ALU.min, negate=True))
                ch.settle()
                dve.sem_inc(s_st, 1)
                dve.wait_ge(s_red, which + 1)
                r = rg[:, which, 5:7]
                d, q, e, f, n_ = (rg[:, which, 7 + j:8 + j] for j in range(5))
                ch.then(V.tensor_scalar(r, red[:, which, :], 0.0, 1.0 if k is None else k, ALU.max, ALU.mult))
                ch.then(V.tensor_tensor(d, r[:, 0:1], r[:, 1:2], ALU.add))
                ch.then(V.tensor_scalar(q, d, 1.0 / QMAX, None, ALU.mult))
                ch.then(V.scalar_tensor_tensor(e, q, -65536.0, d, ALU.mult, ALU.add))
                ch.then(V.tensor_tensor(f, e, q, ALU.add))
                ch.then(V.scalar_tensor_tensor(n_, f, 1.0 / QMAX, q, ALU.mult, ALU.add))
                ch.then(V.tensor_scalar(par(which, SC), n_, TINY, None, ALU.max))
                ch.then(V.reciprocal(par(which, INV), par(which, SC)))
                ch.then(V.tensor_scalar(par(which, ZP), r[:, 1:2], par(which, INV), MAGIC, ALU.mult, ALU.add))
                ch.then(V.tensor_scalar(par(which, ZP), par(which, ZP), MAGIC, None, ALU.subtract))
                if k is not None:
                    ch.then(V.tensor_scalar(par(which, INV), par(which, INV), k, None, ALU.mult))
                ch.then(V.tensor_scalar(par(which, NSC), par(which, SC), -1.0, None, ALU.mult))
                ch.then(V.tensor_scalar(par(which, NINV), par(which, INV), -1.0, None, ALU.mult))

            known_range(X, 2 * GROUPS)
            dve.sem_inc(s_par, 1)
            ch.then(V.tensor_scalar(gS[:, :], gS[:, :], par(X, SC), 1.0 / (WUP * VDN), ALU.mult, ALU.mult))

            def x_integer(c, s):
                dve.wait_ge(xq_q, c + 1)
                dve.wait_ge(xq_hi, c + 1)
                if not (isinstance(c, int) and c < 2):
                    dve.wait_ge(xq_lo, c - 1)
                V.tensor_scalar(xv[:, s], xq, par(X, ZP), VDN, ALU.subtract, ALU.mult).then_inc(xq_v, 1)

            def x_low(c, s):
                dve.wait_ge(xq_hi, c + 3)
                dve.wait_ge(xq_t, c * SUP + SUP)
                V.tensor_tensor(xhl[:, s, 1], xv[:, s], xhl[:, s, 0], ALU.subtract).then_inc(xq_lo, 1)

            def x_copy(c):
                for t in range(3):
                    dve.wait_ge(xq_t, c * SUP + t + 1 + 2 * SUP)
                    tile = c * SUP + t
                    dst = xT[:, :, tile * P:(tile + 1) * P] if isinstance(c, int) else xT[:, :, ds(tile * P, P)]
                    src = bank[4 + t][:, :].bitcast(F16).rearrange("p (a b) -> p a b", a=8)
                    V.tensor_copy(dst, src).then_inc(xq_ed, 1)

            dve.wait_ge(s_x1o, 16 * GROUPS)
            dve.wait_ge(s_par, 1)
            x_integer(0, 0)
            x_low(0, 0)
            x_integer(1, 1)
            with dve.Fori(0, (CHUNKS - 2) // 2) as i:
                for s in range(2):
                    c = i * 2 + s + 1
                    x_low(c, 1 - s)
                    x_integer(c + 1, s)
                    x_copy(c - 1)
            x_low(CHUNKS - 1, 1)
            x_copy(CHUNKS - 2)
            x_copy(CHUNKS - 1)

            def raw_range(m, buf, slot, ev, rd):
                dve.wait_ge(ev, m * CHUNKS + CHUNKS + 4)
                col = slice(m, m + 1) if isinstance(m, int) else ds(m, 1)
                ch(V.tensor_reduce(st_hi[:, col], buf[:, slot], AX.X, ALU.max))
                V.tensor_reduce(st_lo[:, col], buf[:, slot], AX.X, ALU.min).then_inc(rd, 1)

            def units(m, clear=False):
                prep(prep_b, m + U0, 0, uS[:, m:m + 1] if isinstance(m, int) else uS[:, ds(m, 1)], clear,
                     factor=par(X, SC))
                prep(prep_b, m + U1, 1, None, clear)

            raw_range(0, gbuf, 0, g_ev, g_rd)
            start = ch.start()
            PER = 2 * (PREP_G + PREP_D + 1)
            with dve.Fori(0, (MT - 3) // 2) as i:
                ch.iteration(start, i, PER)
                for s in range(2):
                    units(i * 2 + s)
                    raw_range(i * 2 + s + 1, gbuf, 1 - s, g_ev, g_rd)
            ch.end(start, (MT - 3) // 2, PER)
            units(MT - 3)
            raw_range(MT - 2, gbuf, 1, g_ev, g_rd)
            units(MT - 2, clear=True)
            units(MT - 1)
            raw_range(MT - 1, gbuf, 0, g_ev, g_rd)
            dve.wait_ge(g_rd, 2 + MT)
            known_range(G, MT)
            dve.sem_inc(s_par, 1)

            dve.wait_ge(s_vma, 1)
            V.tensor_scalar(vm[:, 0:1], vmq[:, 0:1], -1.0, par(G, ZP), ALU.mult, ALU.add).then_inc(s_vm, 1)
            dve.wait_ge(s_vma, 2)
            ch.then(V.tensor_scalar(vmq[:, 1:2], vm[:, 1:2], SIG_ONE, None, ALU.mult))
            ch.then(V.tensor_tensor(vm[:, 2:3], vm[:, 0:1], vmq[:, 1:2], ALU.mult))
            ch.then(V.tensor_scalar(st[:, S, 0:1], vm[:, 2:3], -1.0, None, ALU.mult))

            def gated(m, half):
                n = m * 2 + half
                dve.wait_ge(s_gq, n + 1)
                dve.wait_ge(s_pst[half], m * 16 + 16)
                V.tensor_scalar(nv[:, half], gq, -1.0, par(G, ZP), ALU.mult, ALU.add).then_inc(s_nv, 1)
                dve.wait_ge(s_sig, n + 1)
                V.tensor_scalar(sq, sig, SIG_ONE, None, ALU.mult).then_inc(s_sq, 1)
                settle_wait(dve, (s_sq, n + 2))
                V.tensor_tensor_reduce(nv[:, half], nv[:, half], sq, 1.0, st2[:, 0:1], ALU.mult, ALU.max,
                                       st2[:, 0:1]).then_inc(s_pr, 1)

            gated(0, 0)
            raw_range(0, ubuf, 1, u_ev, u_rd)
            start = ch.start()
            with dve.Fori(0, (MT - 1) // 2) as i:
                ch.iteration(start, i, 2)
                for s in range(2):
                    m = i * 2 + s + 1
                    gated(m - 1, 1)
                    gated(m, 0)
                    raw_range(m, ubuf, s, u_ev, u_rd)
            ch.end(start, (MT - 1) // 2, 2)
            gated(MT - 1, 1)
            dve.wait_ge(s_pr, 2 * MT)
            ch(V.tensor_scalar(st[:, S, 1:2], st2[:, 0:1], 1.0, None, ALU.mult))
            ch.then(V.tensor_scalar(vm[:, 3:4], par(G, SC), 1.0 / SIG_ONE, None, ALU.mult))
            known_range(S, 0, k=vm[:, 3:4])
            dve.wait_ge(u_rd, 2 + MT)
            known_range(U, MT)
            dve.sem_inc(s_par, 2)

            def product(m, half):
                n = m * 2 + half
                dve.wait_ge(s_q2, n * 2 + 1)
                V.tensor_scalar(vg, qg[:, half], par(S, ZP), None, ALU.subtract).then_inc(s_v2, 1)
                dve.wait_ge(s_q2, n * 2 + 2)
                V.tensor_scalar(vu, qu[:, half], par(U, ZP), None, ALU.subtract).then_inc(s_v2, 1)
                settle_wait(dve, (s_v2, n * 2 + 2 + 4), (s_pos[half], m * 16 + 16))
                col = slice(n, n + 1) if isinstance(n, int) else ds(n, 1)
                V.tensor_tensor_reduce(prod[:, half], vg, vu, 1.0, st2[:, 1:2], ALU.mult, ALU.max,
                                       st2[:, 1:2]).then_inc(s_po, 1)
                dve.wait_ge(s_po, n + 1)
                ch(V.tensor_reduce(st_lo[:, col], prod[:, half], AX.X, ALU.min))

            start = ch.start()
            with dve.Fori(0, MT) as m:
                ch.iteration(start, m, 2)
                for half in range(2):
                    product(m, half)
            ch.end(start, MT, 2)
            ch.then(V.tensor_tensor(vm[:, 3:4], par(S, SC), par(U, SC), ALU.mult))
            ch(V.tensor_reduce(st[:, O, 1:2], st_lo[:, 0:2 * MT], AX.X, ALU.min, negate=True))
            ch(V.tensor_scalar(st[:, O, 0:1], st2[:, 1:2], 1.0, None, ALU.mult))
            known_range(O, 0, k=vm[:, 3:4])
            dve.sem_inc(s_par, 1)

            def d_integer(c, s):
                dve.wait_ge(s_dq, c + 1)
                dve.wait_ge(s_dhi, c + 1)
                V.tensor_scalar(vd, qd, par(O, ZP), VDN, ALU.subtract, ALU.mult).then_inc(s_dv, 1)
                dve.wait_ge(s_dhi, c + 2)
                dve.wait_ge(s_dmm, c * SUP + SUP)
                V.tensor_tensor(hd[:, s, CH:2 * CH], vd, hd[:, s, 0:CH], ALU.subtract).then_inc(s_dlo, 1)

            def d_out(c, s):
                for t in range(SUP):
                    dve.wait_ge(s_dmm, c * SUP + t + 1 + 2 * SUP)
                    V.tensor_tensor(otmp[:, t % 2], bank[t][:, :], rowv[:, :], ALU.mult).then_inc(s_dev, 1)
                    dve.wait_ge(s_dev, c * SUP + t + 1 + SUP)
                    V.tensor_tensor(ob[:, s, t * H:(t + 1) * H], otmp[:, t % 2], x1b[:, s, t * H:(t + 1) * H],
                                    ALU.add).then_inc(s_ob, 1)

            def d_room(pair, s):
                dve.wait_ge(s_x1i[s], pair * 16 + 16)
                dve.wait_ge(s_out[s], pair * 16 + 16)

            dve.wait_ge(s_par, 5)
            d_integer(0, 0)
            for t in range(KT):
                ch.then(V.tensor_scalar(dgS[:, :], ident, dS[:, t:t + 1], None, ALU.mult))
                dve.sem_inc(s_dg, 1)
                dve.wait_ge(s_row, t + 1)
            ch.then(V.tensor_scalar(rowv[:, :], bank[7][:, :], par(O, SC), 1.0 / (WUP * VDN), ALU.mult, ALU.mult))
            with dve.Fori(0, (CHUNKS - 2) // 2) as i:
                for s in range(2):
                    c = i * 2 + s
                    d_integer(c + 1, 1 - s)
                    d_room(i, s)
                    d_out(c, s)
            d_integer(CHUNKS - 1, 1)
            for s in range(2):
                d_room((CHUNKS - 2) // 2, s)
                d_out(CHUNKS - 2 + s, s)

        @block.scalar
        def _(act):
            A = nc.scalar
            act.wait_ge(s_zero, 2)
            for j in range(BPT):
                for g in range(4):
                    r = 8 * g
                    act.dma_start(wk[CHAN * j + r:CHAN * j + r + 8, r:r + 8, :],
                                  a["L1_cond_weight"][r:r + 8].rearrange("o i k -> i o k")).then_inc(s_wk, 16)
            act.sem_inc(xq_hi, 2)
            act.sem_inc(xq_ea, 1)
            act.sem_inc(s_y0e, 2)
            act.sem_inc(s_cve, 2)
            act.sem_inc(g_ev, 4)
            act.sem_inc(u_ev, 4)
            act.sem_inc(s_dhi, 1)
            for s in range(2):
                act.sem_inc(wt_copied[s], 1)
            act.wait_ge(s_pe, PE_AT["h1"])
            A.activation(h1T, bank[5][:, 0:P], ACT.Gelu, bias=b01[:, 0:1]).then_inc(s_act, 1)
            act.wait_ge(s_pe, PE_AT["h2"])
            A.activation(h2T, bank[6][:, 0:P], ACT.Gelu, bias=b01[:, 1:2]).then_inc(s_act, 1)
            act.wait_ge(s_ev, EV_AT["negmax"])
            A.activation(expv, bank[7][:, 0:MIX_K], ACT.Exp, bias=smx[:, 0:1], accum_out=smx[:, 1:2])\
                .then_inc(s_act, 1)

            def copy_weights(u, slot, dst):
                settle_wait(act, (hl_turned[slot], u + 2))
                A.activation(dst, bank[4 + slot][:, :].bitcast(F16).rearrange("p (a b) -> p a b", a=8), ACT.Copy)\
                    .then_inc(wt_copied[slot], 1)

            def y0_out(g):
                for t in range(GT):
                    act.wait_ge(s_y0, g * GT + t + 1)
                    if t >= 2:
                        act.wait_ge(s_z1, g * GT + t - 1)
                    A.activation(y0T[:, t % 2], bank[t % 2][:, :], ACT.Copy).then_inc(s_y0e, 1)

            def gates_exp(g):
                act.wait_ge(s_d4, g + 1)
                A.activation(gate_t[:, 5, 0:GT * EXP_N], gate_t[:, 4, 0:GT * EXP_N], ACT.Exp).then_inc(s_exp, 1)

            def gmid_out(g):
                for h in range(2):
                    act.wait_ge(s_gt, g * 2 + h + 1)
                    A.activation(gmidT[0:ER, h * SUP:(h + 1) * SUP].rearrange("p a b -> p (a b)"),
                                 bank[4 + h][0:ER, :], ACT.Copy).then_inc(s_gte, 1)

            def x1_high(g):
                for s in range(2):
                    act.wait_ge(s_x1, g * GT + s * SUP + SUP + 2)
                    ts = slice(s * SUP, (s + 1) * SUP)
                    A.activation(xh0[:, ts, PAD:PAD + H], xres[:, ts], ACT.Copy).then_inc(s_hi0, 1)

            def conv_out(g, t):
                settle_wait(act, (s_cv, g * GT + t + 1))
                tile = g * GT + t
                bias = ctxcol[:, tile:tile + 1] if isinstance(g, int) else ctxcol[:, ds(tile, 1)]
                A.activation(pick1(y1, tile), bank[t % 2][:, :], ACT.Identity, bias=bias, scale=1.0 / KUP)\
                    .then_inc(s_cve, 1)

            act.wait_ge(s_ev, EV_AT["ctx"])
            y0_out(0)
            gates_exp(0)
            with act.Fori(0, GROUPS - 1) as g:
                gmid_out(g)
                x1_high(g)
                y0_out(g + 1)
                gates_exp(g + 1)
                for t in range(GT):
                    conv_out(g, t)
                for s in range(2):
                    copy_weights(g, s, wgT[:, :, ds(g * 2 * P + s * P, P)])
            gmid_out(GROUPS - 1)
            x1_high(GROUPS - 1)
            for t in range(GT):
                conv_out(GROUPS - 1, t)
                m = TURN_AFTER.get(t)
                if m is not None:
                    copy_weights(m // 2, m % 2, wgT[:, :, m * P:(m + 1) * P])

            def x_quant(c):
                settle_wait(act, (xq_v, c + 1))
                v = y1[:, c * SUP:(c + 1) * SUP] if isinstance(c, int) else y1[:, ds(c * SUP, SUP)]
                A.activation(xq, v.rearrange("p a b -> p (a b)"), ACT.Identity, bias=par(X, ZP), scale=par(X, INV))\
                    .then_inc(xq_q, 1)

            def x_high(c, s):
                act.wait_ge(xq_v, c + 2)
                act.wait_ge(xq_t, c * SUP + SUP)
                A.activation(xhl[:, s, 0], xv[:, s], ACT.Copy).then_inc(xq_hi, 1)

            def x_copy(c):
                settle_wait(act, (xq_t, c * SUP + SUP + 2 * SUP))
                tile = c * SUP + SUP - 1
                dst = xT[:, :, tile * P:(tile + 1) * P] if isinstance(c, int) else xT[:, :, ds(tile * P, P)]
                A.activation(dst, bank[7][:, :].bitcast(F16).rearrange("p (a b) -> p a b", a=8), ACT.Copy)\
                    .then_inc(xq_ea, 1)

            def first_gate_out(c, s):
                settle_wait(act, (g_mm, c + 1))
                dst = gbuf[:, 0, c * NC:(c + 1) * NC] if isinstance(c, int) else gbuf[:, 0, ds(c * NC, NC)]
                A.activation(dst, bank[s][:, :], ACT.Copy, scale=gS[:, 0:1]).then_inc(g_ev, 1)

            act.wait_ge(s_par, 1)
            x_quant(0)
            x_high(0, 0)
            x_quant(1)
            x_high(1, 1)
            x_quant(2)
            x_copy(0)
            with act.Fori(0, (CHUNKS - 4) // 2) as i:
                for s in range(2):
                    c = i * 2 + s + 2
                    x_high(c, s)
                    x_quant(c + 1)
                    x_copy(c - 1)
                    first_gate_out(c - 2, s)
            x_high(CHUNKS - 2, 0)
            x_quant(CHUNKS - 1)
            x_copy(CHUNKS - 3)
            first_gate_out(CHUNKS - 4, 0)
            x_high(CHUNKS - 1, 1)
            x_copy(CHUNKS - 2)
            first_gate_out(CHUNKS - 3, 1)
            x_copy(CHUNKS - 1)
            first_gate_out(CHUNKS - 2, 0)
            first_gate_out(CHUNKS - 1, 1)

            def raw_out(pair, m, slot, c, buf, place, mm, ev, rd, stored, scale):
                if c == 0:
                    act.wait_ge(stored[slot], pair * 16 + 16)
                    act.wait_ge(rd, m + 1)
                settle_wait(act, (mm, m * CHUNKS + c + 1))
                col = scale[:, m:m + 1] if isinstance(m, int) else scale[:, ds(m, 1)]
                A.activation(buf[:, place, c * NC:(c + 1) * NC], bank[c % 4][:, :], ACT.Copy, scale=col)\
                    .then_inc(ev, 1)

            def copy_unit(m, slot):
                if slot == 0:
                    copy_weights(m + U0, 0, wuT[:, :, m * P:(m + 1) * P] if isinstance(m, int) else
                                 wuT[:, :, ds(m * P, P)])
                else:
                    copy_weights(m + U1, 1, wdT8[:, m] if isinstance(m, int) else
                                 wdT8[:, ds(m, 1)].rearrange("p a b c -> p (a b) c"))

            def gate_step(pair, slot):
                m = pair * 2 + slot
                for c in range(CHUNKS):
                    raw_out(pair, m, slot, c, gbuf, slot, g_mm, g_ev, g_rd, g_st, gS)
                    if c in UNIT_AFTER:
                        copy_unit(m - 1, UNIT_AFTER[c])

            with act.Fori(0, (MT - 1) // 2) as i:
                gate_step(i, 1)
                gate_step(i + 1, 0)

            def gate_quant(m, half):
                n = m * 2 + half
                act.wait_ge(s_gin[half], m * 16 + 16)
                act.wait_ge(s_nv, n + 1)
                A.activation(gq, graw[:, half], ACT.Identity, bias=par(G, ZP), scale=par(G, INV)).then_inc(s_gq, 1)

            def gate_sigmoid(m, half):
                n = m * 2 + half
                act.wait_ge(s_nv, n + 2)
                act.wait_ge(s_sq, n + 1)
                A.activation(sig, nv[:, half], ACT.Sigmoid, scale=par(G, NSC)).then_inc(s_sig, 1)

            def up_step(pair, slot):
                m = pair * 2 + slot
                for c in range(CHUNKS):
                    raw_out(pair, m, slot, c, ubuf, 1 - slot, u_mm, u_ev, u_rd, u_st, uS)
                    if isinstance(m, int):
                        if c in LAST_UNIT_AFTER:
                            copy_unit(MT - 1, LAST_UNIT_AFTER[c])
                        if c == 5:
                            act.wait_ge(s_par, 2)
                            A.activation(vmq[:, 0:1], par(G, 5), ACT.Identity, bias=par(G, ZP), scale=par(G, INV))\
                                .then_inc(s_vma, 1)
                            act.wait_ge(s_vm, 1)
                            A.activation(vm[:, 1:2], vm[:, 0:1], ACT.Sigmoid, scale=par(G, NSC)).then_inc(s_vma, 1)
                            for s in range(2):
                                act.wait_ge(g_st[s], 16 + 16 * N_SLOT[s])
                    elif c == 1:
                        gate_quant(m - 1, 1)
                    elif c == 3:
                        gate_sigmoid(m - 1, 1)
                    if c == 5:
                        gate_quant(m, 0)
                    if c == 7:
                        gate_sigmoid(m, 0)

            act.wait_ge(g_rd, 2 + MT - 1)
            up_step(0, 0)
            with act.Fori(0, (MT - 1) // 2) as i:
                up_step(i, 1)
                up_step(i + 1, 0)
            gate_quant(MT - 1, 1)
            gate_sigmoid(MT - 1, 1)

            act.wait_ge(s_par, 4)
            with act.Fori(0, MT) as m:
                for half in range(2):
                    act.wait_ge(s_pin[half], m * 32 + 32)
                    act.wait_ge(s_v2, m * 4 + half * 2 + 2)
                    A.activation(qg[:, half], pin[:, half], ACT.Identity, bias=par(S, ZP), scale=par(S, NINV))\
                        .then_inc(s_q2, 1)
                    A.activation(qu[:, half], uin[:, half], ACT.Identity, bias=par(U, ZP), scale=par(U, INV))\
                        .then_inc(s_q2, 1)

            act.wait_ge(s_par, 5)
            with act.Fori(0, CHUNKS // 2) as i:
                for s in range(2):
                    c = i * 2 + s
                    act.wait_ge(s_din[s], i * 16 + 16)
                    act.wait_ge(s_dv, c + 1)
                    A.activation(qd, pd[:, s], ACT.Identity, bias=par(O, ZP), scale=par(O, INV)).then_inc(s_dq, 1)
                    act.wait_ge(s_dv, c + 2)
                    act.wait_ge(s_dmm, c * SUP + SUP)
                    A.activation(hd[:, s, 0:CH], vd, ACT.Copy).then_inc(s_dhi, 1)

        @block.gpsimd
        def _(pool):
            G_ = nc.gpsimd
            pc = Chain(pool, pch)

            def load(dst, src, signal):
                pool.dma_start(dst, src).then_inc(signal, 16)

            load(cw[0:CHAN, :], a["L1_cond_c_weight"], s_mixn)
            mix_v = a["L0_cond_weight"].rearrange("k o i a -> (k o) (i a)").rearrange("(t p) i -> p t i", p=P)
            for j in range(BPT):
                load(mixnat[:, :, CHAN * j:CHAN * (j + 1)], mix_v, s_mixn)
                load(side[CHAN * j:CHAN * (j + 1), :], a["fside_S_0"].rearrange("(p a) -> p a", a=1), s_mixn)

            MIX_STEPS = 14

            def mix(g):

                def part(k, dst, lo=0, n=P):
                    rep = attrep[lo:lo + n, g * GT:(g + 1) * GT, k] if isinstance(g, int) else \
                        attrep[lo:lo + n, ds(g * GT, GT), k]
                    s_ = [n, GT, CHAN]
                    return G_.tensor_tensor(dst, mixT[lo:lo + n, k].unsqueeze(1).broadcast_to(s_),
                                            rep.unsqueeze(2).broadcast_to(s_), ALU.mult)

                acc = mixacc[:, 0].rearrange("p (t o) -> p t o", t=GT)
                tmp = [mixtmp[:, j].rearrange("p (t o) -> p t o", t=GT) for j in range(2)]
                pc(part(0, acc))
                for k in range(1, MIX_K):
                    pc.then(part(k, tmp[k % 2]))
                    if k < MIX_K - 1:
                        pc(G_.tensor_tensor(acc, acc, tmp[k % 2], ALU.add))
                pc.settle()
                if not isinstance(g, int):
                    pool.wait_ge(s_y0, g * GT)
                for b in range(BPT):
                    r = slice(CHAN * b, CHAN * (b + 1))
                    G_.tensor_tensor(mixbd[r, :, r], acc[r], tmp[(MIX_K - 1) % 2][r], ALU.add).then_inc(s_bd, 1)
                pool.wait_ge(s_bd, g * BPT + BPT)

            pool.wait_ge(s_ev, EV_AT["attrep"])
            mix(0)
            start = pc.start()
            with pool.Fori(0, GROUPS - 1) as i:
                pc.iteration(start, i, MIX_STEPS)
                mix(i + 1)
            pc.end(start, GROUPS - 1, MIX_STEPS)
            for which in (X, G, S, U, O):
                pool.wait_ge(s_st, which + 1)
                G_.partition_all_reduce(red[:, which, :], st[:, which, :], P, RMAX).then_inc(s_red, 1)

        @block.tensor
        def _(pe):
            T = nc.tensor
            for s in range(2):
                pe.sem_inc(hl_turned[s], 1)
            pe.sem_inc(xq_t, 2 * SUP)
            pe.sem_inc(s_dmm, 2 * SUP)

            def b16(i):
                return bank[i][:, :].bitcast(F16)

            pe.wait_ge(s_load, 16 * N_SMALL)
            pe.wait_ge(s_mixn, 16 * 9)
            pe.wait_ge(s_zero, 2)
            T.transpose(bank[0][:, 0:P], cond, ident).then_inc(s_pe, 1)
            for t in range(KT):
                last = T.transpose(bank[1][:, t * AWN:(t + 1) * AWN], aw[0:AWN, t * P:(t + 1) * P],
                                   cst[0:AWN, C_ID:C_ID + AWN])
            last.then_inc(s_pe, 1)
            for t in range(4):
                last = T.transpose(bank[2][0:ER, t * P:(t + 1) * P], bnat[:, t], ident)
            last.then_inc(s_pe, 1)
            for t in range(2):
                last = T.transpose(bank[3][:, t * P:(t + 1) * P], mixnat[:, t], ident)
            last.then_inc(s_pe, 1)
            T.transpose(bank[4][:, 0:CHAN], cw[0:CHAN, :], cst[0:CHAN, C_ID:C_ID + CHAN]).then_inc(s_pe, 1)
            pe.wait_ge(s_ev, EV_AT["condT"])
            T.matmul(bank[5][:, 0:P], w0, condT, start=True, stop=True).then_inc(s_pe, 1)
            pe.wait_ge(s_act, 1)
            T.matmul(bank[6][:, 0:P], w1, h1T, start=True, stop=True).then_inc(s_pe, 1)
            pe.wait_ge(s_act, 2)
            T.matmul(bank[7][:, 0:MIX_K], h2T, w2, start=True, stop=False)
            T.matmul(bank[7][:, 0:MIX_K], ones[0:1, :], b2[0:1, :], start=False, stop=True).then_inc(s_pe, 1)
            pe.wait_ge(s_ev, EV_AT["att"])
            T.transpose(bank[0][0:MIX_K, 0:P], att, ident).then_inc(s_pe, 1)
            pe.wait_ge(s_ev, EV_AT["attT"])
            attT_v = attT[0:MIX_K, :].rearrange("k (q b) -> k b q", b=BPT)
            for b in range(BPT):
                last = T.matmul(bank[1][CHAN * b:CHAN * (b + 1), 0:TILES], biask[0:MIX_K, :], attT_v[:, b],
                                start=True, stop=True)
            last.then_inc(s_pe, 1)
            condT_v = condT.rearrange("d (t b) -> d b t", b=BPT)
            for b in range(BPT):
                last = T.matmul(bank[2][CHAN * b:CHAN * (b + 1), 0:TILES], cwT, condT_v[:, b], start=True, stop=True)
            last.then_inc(s_pe, 1)
            pe.wait_ge(s_ev, EV_AT["attexp"])
            T.matmul(bank[3][:, 0:TILES * MIX_K], cst[:, C_PICK:C_PICK + P], attexp.rearrange("p a b -> p (a b)"),
                     start=True, stop=True).then_inc(s_pe, 1)
            for t in range(KT):
                last = T.matmul(bank[4][:, 0:AWN], ones[:, :], awT[:, t], start=(t == 0), stop=(t == KT - 1))
            last.then_inc(s_pe, 1)

            def turn(wsp, u, slot):
                pe.wait_ge(hl_ready[slot], u + 1)
                pe.wait_ge(wt_copied[slot], u + 1)
                for b in range(8):
                    last = T.transpose(b16(4 + slot)[:, b * P:(b + 1) * P], wsp[:, slot, b * P:(b + 1) * P], id16[:, :])
                last.then_inc(hl_turned[slot], 1)

            pe.wait_ge(s_ev, EV_AT["sumaw"])
            def y0(g, t):
                pe.wait_ge(s_y0e, g * GT + t + 1)
                for k in range(KT):
                    last = T.matmul(bank[t % 2][:, k * P:(k + 1) * P], xin[:, t, k * P:(k + 1) * P], mixbd[:, t],
                                    start=True, stop=True)
                last.then_inc(s_y0, 1)

            def z(g, t):
                pe.wait_ge(s_y0e, g * GT + t + 3)
                for k in range(KT):
                    last = T.matmul(bank[2 + t // SUP][:, (t % SUP) * AWN:(t % SUP + 1) * AWN],
                                    y0T[:, t % 2, k * P:(k + 1) * P], awT[:, k], start=(k == 0), stop=(k == KT - 1))
                last.then_inc(s_z1, 1)

            def mixed(g):
                pe.wait_ge(s_bd, g * BPT + BPT)
                pe.wait_ge(s_xin, g * 16 + 16)
                if not isinstance(g, int):
                    pe.wait_ge(s_cve, (g - 1) * GT + 2)
                    pe.wait_ge(s_ze, g * 2)
                y0(g, 0)
                for t in range(GT):
                    if t + 1 < GT:
                        y0(g, t + 1)
                    z(g, t)

            def delta(g):
                settle_wait(pe, (s_gm, g + 1), (wt_copied[0], g + 1), (wt_copied[1], g + 1))
                for h in range(2):
                    for t in range(SUP):
                        last = T.transpose(bank[4 + h][0:ER, t * P:(t + 1) * P], gmid[:, h * SUP + t], ident)
                    last.then_inc(s_gt, 1)
                for t in range(GT):
                    if t % SUP == 0:
                        pe.wait_ge(s_gte, g * 2 + t // SUP + 1)
                    pe.wait_ge(s_x1, g * GT + t + 1)
                    T.matmul(bank[6 + t % 2][:, :], gmidT[0:ER, t], bT[0:ER, 0], start=True, stop=True)\
                        .then_inc(s_dl, 1)

            def convolve(g, t):
                if t % SUP == 0:
                    pe.wait_ge(s_lo0, g * 2 + t // SUP + 1)
                pe.wait_ge(s_cve, g * GT + t + 1)
                n = 0
                for k in range(KTAP):
                    for wh, half in ((0, xh0), (0, xl0), (1, xh0)):
                        last = T.matmul(bank[t % 2][:, :], wbd[:, wh, k], half[:, t, k:k + H], start=(n == 0),
                                        stop=(n == 3 * KTAP - 1))
                        n += 1
                last.then_inc(s_cv, 1)

            mixed(0)
            pe.wait_ge(s_wbd, BPT)
            with pe.Fori(0, GROUPS - 1) as g:
                delta(g)
                mixed(g + 1)
                pe.wait_ge(s_y0e, g * GT + 2 * GT + 2)
                for t in range(GT):
                    convolve(g, t)
                for s in range(2):
                    turn(prep_a[2], g, s)
            delta(GROUPS - 1)
            for t in range(GT):
                convolve(GROUPS - 1, t)
                m = TURN_AFTER.get(t)
                if m is not None:
                    turn(prep_a[2], m // 2, m % 2)

            def x_turn(c, s):
                pe.wait_ge(xq_lo, c + 1)
                for t in range(SUP):
                    if t < 3:
                        pe.wait_ge(xq_ed, c * 3 + t + 1)
                    else:
                        pe.wait_ge(xq_ea, c + 1)
                    for b in range(8):
                        src = xhl[:, s, b // KT, t * H + (b % KT) * P:t * H + (b % KT + 1) * P]
                        last = T.transpose(b16(4 + t)[:, b * P:(b + 1) * P], src, id16[:, :])
                    last.then_inc(xq_t, 1)

            pe.wait_ge(wt_copied[0], U0 + 1)
            pe.wait_ge(wt_copied[1], U1 + 1)
            def product(w, m, rhs_of, dst):
                n = 0
                for k in range(KT):
                    for wh, xh in ((0, 0), (0, 1), (1, 0)):
                        blk = wh * KT + k
                        lhs = w[:, blk, m * P:(m + 1) * P] if isinstance(m, int) else w[:, blk, ds(m * P, P)]
                        last = T.matmul(dst, lhs, rhs_of(xh * KT + k), start=(n == 0), stop=(n == 3 * KT - 1))
                        n += 1
                return last

            def first_gate(c, s):
                settle_wait(pe, (xq_ed, c * 3 + 6), (xq_ea, c + 2), (g_ev, c + 3))
                product(wgT, 0, lambda b: xT[:, b, c * NC:(c + 1) * NC] if isinstance(c, int) else
                        xT[:, b, ds(c * NC, NC)], bank[s][:, :]).then_inc(g_mm, 1)

            pe.wait_ge(s_cve, GROUPS * GT + 2)
            x_turn(0, 0)
            with pe.Fori(0, (CHUNKS - 2) // 2) as i:
                for s in range(2):
                    x_turn(i * 2 + s + 1, 1 - s)
                    first_gate(i * 2 + s, s)
            x_turn(CHUNKS - 1, 1)
            first_gate(CHUNKS - 2, 0)
            first_gate(CHUNKS - 1, 1)

            def project(m, w, mm, ev, unit=None, after=UNIT_AFTER):
                for c in range(CHUNKS):
                    pe.wait_ge(ev, m * CHUNKS + c + 1)
                    product(w, m, lambda b: xT[:, b, c * NC:(c + 1) * NC], bank[c % 4][:, :]).then_inc(mm, 1)
                    if unit is not None and c in after:
                        slot = after[c]
                        turn(prep_b[2], unit + (U0, U1)[slot], slot)

            pe.wait_ge(g_ev, CHUNKS + 4)
            with pe.Fori(0, MT - 1) as i:
                project(i + 1, wgT, g_mm, g_ev, i)
            pe.wait_ge(g_ev, MT * CHUNKS + 4)
            project(0, wuT, u_mm, u_ev, MT - 1, LAST_UNIT_AFTER)
            pe.wait_ge(wt_copied[0], U0 + MT + 1)
            with pe.Fori(0, MT - 1) as i:
                project(i + 1, wuT, u_mm, u_ev)
            pe.wait_ge(wt_copied[1], U1 + MT + 1)

            for t in range(KT):
                pe.wait_ge(s_dg, t + 1)
                T.matmul(bank[7][:, t * P:(t + 1) * P], ones[:, :], dgS[:, :], start=True, stop=True)\
                    .then_inc(s_row, 1)

            def down(c, s):
                pe.wait_ge(s_dlo, c + 1)
                for t in range(SUP):
                    pe.wait_ge(s_dev, c * SUP + t + 1)
                    n = 0
                    for m in range(MT):
                        for vh, wh in ((0, 0), (0, 1), (1, 0)):
                            o_ = vh * CH + m * NC + t * P
                            last = T.matmul(bank[t][:, :], hd[:, s, o_:o_ + P], wdT[:, m, wh], start=(n == 0),
                                            stop=(n == 3 * MT - 1))
                            n += 1
                    last.then_inc(s_dmm, 1)

            pe.wait_ge(u_ev, MT * CHUNKS + 4)
            with pe.Fori(0, CHUNKS // 2) as i:
                for s in range(2):
                    down(i * 2 + s, s)


_INS = ["x", "cond_128", "fside_S_0", "L0_cond_W0", "L0_cond_b0", "L0_cond_W1", "L0_cond_b1", "L0_cond_W2",
        "L0_cond_b2", "L0_cond_weight", "L0_cond_bias_k", "L0_ffn_A", "L0_ffn_B", "L0_ffn_Wr", "L1_cond_weight",
        "L1_cond_c_weight", "L1_ffn_w_gate", "L1_ffn_w_up", "L1_ffn_w_down"]


def kernel(**inputs):
    import concourse.bacc as bacc
    from concourse.bass_utils import run_bass_kernel_spmd

    nc = bacc.Bacc("TRN2", target_bir_lowering=False, num_devices=1)
    arrays, args = {}, {}
    for name in _INS + ["consts"]:
        v = constants() if name == "consts" else np.ascontiguousarray(inputs[name])
        arrays[f"in_{name}"] = v
        args[name] = nc.dram_tensor(f"in_{name}", v.shape, mybir.dt.from_np(v.dtype), kind="ExternalInput").ap()
    result = nc.dram_tensor("out", (BATCH, CHAN, H), F32, kind="ExternalOutput").ap()
    build(nc, args, result)
    r = run_bass_kernel_spmd(nc, [arrays], core_ids=[0])
    return r.results[0]["out"]
```

```python
from contextlib import ExitStack

import numpy as np

import concourse.bass as bass
from concourse import mybir

ALU = mybir.AluOpType
ACT = mybir.ActivationFunctionType
AX = mybir.AxisListType
F32 = mybir.dt.float32
F16 = mybir.dt.float16
I32 = mybir.dt.int32
U16 = mybir.dt.uint16
RMAX = bass.bass_isa.ReduceOp.max
ds = bass.ds

P = 128
BATCH, CHAN, H = 128, 32, 512
TOK = BATCH * CHAN
TILES = TOK // P
BPT = P // CHAN
GT = 8
GROUPS = TILES // GT
SUP = 4
KTAP, PAD = 9, 4
KUP = 64.0
KT = H // P
EXP_N, TOPK, RANK, MIX_K = 4, 2, 16, 8
ER = EXP_N * RANK
AWN = ER + EXP_N
SCALE = 16.0 / 4.0
INNER = 1376
MT = -(-INNER // P)
INNER_P = MT * P
LAST = INNER - (MT - 1) * P
NC = 512
CHUNKS = TOK // NC
HALF = TOK // 2
SPILLED = 5
DC, DT = 256, 2
DCHUNKS = TOK // DC
CH = MT * DC
BLK = 32
NB = H // BLK
MAGIC = 1.5 * 2.0 ** 23
QMAX = 65535.0
WMAX = 7.0
TINY = 1e-12
WUP = 1024.0
VDN = 1.0 / 16.0
SIG_ONE = 65536.0


def constants():
    ident = np.eye(P, dtype=np.float32)
    b = np.arange(P)
    pick = (b[:, None] % BPT == b[None, :] // CHAN).astype(np.float32)
    tile_of = (b[:, None] // BPT == np.arange(TILES)[None, :]).astype(np.float32)
    e, j = np.meshgrid(np.arange(EXP_N), np.arange(EXP_N), indexing="ij")
    before = np.broadcast_to((j < e).astype(np.float32).reshape(1, -1), (P, EXP_N * EXP_N))
    after = np.broadcast_to((j > e).astype(np.float32).reshape(1, -1), (P, EXP_N * EXP_N))
    return np.ascontiguousarray(np.concatenate([ident, pick, tile_of, before, after], axis=1))


C_ID, C_PICK, C_TILE, C_BEF, C_AFT, C_END = 0, P, 2 * P, 2 * P + TILES, 2 * P + TILES + 16, 2 * P + TILES + 32

PE_SETUP = ["condT", "awT", "bT", "mixT", "cwT", "h1", "h2", "logits", "attT", "aggb", "ctx", "attrep", "sumaw"]
EV_SETUP = ["id16", "condT", "awT", "bT", "mixT", "cwT", "negmax", "att", "attT", "aggb", "attexp", "attrep",
            "sumaw", "ctx"]
PE_AT = {n: i + 1 for i, n in enumerate(PE_SETUP)}
EV_AT = {n: i + 1 for i, n in enumerate(EV_SETUP)}


def pick1(ap, i):
    if isinstance(i, int):
        return ap[:, i]
    one = ap[:, ds(i, 1)]
    return one.rearrange("p a b -> p (a b)") if len(one.shape) == 3 else one.rearrange("p a b c -> p (a b) c")


class Chain:

    def __init__(self, eng, sem):
        self.eng, self.sem, self.base, self.n = eng, sem, 0, 0

    def __call__(self, ins):
        ins.then_inc(self.sem, 1)
        self.n += 1
        return ins

    def settle(self):
        self.eng.wait_ge(self.sem, self.base + self.n)

    def then(self, ins):
        self(ins)
        self.settle()

    def start(self):
        self.base, self.n = self.base + self.n, 0
        return self.base

    def iteration(self, start, i, per):
        self.base, self.n = start + i * per, 0

    def end(self, start, count, per):
        assert self.n == per, (self.n, per)
        self.base, self.n = start + count * per, 0


def build(nc, a, out):
    with ExitStack() as ctx:
        def sb(name, shape, dt):
            return ctx.enter_context(nc.sbuf_tensor("sb_" + name, shape, dt))

        def sem(name):
            return ctx.enter_context(nc.semaphore(name))

        def dram(name, shape):
            return nc.dram_tensor(name, shape, F32, kind="Internal").ap()

        KB = 1024
        WT = 8 * INNER_P * 2
        O_A, O_B, O_WG, O_WU = 0, 64 * KB, 128 * KB, 128 * KB + WT
        arena = sb("arena", [P, (O_WU + WT) // 4], F32)
        wd_region = sb("wd_region", [P, WT // 4], F32)

        def view(region, off, shape, dt):
            size = int(np.prod(shape)) * (2 if dt in (F16, U16) else 4)
            assert off % 4 == 0 and size % 4 == 0
            v = region[:, off // 4:(off + size) // 4]
            if dt != F32:
                v = v.bitcast(dt)
            if len(shape) == 2:
                v = v.rearrange("p (a b) -> p a b", a=shape[0])
            if len(shape) == 3:
                v = v.rearrange("p (a b c) -> p a b c", a=shape[0], b=shape[1])
            return v

        at = lambda off, shape, dt: view(arena, off, shape, dt)

        wgT = at(O_WG, [8, INNER_P], F16)
        wuT = at(O_WU, [8, INNER_P], F16)
        wdT = view(wd_region, 0, [MT, 2, H], F16)
        wdT8 = view(wd_region, 0, [MT, 8, P], F16)
        xT = at(O_B, [8, TOK], F16)
        y1 = at(O_A, [TILES, H], F32)
        xin = at(O_B, [GT, H], F32)
        xres = at(O_B + 16 * KB, [GT, H], F32)
        PW = H + 2 * PAD
        xpair = [at(O_B + 32 * KB + i * GT * PW * 2, [GT, PW], F16) for i in range(2)]
        OWN = [slice(0, P // 2), slice(P // 2, P)]
        o = O_B + 32 * KB + GT * PW * 4
        mixbd = at(o, [GT, P], F32)
        o += GT * P * 4
        y0T = at(o, [2, H], F32)
        o += 2 * H * 4
        zbuf = at(o, [GT, AWN], F32)
        o += GT * AWN * 4
        zbias = at(o, [SUP, AWN], F32)
        o += SUP * AWN * 4
        gmid = at(o, [GT, ER], F32)
        assert o + GT * ER * 4 <= O_WG
        o = O_WU
        gmidT = at(o, [GT, P], F32)
        o += GT * P * 4
        mixtmp = at(o, [2, GT * CHAN], F32)
        o += 2 * GT * CHAN * 4
        mixacc = at(o, [1, GT * CHAN], F32)
        o += GT * CHAN * 4
        gate_t = at(o, [8, GT * 16], F32)
        o += 8 * GT * 16 * 4
        wk = at(o, [CHAN, KTAP], F32)
        o += CHAN * KTAP * 4
        mixT = at(o, [MIX_K, CHAN], F32)
        o += MIX_K * CHAN * 4
        attrep = at(o, [TILES, MIX_K], F32)
        o += TILES * MIX_K * 4
        awT = at(o, [KT, AWN], F32)
        o += KT * AWN * 4
        sumaw = at(o, [1, AWN], F32)
        o += AWN * 4
        bT = at(o, [1, H], F32)
        o += H * 4
        aggb = at(o, [1, TILES], F32)
        o += TILES * 4
        assert o <= O_WU + WT
        o = O_A
        cond = at(o, [1, P], F32)[:, 0]
        condT = at(o + 512, [1, P], F32)[:, 0]
        w0 = at(o + 1024, [1, P], F32)[:, 0]
        w1 = at(o + 1536, [1, P], F32)[:, 0]
        h1T = at(o + 2048, [1, P], F32)[:, 0]
        h2T = at(o + 2560, [1, P], F32)[:, 0]
        w2 = at(o + 3072, [1, MIX_K], F32)[:, 0]
        b2 = at(o + 3104, [1, MIX_K], F32)[:, 0]
        b01 = at(o + 3136, [1, 2], F32)[:, 0]
        side = at(o + 3144, [1, 1], F32)[:, 0]
        smx = at(o + 3148, [1, 4], F32)[:, 0]
        expv = at(o + 3164, [1, MIX_K], F32)[:, 0]
        att = at(o + 3196, [1, MIX_K], F32)[:, 0]
        biask = at(o + 3228, [1, CHAN], F32)[:, 0]
        attT = at(o + 3356, [1, P], F32)[:, 0]
        cw = at(o + 3868, [1, P], F32)[:, 0]
        cwT = at(o + 4380, [1, CHAN], F32)[:, 0]
        attexp = at(o + 4508, [TILES, MIX_K], F32)
        aw = at(o + 6144, [1, H], F32)[:, 0]
        bnat = at(o + 8192, [4, ER], F32)
        mixnat = at(o + 9216, [2, P], F32)
        def prep_buffers(region, o):
            return (view(region, o, [2, H], F32), view(region, o + 4 * KB, [2, H], F32),
                    view(region, o + 8 * KB, [2, 8 * P], F16), view(region, o + 12 * KB, [8, NB], F32))

        prep_a, prep_b = prep_buffers(wd_region, 0), prep_buffers(arena, O_A + 48 * KB)
        wbd = view(wd_region, 13 * KB, [2, KTAP, P // 2], F16)
        wdnat = at(O_A + 16 * KB, [KT, INNER], F32)
        xq = at(O_WU, [1, SUP * H], U16)[:, 0]
        xv = at(O_WU + 4 * KB, [2, SUP * H], F32)
        xhl = view(wd_region, 0, [2, 2, SUP * H], F16)
        gbuf = at(O_A, [2, TOK], F32)
        ubuf = at(O_A, [2, TOK], F32)
        graw = at(O_A + 32 * KB, [2, HALF], F32)
        gq = at(O_A + 48 * KB, [1, HALF], U16)[:, 0]
        sq = at(O_A + 52 * KB, [1, HALF], U16)[:, 0]
        sig = at(O_A + 56 * KB, [1, HALF], F32)[:, 0]
        nv = at(O_WG, [2, HALF], F32)
        R_OFF = O_B
        R_END = R_OFF + (MT - SPILLED) * TOK * 4
        kept = at(R_OFF, [MT - SPILLED, TOK], F32)
        pin = at(O_A, [2, HALF], F32)
        uin = at(O_A + 16 * KB, [2, HALF], F32)
        pinb, uinb = (kept[:, i].rearrange("p (a b) -> p a b", a=2) for i in (1, 2))
        pin9 = kept[:, 3].rearrange("p (a b) -> p a b", a=2)
        prod = kept[:, 0].rearrange("p (a b) -> p a b", a=2)
        qg = at(O_A + 32 * KB, [2, HALF], U16)
        qu = at(O_A + 40 * KB, [2, HALF], U16)
        vg = at(O_A + 48 * KB, [1, HALF], F32)[:, 0]
        vu = (at(O_A + 56 * KB, [1, HALF], F32)[:, 0], at(R_END, [1, HALF], F32)[:, 0])
        assert R_END + HALF * 4 <= O_WU + WT
        o = O_A
        pd = at(o, [2, SPILLED * DC], F32)
        o += 2 * SPILLED * DC * 4
        qd = at(o, [1, CH], U16)[:, 0]
        o += CH * 2
        vd = at(o, [1, CH], F32)[:, 0]
        o += CH * 4
        hd = at(o, [2, 2 * CH], F16)
        o += 2 * CH * 4
        ob = at(o, [2, DT * H], F32)
        o += 2 * DT * H * 4
        otmp = at(o, [2, H], F32)
        o += 2 * H * 4
        assert o <= R_OFF
        x1b = at(R_END, [2, DT * H], F32)
        assert R_END + 2 * DT * H * 4 <= O_WU + WT

        cst = sb("cst", [P, C_END], F32)
        id16 = sb("id16", [P, P], F16)
        ones = sb("ones", [P, P], F32)
        ctxcol = sb("ctxcol", [P, TILES], F32)
        gS = sb("gS", [P, MT], F32)
        uS = sb("uS", [P, MT], F32)
        dS = sb("dS", [P, KT], F32)
        dR = sb("dR", [P, KT], F32)
        rS = sb("rS", [P, 2, 1], F32)
        rowv = sb("rowv", [P, H], F32)
        dgS = sb("dgS", [P, P], F32)
        st_hi = sb("st_hi", [P, 2 * MT], F32)
        st_lo = sb("st_lo", [P, 2 * MT], F32)
        st = sb("st", [P, 5, 2], F32)
        red = sb("red", [P, 5, 2], F32)
        rg = sb("rg", [P, 5, 16], F32)
        vm = sb("vm", [P, 4], F32)
        vmq = sb("vmq", [P, 2], U16)
        st2 = sb("st2", [P, 2], F32)
        ident = cst[:, C_ID:C_ID + P]
        bank = [ctx.enter_context(nc.psum_tensor(f"bank{i}", [P, 512], F32)) for i in range(8)]

        X, G, U, S, O = range(5)
        SC, INV, ZP, NSC, NINV, NZP = 0, 1, 2, 3, 4, 12

        def par(which, col):
            return rg[:, which, col:col + 1]

        x1d = dram("x1_rows", (TOK, H))
        gd = dram("gate_raw", (MT, P, TOK))
        ud = dram("up_raw", (MT - 2, P, TOK))
        sd = dram("gated_raw", (MT - 1, P, TOK))
        od = dram("product_raw", (SPILLED, P, TOK))

        s_load = sem("setup_loaded")
        s_wk = sem("conv_weights_loaded")
        s_wdn = sem("down_rows_loaded")
        s_pe = sem("setup_pe")
        s_ev = sem("setup_evacuated")
        s_act = sem("setup_act")
        s_wbd = sem("conv_weights_split")
        s_hi0 = sem("x1_high")
        s_lo0 = sem("x1_low")
        s_zero = sem("zeroed")
        s_none = sem("carries_waits")
        dch = sem("vector_steps")
        pch = sem("pool_steps")
        s_xin = sem("xin_loaded")
        s_xres = sem("xres_loaded")
        s_bd = sem("mix_ready")
        s_y0 = sem("y0_done")
        s_y0e = sem("y0_evacuated")
        s_ze = sem("z_evacuated")
        s_d4 = sem("logits_shifted")
        s_exp = sem("gates_exp")
        s_gm = sem("gated_mid")
        s_gt = sem("gated_mid_turned")
        s_gte = sem("gated_mid_copied")
        s_dl = sem("delta_done")
        s_x1 = sem("x1_ready")
        s_x1o = sem("x1_stored")
        s_cv = sem("conv_done")
        s_cve = sem("conv_evacuated")
        wn_in = [sem(f"wn_loaded{i}") for i in range(2)]
        wn_used = [sem(f"wn_used{i}") for i in range(2)]
        hl_ready = [sem(f"w_split{i}") for i in range(2)]
        hl_turned = [sem(f"w_turned{i}") for i in range(2)]
        wt_copied = [sem(f"w_copied{i}") for i in range(2)]
        s_mixn = sem("setup_loaded_pool")
        s_side = sem("convolution_bias_loaded")
        s_z1 = sem("z_tile_done")
        s_dg = sem("diagonal_ready")
        s_row = sem("row_scales_done")
        s_ob = sem("out_ready")
        s_st = sem("stats_ready")
        s_red = sem("range_reduced")
        s_par = sem("range_known")
        s_vm = sem("largest_gate")
        s_vma = sem("largest_gate_act")
        xq_q = sem("x_quantised")
        xq_v = sem("x_integer")
        xq_hi = sem("x_high")
        xq_lo = sem("x_low")
        xq_t = sem("x_turned")
        xq_ed = sem("x_turned_copied_dve")
        xq_ea = sem("x_turned_copied_act")
        g_mm = sem("gate_mm")
        g_ev = sem("gate_evacuated")
        g_st = [sem(f"gate_stored{i}") for i in range(2)]
        g_rd = sem("gate_reduced")
        u_mm = sem("up_mm")
        u_ev = sem("up_evacuated")
        u_st = [sem(f"up_stored{i}") for i in range(2)]
        u_rd = sem("up_reduced")
        s_gin = [sem(f"gate_loaded{i}") for i in range(2)]
        s_gq = sem("gate_quantised")
        s_nv = sem("gate_integer")
        s_sig = sem("sigmoid_done")
        s_sq = sem("sigmoid_quantised")
        s_pr = sem("gated_ready")
        s_pst = [sem(f"gated_stored{i}") for i in range(2)]
        s_p9 = sem("late_gate_product_loaded")
        s_p5 = [sem(f"last_gate_product_loaded{i}") for i in range(2)]
        s_pinb = [sem(f"first_product_inputs_loaded{i}") for i in range(2)]
        s_pin = [sem(f"product_inputs_loaded{i}") for i in range(2)]
        s_q2g = sem("product_gate_quantised")
        s_q2u = sem("product_up_quantised")
        s_vg2 = sem("product_gate_integer")
        s_vu2 = sem("product_up_integer")
        s_po = sem("product_ready")
        s_pos = [sem(f"product_stored{i}") for i in range(2)]
        s_din = [sem(f"down_input_loaded{i}") for i in range(2)]
        s_dq = sem("down_quantised")
        s_dv = sem("down_integer")
        s_dhi = sem("down_high")
        s_dlo = sem("down_low")
        s_dmm = sem("down_mm")
        s_dev = sem("down_evacuated")
        s_x1i = [sem(f"x1_loaded{i}") for i in range(2)]
        s_out = [sem(f"out_stored{i}") for i in range(2)]

        N_SMALL = 15
        N_UP = (MT // 2, (MT - 2) // 2)
        N_SLOT = ((MT + 1) // 2, MT // 2)
        U0, U1 = N_SLOT

        PAIR_AFTER = {5: 0, 6: 1}
        GATED_AFTER = 3
        TURN_AFTER = {t: 2 * (GROUPS - 1) + k for k, t in enumerate((0, 1, 2, 3, 5))}
        assert max(TURN_AFTER.values()) == MT - 1

        UNIT_AFTER = {5: 0, 7: 1}
        LAST_UNIT_AFTER = {2: 0, 4: 1}

        def tile_of(k):
            return MT - 1 - k if k < 2 else k - 2 if k < SPILLED + 2 else MT - 3 - (k - SPILLED - 2)

        def settle_wait(eng, *waits):
            for s, v in waits:
                eng.wait_ge(s, v)
            eng.sem_inc(s_none, 1)

        MIX_STEPS = 14

        def mix(eng, E, pc, g):

            def part(k, dst, lo=0, n=P):
                rep = attrep[lo:lo + n, g * GT:(g + 1) * GT, k] if isinstance(g, int) else \
                    attrep[lo:lo + n, ds(g * GT, GT), k]
                s_ = [n, GT, CHAN]
                return E.tensor_tensor(dst, mixT[lo:lo + n, k].unsqueeze(1).broadcast_to(s_),
                                       rep.unsqueeze(2).broadcast_to(s_), ALU.mult)

            acc = mixacc[:, 0].rearrange("p (t o) -> p t o", t=GT)
            tmp = [mixtmp[:, j].rearrange("p (t o) -> p t o", t=GT) for j in range(2)]
            pc(part(0, acc))
            for k in range(1, MIX_K):
                pc.then(part(k, tmp[k % 2]))
                if k < MIX_K - 1:
                    pc(E.tensor_tensor(acc, acc, tmp[k % 2], ALU.add))
            pc.settle()
            if not isinstance(g, int):
                eng.wait_ge(s_y0, g * GT)
            for b in range(BPT):
                r = slice(CHAN * b, CHAN * (b + 1))
                E.tensor_tensor(mixbd[r, :, r], acc[r], tmp[(MIX_K - 1) % 2][r], ALU.add).then_inc(s_bd, 1)
            eng.wait_ge(s_bd, g * BPT + BPT)

        block = ctx.enter_context(nc.Block())

        @block.sync
        def _(sp):
            def small(dst, src):
                sp.dma_start(dst, src).then_inc(s_load, 16)

            small(cst[:, :], a["consts"])
            small(cond, a["cond_128"])
            small(w0, a["L0_cond_W0"])
            small(w1, a["L0_cond_W1"])
            small(w2, a["L0_cond_W2"])
            small(b01[:, 0:1], a["L0_cond_b0"].rearrange("(p a) -> p a", a=1))
            small(b01[:, 1:2], a["L0_cond_b1"].rearrange("(p a) -> p a", a=1))
            small(b2[0:1, :], a["L0_cond_b2"].rearrange("(a k) -> a k", a=1))
            small(biask[0:MIX_K, :], a["L0_cond_bias_k"])
            small(aw[0:ER, :], a["L0_ffn_A"].rearrange("e r f -> (e r) f"))
            small(aw[ER:AWN, :], a["L0_ffn_Wr"])
            for e in range(EXP_N):
                small(bnat.rearrange("p t (e r) -> p t e r", e=EXP_N)[:, :, e, :],
                      a["L0_ffn_B"][e].rearrange("(t p) r -> p t r", p=P))
            x_v = a["x"].rearrange("(t b) c h -> (b c) t h", b=BPT)
            sp.dma_start(xin, x_v[:, 0:GT, :]).then_inc(s_xin, 16)
            sp.dma_start(xres, x_v[:, 0:GT, :]).then_inc(s_xres, 16)
            sp.wait_ge(s_zero, 2)
            for j in range(BPT):
                for g in range(4):
                    r = 8 * g
                    sp.dma_start(wk[CHAN * j + r:CHAN * j + r + 8, r:r + 8, :],
                                 a["L1_cond_weight"][r:r + 8].rearrange("o i k -> i o k")).then_inc(s_wk, 16)
            wn, wg_v, wu_v = prep_a[0], a["L1_ffn_w_gate"], a["L1_ffn_w_up"]
            for s in range(2):
                sp.dma_start(wn[:, s], wg_v[s * P:(s + 1) * P, :]).then_inc(wn_in[s], 16)
            sp.dma_start(wdnat, a["L1_ffn_w_down"].rearrange("(t p) i -> p t i", p=P)).then_inc(s_wdn, 16)
            wd_v = a["L1_ffn_w_down"].rearrange("(t p) i -> p t i", p=P)

            rows = x1d.rearrange("(t p) h -> p t h", p=P)
            with sp.Fori(0, GROUPS - 1) as g:
                sp.wait_ge(s_y0, (g + 1) * GT)
                sp.dma_start(xin, x_v[:, ds((g + 1) * GT, GT), :]).then_inc(s_xin, 16)
                sp.wait_ge(s_x1, (g + 1) * GT + 2)
                sp.dma_start(rows[:, ds(g * GT, GT), :], xres).then_inc(s_x1o, 16)
                sp.wait_ge(s_lo0, g * 4 + 4)
                sp.wait_ge(s_x1o, g * 16 + 16)
                sp.dma_start(xres, x_v[:, ds((g + 1) * GT, GT), :]).then_inc(s_xres, 16)
                for s in range(2):
                    settle_wait(sp, (wn_used[s], g + 2))
                    sp.dma_start(wn[:, s], wg_v[ds(g * 2 * P + (2 + s) * P, P), :]).then_inc(wn_in[s], 16)
            sp.wait_ge(s_x1, GROUPS * GT + 2)
            sp.dma_start(rows[:, (GROUPS - 1) * GT:, :], xres).then_inc(s_x1o, 16)
            for m in range(2 * GROUPS, MT - 1):
                sp.wait_ge(wn_used[m % 2], m // 2 + 1)
                sp.dma_start(wn[:, m % 2], wg_v[m * P:(m + 1) * P, :]).then_inc(wn_in[m % 2], 16)
            sp.wait_ge(wn_used[0], (MT - 1) // 2 + 1)
            sp.dma_start(wn[0:LAST, 0], wg_v[(MT - 1) * P:INNER, :]).then_inc(wn_in[0], 16)
            wn = prep_b[0]
            wn3 = wn.rearrange("p s (t i) -> p s t i", t=KT)

            sp.wait_ge(xq_q, CHUNKS)
            for s in range(2):
                sp.sem_inc(g_st[s], 16)

            def load_units(m):
                settle_wait(sp, (wn_used[0], m + U0 + 1))
                sp.dma_start(wn[:, 0], wu_v[ds(m * P, P), :]).then_inc(wn_in[0], 16)
                settle_wait(sp, (wn_used[1], m + U1 + 1))
                sp.dma_start(wn3[:, 1], wd_v[:, :, ds(m * P, P)]).then_inc(wn_in[1], 16)

            def load_last_units():
                sp.wait_ge(wn_used[0], MT - 1 + U0 + 1)
                sp.dma_start(wn[0:LAST, 0], wu_v[(MT - 1) * P:INNER, :]).then_inc(wn_in[0], 16)
                sp.wait_ge(wn_used[1], MT - 1 + U1 + 1)
                sp.dma_start(wn3[:, 1, :, 0:LAST], wd_v[:, :, (MT - 1) * P:INNER]).then_inc(wn_in[1], 16)

            gd_v, ud_v, sd_v, od_v = (t.rearrange("m p t -> p m t") for t in (gd, ud, sd, od))

            def store_gate(m, slot):
                sp.wait_ge(g_ev, (m + 1) * CHUNKS + 4)
                sp.dma_start(pick1(gd_v, m), gbuf[:, slot]).then_inc(g_st[slot], 16)

            load_units(0)
            store_gate(0, 0)
            with sp.Fori(0, (MT - 3) // 2) as i:
                for s in range(2):
                    load_units(i * 2 + s + 1)
                    store_gate(i * 2 + s + 1, 1 - s)
            load_units(MT - 2)
            store_gate(MT - 2, 1)
            load_last_units()
            store_gate(MT - 1, 0)

            def load_gate(m, half):
                sp.wait_ge(s_gq, m * 2 + half - 1)
                sp.dma_start(graw[:, half], pick1(gd_v, m)[:, half * HALF:(half + 1) * HALF])\
                    .then_inc(s_gin[half], 16)

            def store_gated(m, half):
                settle_wait(sp, (s_pr, m * 2 + half + 1))
                sp.dma_start(pick1(sd_v, m)[:, half * HALF:(half + 1) * HALF], nv[:, half]).then_inc(s_pst[half], 16)

            def store_up(m, slot):
                sp.wait_ge(u_ev, (m + 1) * CHUNKS + 4)
                sp.dma_start(pick1(ud_v, m), ubuf[:, 1 - slot]).then_inc(u_st[slot], 16)

            def up_step(m, slot):
                load_gate(m, 1)
                store_gated(m - 1, 1)
                load_gate(m + 1, 0)
                store_gated(m, 0)
                store_up(m, slot)

            for s in (1, 0):
                sp.wait_ge(g_st[s], 16 + 16 * N_SLOT[s])
                sp.sem_inc(u_st[1 - s], 16)
                sp.sem_inc(s_pst[s], 16)
            for half in range(2):
                sp.dma_start(graw[:, half], gd_v[:, 0, half * HALF:(half + 1) * HALF]).then_inc(s_gin[half], 16)
            load_gate(1, 0)
            store_gated(0, 0)
            store_up(0, 0)
            with sp.Fori(0, (MT - 3) // 2) as i:
                for s in range(2):
                    up_step(i * 2 + s + 1, 1 - s)
            load_gate(MT - 2, 1)
            store_gated(MT - 3, 1)
            load_gate(MT - 1, 0)
            store_gated(MT - 2, 0)
            load_gate(MT - 1, 1)
            store_gated(MT - 2, 1)

            for s in range(2):
                sp.wait_ge(u_st[s], 16 + 16 * N_UP[s])
                sp.wait_ge(s_pst[s], 16 + 16 * (MT - 1))
                sp.sem_inc(s_pos[s], 16)
            sp.wait_ge(u_ev, MT * CHUNKS + 4)
            for half in range(2):
                sp.dma_start(pin9[:, half], sd_v[:, MT - 2, half * HALF:(half + 1) * HALF]).then_inc(s_p9, 16)

            def load_factor(src, m, half, dst, loaded):
                sp.dma_start(dst[:, half], src[:, m, half * HALF:(half + 1) * HALF]).then_inc(loaded[half], 16)

            def load_factors(m, half, gate, up, loaded):
                load_factor(sd_v, m, half, gate, loaded)
                load_factor(ud_v, m, half, up, loaded)

            def store_product(m, half):
                sp.wait_ge(s_po, (m + 2) * 2 + half + 3)
                sp.dma_start(od_v[:, m, half * HALF:(half + 1) * HALF], prod[:, half])\
                    .then_inc(s_pos[half], 16)

            for half in range(2):
                load_factors(0, half, pinb, uinb, s_pinb)
            for half in range(2):
                sp.wait_ge(s_q2g, 1 + half)
                load_factor(ud_v, 1, half, uin, s_pin)
            for half in range(2):
                sp.wait_ge(s_q2g, 3 + half)
                load_factor(sd_v, 1, half, pin, s_pin)
            for k in range(4, MT - 1):
                place = ((pinb, uinb, s_pinb), (pin, uin, s_pin))[k % 2]
                for half in range(2):
                    sp.wait_ge(s_q2g, (k - 2) * 2 + half + 1)
                    load_factors(tile_of(k), half, *place)
                if k - 4 < SPILLED:
                    for half in range(2):
                        store_product(k - 4, half)
            sp.wait_ge(s_po, (SPILLED + 2) * 2 + 3)
            for half in range(2):
                sp.wait_ge(s_pos[half], 16 + 16 * SPILLED)
                load_factor(sd_v, tile_of(MT - 1), half, prod, s_p5)
            for half in range(2):
                sp.wait_ge(s_q2g, (MT - 2) * 2 + half + 1)
                load_factor(ud_v, tile_of(MT - 1), half, uin, s_pin)

            out_v = out.rearrange("(t b) o h -> (b o) t h", b=BPT)

            def rows_of(v, c):
                return v[:, c * DT:(c + 1) * DT] if isinstance(c, int) else v[:, ds(c * DT, DT)]

            def load_chunk(c, slot):
                src = od_v[:, :, c * DC:(c + 1) * DC] if isinstance(c, int) else od_v[:, :, ds(c * DC, DC)]
                sp.dma_start(pd[:, slot].rearrange("p (m t) -> p m t", m=SPILLED), src).then_inc(s_din[slot], 16)

            def load_x1(c, slot):
                sp.dma_start(x1b[:, slot].rearrange("p (i h) -> p i h", i=DT), rows_of(rows, c))\
                    .then_inc(s_x1i[slot], 16)

            def store_out(c, slot):
                settle_wait(sp, (s_ob, c * DT + DT))
                sp.dma_start(rows_of(out_v, c), ob[:, slot].rearrange("p (i h) -> p i h", i=DT))\
                    .then_inc(s_out[slot], 16)

            sp.wait_ge(s_pos[0], 16 + 16 * SPILLED)
            sp.wait_ge(s_pos[1], 16 + 16 * SPILLED)
            sp.wait_ge(s_q2g, 2 * MT)
            for c in range(2):
                load_chunk(c, c)
            sp.wait_ge(s_par, 5)
            for c in range(2):
                sp.sem_inc(s_out[c], 16)
                load_x1(c, c)
            with sp.Fori(0, (DCHUNKS - 2) // 2) as i:
                for s in range(2):
                    settle_wait(sp, (s_dq, i * 4 + s * 2 + 1))
                    load_chunk(i * 2 + s + 2, s)
                    store_out(i * 2 + s, s)
                    load_x1(i * 2 + s + 2, s)
            for c in (DCHUNKS - 2, DCHUNKS - 1):
                store_out(c, c % 2)
            for s in range(2):
                sp.wait_ge(s_out[s], 16 + 16 * (DCHUNKS // 2))

        @block.vector
        def _(dve):
            ch = Chain(dve, dch)
            V = nc.vector

            ch(V.memset(wk.rearrange("p a b -> p (a b)"), 0.0))
            ch(V.memset(mixbd.rearrange("p a b -> p (a b)"), 0.0))
            for half in xpair:
                ch(V.memset(half[:, :, 0:PAD], 0.0))
                ch(V.memset(half[:, :, PAD + H:PW], 0.0))
            ch(V.memset(wbd.rearrange("p a b c -> p (a b c)"), 0.0))
            ch(V.memset(st2[:, :], -3.0e38))
            V.memset(ones[:, :], 1.0).then_inc(s_zero, 1)
            ch.settle()
            dve.sem_inc(s_zero, 1)
            for s in range(2):
                dve.sem_inc(wn_used[s], 1)
            dve.sem_inc(s_x1, 2)
            dve.sem_inc(xq_v, 1)
            dve.sem_inc(xq_ed, 3)
            dve.sem_inc(g_rd, 2)
            dve.sem_inc(u_rd, 2)
            dve.sem_inc(s_nv, 1)
            dve.sem_inc(s_sq, 1)
            dve.sem_inc(s_po, 2)
            dve.sem_inc(s_dv, 1)
            dve.sem_inc(s_dev, 4)

            dve.wait_ge(s_load, 16 * N_SMALL)
            V.tensor_copy(id16[:, :], ident).then_inc(s_ev, 1)
            dve.wait_ge(s_pe, PE_AT["condT"])
            V.tensor_copy(condT, bank[0][:, 0:P]).then_inc(s_ev, 1)
            dve.wait_ge(s_pe, PE_AT["awT"])
            V.tensor_copy(awT.rearrange("p a b -> p (a b)"), bank[1][:, 0:KT * AWN]).then_inc(s_ev, 1)
            dve.wait_ge(s_pe, PE_AT["bT"])
            V.tensor_scalar(bT[0:ER, 0], bank[2][0:ER, :], SCALE, None, ALU.mult).then_inc(s_ev, 1)
            dve.wait_ge(s_pe, PE_AT["mixT"])
            V.tensor_copy(mixT.rearrange("p a b -> p (a b)"), bank[3][:, 0:MIX_K * CHAN]).then_inc(s_ev, 1)
            dve.wait_ge(s_pe, PE_AT["cwT"])
            V.tensor_copy(cwT, bank[4][:, 0:CHAN]).then_inc(s_ev, 1)
            dve.wait_ge(s_pe, PE_AT["logits"])
            V.tensor_reduce(smx[:, 0:1], bank[7][:, 0:MIX_K], AX.X, ALU.max, negate=True).then_inc(s_ev, 1)
            dve.wait_ge(s_act, 3)
            ch.then(V.reciprocal(smx[:, 2:3], smx[:, 1:2]))
            V.tensor_scalar(att, expv, smx[:, 2:3], None, ALU.mult).then_inc(s_ev, 1)
            dve.wait_ge(s_pe, PE_AT["attT"])
            V.tensor_copy(attT[0:MIX_K, :], bank[0][0:MIX_K, 0:P]).then_inc(s_ev, 1)
            dve.wait_ge(s_pe, PE_AT["aggb"])
            V.tensor_copy(aggb[:, 0], bank[1][:, 0:TILES]).then_inc(s_ev, 1)
            dve.wait_ge(s_ev, EV_AT["att"])
            V.tensor_tensor(attexp, att.unsqueeze(1).broadcast_to([P, TILES, MIX_K]),
                            cst[:, C_TILE:C_TILE + TILES].unsqueeze(2).broadcast_to([P, TILES, MIX_K]), ALU.mult)\
                .then_inc(s_ev, 1)
            dve.wait_ge(s_pe, PE_AT["attrep"])
            V.tensor_copy(attrep.rearrange("p a b -> p (a b)"), bank[3][:, 0:TILES * MIX_K]).then_inc(s_ev, 1)
            dve.wait_ge(s_pe, PE_AT["sumaw"])
            V.tensor_copy(sumaw[:, 0], bank[4][:, 0:AWN]).then_inc(s_ev, 1)
            dve.wait_ge(s_ev, EV_AT["attrep"])
            mix(dve, V, ch, 0)
            dve.wait_ge(s_pe, PE_AT["ctx"])
            dve.wait_ge(s_side, 16 * BPT)
            V.tensor_scalar(ctxcol[:, :], bank[2][:, 0:TILES], side, None, ALU.add).then_inc(s_ev, 1)

            def power_of_two(dst, src):
                V_i = src.bitcast(I32)
                ch.then(V.tensor_scalar(dst.bitcast(I32), V_i, 0x7F800000, None, ALU.bitwise_and))

            dve.wait_ge(s_wdn, 16)
            ch.then(V.tensor_reduce(dR[:, :], wdnat, AX.X, ALU.max, apply_absolute_value=True))
            ch.then(V.tensor_scalar(dR[:, :], dR[:, :], 1.0 / WMAX, TINY, ALU.mult, ALU.max))
            power_of_two(dS[:, :], dR[:, :])
            ch.then(V.reciprocal(dR[:, :], dS[:, :]))
            ch.then(V.tensor_scalar(dR[:, :], dR[:, :], WUP, None, ALU.mult))

            PREP_G, PREP_D = 11, 7

            def prep(buffers, u, slot, norm, clear=False, factor=None):
                wn, wint, wsp, wsc = buffers
                w = wn[:, slot]
                wi = wint[:, slot]
                blocks = [NB, BLK]

                def b(v):
                    return v.unsqueeze(2).broadcast_to([P] + blocks)

                dve.wait_ge(wn_in[slot], (u + 1) * 16)
                ch.then(V.tensor_reduce(wsc[:, 0], w.rearrange("p (b k) -> p b k", k=BLK), AX.X, ALU.max,
                                        apply_absolute_value=True))
                ch.then(V.tensor_scalar(wsc[:, 1], wsc[:, 0], 1.0 / WMAX, TINY, ALU.mult, ALU.max))
                ch.then(V.reciprocal(wsc[:, 2], wsc[:, 1]))
                last = V.tensor_tensor(wi.rearrange("p (b k) -> p b k", k=BLK),
                                       w.rearrange("p (b k) -> p b k", k=BLK), b(wsc[:, 2]), ALU.mult)
                if clear:
                    ch.then(last)
                    pad = wn[LAST:P, 0] if slot == 0 else wn[:, 1].rearrange("p (t i) -> p t i", t=KT)[:, :, LAST:P]
                    last = V.memset(pad, 0.0)
                last.then_inc(wn_used[slot], 1)
                dve.wait_ge(wn_used[slot], u + 2)
                ch(V.tensor_scalar(wi, wi, MAGIC, MAGIC, ALU.add, ALU.subtract))
                if norm is not None:
                    ch.then(V.tensor_reduce(wsc[:, 4, 0:1], wsc[:, 1], AX.X, ALU.max))
                    power_of_two(wsc[:, 4, 1:2], wsc[:, 4, 0:1])
                    if factor is None:
                        ch(V.tensor_scalar(norm, wsc[:, 4, 1:2], 1.0, None, ALU.mult))
                    else:
                        ch(V.tensor_scalar(norm, wsc[:, 4, 1:2], factor, 1.0 / (WUP * VDN), ALU.mult, ALU.mult))
                    ch.then(V.reciprocal(rS[:, slot], wsc[:, 4, 1:2]))
                    ch.then(V.tensor_scalar(wsc[:, 3], wsc[:, 1], rS[:, slot], WUP, ALU.mult, ALU.mult))
                else:
                    ch.then(V.tensor_tensor(wsc[:, 3].rearrange("p (t b) -> p t b", t=KT),
                                            wsc[:, 1].rearrange("p (t b) -> p t b", t=KT),
                                            dR[:, :].unsqueeze(2).broadcast_to([P, KT, NB // KT]), ALU.mult))
                ch.then(V.tensor_tensor(wi.rearrange("p (b k) -> p b k", k=BLK),
                                        wi.rearrange("p (b k) -> p b k", k=BLK), b(wsc[:, 3]), ALU.mult))
                dve.wait_ge(hl_turned[slot], u + 1)
                ch.then(V.tensor_copy(wsp[:, slot, 0:H], wi))
                V.tensor_tensor(wsp[:, slot, H:2 * H], wi, wsp[:, slot, 0:H], ALU.subtract)\
                    .then_inc(hl_ready[slot], 1)

            dve.wait_ge(s_wk, 16 * 16)
            for half in range(2):
                for j in range(BPT):
                    r = slice(CHAN * j, CHAN * (j + 1))
                    src = wk[r].rearrange("p o k -> p k o")
                    cols = slice(CHAN * (j % 2), CHAN * (j % 2 + 1))
                    if half == 0:
                        ch(V.tensor_scalar(wbd[r, 0, :, cols], src, KUP, None, ALU.mult))
                    else:
                        V.scalar_tensor_tensor(wbd[r, 1, :, cols], src, KUP, wbd[r, 0, :, cols], ALU.mult,
                                               ALU.subtract).then_inc(s_wbd, 1)
                ch.settle()

            def z_out(g):
                for h in range(2):
                    rows = aggb[:, 0, h * SUP + g * GT:h * SUP + g * GT + SUP] if isinstance(g, int) else \
                        aggb[:, 0, ds(g * GT + h * SUP, SUP)]
                    ch.then(V.tensor_tensor(zbias, sumaw[:, 0].unsqueeze(1).broadcast_to([P, SUP, AWN]),
                                            rows.unsqueeze(2).broadcast_to([P, SUP, AWN]), ALU.mult))
                    dve.wait_ge(s_z1, g * GT + (h + 1) * SUP)
                    V.tensor_tensor(zbuf[:, h * SUP:(h + 1) * SUP],
                                    bank[2 + h][:, 0:SUP * AWN].rearrange("p (t n) -> p t n", t=SUP),
                                    zbias, ALU.add).then_inc(s_ze, 1)
                    dve.wait_ge(s_ze, g * 2 + h + 1)

            Z_STEPS, G_STEPS = 2, 12

            def gates(g):
                v = zbuf[:, :, ER:AWN]
                four = [P, GT, EXP_N, EXP_N]
                vj, ve = v.unsqueeze(2).broadcast_to(four), v.unsqueeze(3).broadcast_to(four)
                t4 = [gate_t[:, k, :].rearrange("p (t e j) -> p t e j", t=GT, e=EXP_N) for k in range(2)]
                flat = [gate_t[:, k, :].rearrange("p (t q) -> p t q", t=GT) for k in range(2)]
                masks = [cst[:, c:c + 16].unsqueeze(1).broadcast_to([P, GT, 16]) for c in (C_BEF, C_AFT)]
                small = [gate_t[:, k, 0:GT * EXP_N].rearrange("p (t e) -> p t e", t=GT) for k in range(2, 6)]
                rank, sel, d, ex = small
                m1, total = gate_t[:, 6, 0:GT], gate_t[:, 6, GT:2 * GT]
                inv = gate_t[:, 6, 2 * GT:3 * GT]
                by_e = lambda x: x.unsqueeze(2).broadcast_to([P, GT, EXP_N])
                ch(V.tensor_tensor(t4[0], vj, ve, ALU.is_ge))
                ch(V.tensor_tensor(t4[1], vj, ve, ALU.is_gt))
                ch.then(V.tensor_reduce(m1, v, AX.X, ALU.max))
                ch(V.tensor_tensor(flat[0], flat[0], masks[0], ALU.mult))
                ch(V.tensor_tensor(flat[1], flat[1], masks[1], ALU.mult))
                V.tensor_tensor(d, v, by_e(m1), ALU.subtract).then_inc(s_d4, 1)
                ch.settle()
                ch.then(V.tensor_tensor(flat[0], flat[0], flat[1], ALU.add))
                ch.then(V.tensor_reduce(rank, t4[0], AX.X, ALU.add))
                ch.then(V.tensor_scalar(sel, rank, TOPK - 0.5, None, ALU.is_lt))
                dve.wait_ge(s_exp, g + 1)
                ch.then(V.tensor_tensor(ex, ex, sel, ALU.mult))
                ch.then(V.tensor_reduce(total, ex, AX.X, ALU.add))
                ch.then(V.reciprocal(inv, total))
                ch.then(V.tensor_tensor(ex, ex, by_e(inv), ALU.mult))
                V.tensor_tensor(gmid.rearrange("p t (e r) -> p t e r", e=EXP_N),
                                zbuf[:, :, 0:ER].rearrange("p t (e r) -> p t e r", e=EXP_N),
                                ex.unsqueeze(3).broadcast_to([P, GT, EXP_N, RANK]), ALU.mult).then_inc(s_gm, 1)

            def add_delta(g):
                dve.wait_ge(s_xres, g * 16 + 16)
                for t in range(GT):
                    dve.wait_ge(s_dl, g * GT + t + 1)
                    V.tensor_tensor(xres[:, t], bank[6 + t % 2][:, :], xres[:, t], ALU.add).then_inc(s_x1, 1)
                for s in range(2):
                    settle_wait(dve, (s_hi0, g * 4 + s * 2 + 2))
                    ts = slice(s * SUP, (s + 1) * SUP)
                    for i in range(2):
                        V.tensor_tensor(xpair[i][OWN[1 - i], ts, PAD:PAD + H], xres[OWN[i], ts],
                                        xpair[i][OWN[i], ts, PAD:PAD + H], ALU.subtract).then_inc(s_lo0, 1)

            PARTS = ((0, 4), (4, 6), (6, GT))

            def y_range(g, part):
                lo, hi = PARTS[part]
                dve.wait_ge(s_cve, g * GT + hi + 2)
                v = y1[:, g * GT + lo:g * GT + hi] if isinstance(g, int) else y1[:, ds(g * GT + lo, hi - lo)]
                col = g * len(PARTS) + part
                col = slice(col, col + 1) if isinstance(g, int) else ds(col, 1)
                v = v.rearrange("p a b -> p (a b)")
                ch(V.tensor_reduce(st_hi[:, col], v, AX.X, ALU.max))
                ch(V.tensor_reduce(st_lo[:, col], v, AX.X, ALU.min))

            dve.wait_ge(s_ev, EV_AT["sumaw"])
            z_out(0)
            gates(0)
            start = ch.start()
            PER = Z_STEPS + G_STEPS + 4 + 2 * PREP_G
            with dve.Fori(0, GROUPS - 1) as g:
                ch.iteration(start, g, PER)
                add_delta(g)
                z_out(g + 1)
                gates(g + 1)
                for s in range(2):
                    prep(prep_a, g, s, gS[:, ds(g * 2 + s, 1)])
                for part in range(2):
                    y_range(g, part)
            ch.end(start, GROUPS - 1, PER)
            add_delta(GROUPS - 1)
            for m in range(2 * (GROUPS - 1), MT):
                prep(prep_a, m // 2, m % 2, gS[:, m:m + 1], clear=(m == MT - 3))
            for g in range(GROUPS - 1):
                y_range(g, 2)
            for part in range(3):
                y_range(GROUPS - 1, part)

            def known_range(which, n, k=None, negated=()):
                ch.settle()
                if n:
                    ch(V.tensor_reduce(st[:, which, 0:1], st_hi[:, 0:n], AX.X, ALU.max))
                    ch(V.tensor_reduce(st[:, which, 1:2], st_lo[:, 0:n], AX.X, ALU.min, negate=True))
                ch.settle()
                dve.sem_inc(s_st, 1)
                dve.wait_ge(s_red, which + 1)
                r = rg[:, which, 5:7]
                d, q, e, f, n_ = (rg[:, which, 7 + j:8 + j] for j in range(5))
                ch.then(V.tensor_scalar(r, red[:, which, :], 0.0, 1.0 if k is None else k, ALU.max, ALU.mult))
                ch.then(V.tensor_tensor(d, r[:, 0:1], r[:, 1:2], ALU.add))
                ch.then(V.tensor_scalar(q, d, 1.0 / QMAX, None, ALU.mult))
                ch.then(V.scalar_tensor_tensor(e, q, -65536.0, d, ALU.mult, ALU.add))
                ch.then(V.tensor_tensor(f, e, q, ALU.add))
                ch.then(V.scalar_tensor_tensor(n_, f, 1.0 / QMAX, q, ALU.mult, ALU.add))
                ch.then(V.tensor_scalar(par(which, SC), n_, TINY, None, ALU.max))
                ch.then(V.reciprocal(par(which, INV), par(which, SC)))
                ch.then(V.tensor_scalar(par(which, ZP), r[:, 1:2], par(which, INV), MAGIC, ALU.mult, ALU.add))
                ch.then(V.tensor_scalar(par(which, ZP), par(which, ZP), MAGIC, None, ALU.subtract))
                if k is not None:
                    ch.then(V.tensor_scalar(par(which, INV), par(which, INV), k, None, ALU.mult))
                for dst, src in negated:
                    ch.then(V.tensor_scalar(par(which, dst), par(which, src), -1.0, None, ALU.mult))

            known_range(X, len(PARTS) * GROUPS)
            dve.sem_inc(s_par, 1)
            ch.then(V.tensor_scalar(gS[:, :], gS[:, :], par(X, SC), 1.0 / (WUP * VDN), ALU.mult, ALU.mult))

            def x_integer(c, s):
                dve.wait_ge(xq_q, c + 1)
                dve.wait_ge(xq_hi, c + 1)
                if not (isinstance(c, int) and c < 2):
                    dve.wait_ge(xq_lo, c - 1)
                V.tensor_scalar(xv[:, s], xq, par(X, ZP), VDN, ALU.subtract, ALU.mult).then_inc(xq_v, 1)

            def x_low(c, s):
                dve.wait_ge(xq_hi, c + 3)
                dve.wait_ge(xq_t, c * SUP + SUP)
                V.tensor_tensor(xhl[:, s, 1], xv[:, s], xhl[:, s, 0], ALU.subtract).then_inc(xq_lo, 1)

            def x_copy(c):
                for t in range(3):
                    dve.wait_ge(xq_t, c * SUP + t + 1 + 2 * SUP)
                    tile = c * SUP + t
                    dst = xT[:, :, tile * P:(tile + 1) * P] if isinstance(c, int) else xT[:, :, ds(tile * P, P)]
                    src = bank[4 + t][:, :].bitcast(F16).rearrange("p (a b) -> p a b", a=8)
                    V.tensor_copy(dst, src).then_inc(xq_ed, 1)

            dve.wait_ge(s_x1o, 16 * GROUPS)
            dve.wait_ge(s_par, 1)
            x_integer(0, 0)
            x_low(0, 0)
            x_integer(1, 1)
            with dve.Fori(0, (CHUNKS - 2) // 2) as i:
                for s in range(2):
                    c = i * 2 + s + 1
                    x_low(c, 1 - s)
                    x_integer(c + 1, s)
                    x_copy(c - 1)
            x_low(CHUNKS - 1, 1)
            x_copy(CHUNKS - 2)
            x_copy(CHUNKS - 1)

            def raw_range(m, half, buf, slot, ev, rd):
                dve.wait_ge(ev, m * CHUNKS + (half + 1) * CHUNKS // 2 + 4)
                col = m * 2 + half
                col = slice(col, col + 1) if isinstance(m, int) else ds(col, 1)
                v = buf[:, slot, half * HALF:(half + 1) * HALF]
                ch(V.tensor_reduce(st_hi[:, col], v, AX.X, ALU.max))
                last = V.tensor_reduce(st_lo[:, col], v, AX.X, ALU.min)
                if half == 0:
                    ch(last)
                else:
                    last.then_inc(rd, 1)

            def gate_range(m, slot):
                for half in range(2):
                    raw_range(m, half, gbuf, slot, g_ev, g_rd)

            def units(m, clear=False):
                prep(prep_b, m + U0, 0, uS[:, m:m + 1] if isinstance(m, int) else uS[:, ds(m, 1)], clear,
                     factor=par(X, SC))
                prep(prep_b, m + U1, 1, None, clear)

            gate_range(0, 0)
            start = ch.start()
            PER = 2 * (PREP_G + PREP_D + 3)
            with dve.Fori(0, (MT - 3) // 2) as i:
                ch.iteration(start, i, PER)
                for s in range(2):
                    units(i * 2 + s)
                    gate_range(i * 2 + s + 1, 1 - s)
            ch.end(start, (MT - 3) // 2, PER)
            units(MT - 3)
            gate_range(MT - 2, 1)
            units(MT - 2, clear=True)
            units(MT - 1)
            gate_range(MT - 1, 0)
            dve.wait_ge(g_rd, 2 + MT)
            known_range(G, 2 * MT, negated=((NSC, SC),))
            dve.sem_inc(s_par, 1)

            dve.wait_ge(s_vma, 1)
            V.tensor_scalar(vm[:, 0:1], vmq[:, 0:1], -1.0, par(G, ZP), ALU.mult, ALU.add).then_inc(s_vm, 1)
            dve.wait_ge(s_vma, 2)
            ch.then(V.tensor_scalar(vmq[:, 1:2], vm[:, 1:2], SIG_ONE, None, ALU.mult))
            ch.then(V.tensor_tensor(vm[:, 2:3], vm[:, 0:1], vmq[:, 1:2], ALU.mult))
            ch.then(V.tensor_scalar(st[:, S, 0:1], vm[:, 2:3], -1.0, None, ALU.mult))

            def gated(m, half, beside=None, quantise=False):
                n = m * 2 + half
                dve.wait_ge(s_gq, n + 1)
                dve.wait_ge(s_pst[half], m * 16 + 16)
                V.tensor_scalar(nv[:, half], gq, -1.0, par(G, ZP), ALU.mult, ALU.add).then_inc(s_nv, 1)
                if beside is not None:
                    m_up, half_up, place = beside
                    raw_range(m_up, half_up, ubuf, place, u_ev, u_rd)
                if quantise:
                    dve.wait_ge(s_sig, n + 1)
                    V.tensor_scalar(sq, sig, SIG_ONE, None, ALU.mult).then_inc(s_sq, 1)
                settle_wait(dve, (s_sq, n + 2))
                V.tensor_tensor_reduce(nv[:, half], nv[:, half], sq, 1.0, st2[:, 0:1], ALU.mult, ALU.max,
                                       st2[:, 0:1]).then_inc(s_pr, 1)

            gated(0, 0, (0, 0, 1))
            start = ch.start()
            with dve.Fori(0, (MT - 3) // 2) as i:
                ch.iteration(start, i, 6)
                for s in range(2):
                    m = i * 2 + s + 1
                    gated(m - 1, 1, (m - 1, 1, 1 - s))
                    gated(m, 0, (m, 0, s))
            ch.end(start, (MT - 3) // 2, 6)
            gated(MT - 3, 1, (MT - 3, 1, 1), quantise=True)
            gated(MT - 2, 0, (MT - 2, 0, 0), quantise=True)
            gated(MT - 2, 1, quantise=True)
            gated(MT - 1, 0, (MT - 2, 1, 0), quantise=True)
            gated(MT - 1, 1, (MT - 1, 0, 1), quantise=True)
            raw_range(MT - 1, 1, ubuf, 1, u_ev, u_rd)
            dve.wait_ge(u_rd, 2 + MT)
            known_range(U, 2 * MT, negated=((NZP, ZP),))
            dve.sem_inc(s_par, 1)
            dve.wait_ge(s_pr, 2 * MT)
            ch(V.tensor_scalar(st[:, S, 1:2], st2[:, 0:1], 1.0, None, ALU.mult))
            ch.then(V.tensor_scalar(vm[:, 3:4], par(G, SC), 1.0 / SIG_ONE, None, ALU.mult))
            known_range(S, 0, k=vm[:, 3:4], negated=((NINV, INV),))
            dve.sem_inc(s_par, 1)

            def product(k, half, dst):
                n = k * 2 + half
                dve.wait_ge(s_q2g, n + 1)
                dve.wait_ge(s_po, n + 2)
                V.tensor_scalar(vg, qg[:, half], par(S, ZP), None, ALU.subtract).then_inc(s_vg2, 1)
                settle_wait(dve, (s_vg2, n + 1), (s_vu2, n + 1))
                V.tensor_tensor_reduce(dst, vg, vu[half], 1.0, st2[:, 1:2], ALU.mult, ALU.max,
                                       st2[:, 1:2]).then_inc(s_po, 1)
                dve.wait_ge(s_po, n + 3)
                col = slice(n, n + 1) if isinstance(n, int) else ds(n, 1)
                ch.then(V.tensor_reduce(st_lo[:, col], dst, AX.X, ALU.min))

            def keep(m, half):
                return pick1(kept, m - SPILLED)[:, half * HALF:(half + 1) * HALF]

            for k in range(2):
                for half in range(2):
                    product(k, half, keep(MT - 1 - k, half))
            start = ch.start()
            with dve.Fori(0, SPILLED) as m:
                ch.iteration(start, m, 2)
                for half in range(2):
                    settle_wait(dve, (s_pos[half], m * 16 + 16))
                    product(m + 2, half, prod[:, half])
            ch.end(start, SPILLED, 2)
            for k in range(SPILLED + 2, MT):
                for half in range(2):
                    if k == MT - 1:
                        dve.wait_ge(s_pos[half], 16 + 16 * SPILLED)
                    product(k, half, keep(tile_of(k), half))
            ch.then(V.tensor_tensor(vm[:, 3:4], par(S, SC), par(U, SC), ALU.mult))
            ch(V.tensor_reduce(st[:, O, 1:2], st_lo[:, 0:2 * MT], AX.X, ALU.min, negate=True))
            ch(V.tensor_scalar(st[:, O, 0:1], st2[:, 1:2], 1.0, None, ALU.mult))
            known_range(O, 0, k=vm[:, 3:4])
            dve.sem_inc(s_par, 1)

            def d_integer(c, s):
                settle_wait(dve, (s_dq, c * 2 + 2))
                dve.wait_ge(s_dhi, c + 1)
                V.tensor_scalar(vd, qd, par(O, ZP), VDN, ALU.subtract, ALU.mult).then_inc(s_dv, 1)
                dve.wait_ge(s_dhi, c + 2)
                dve.wait_ge(s_dmm, c * DT + DT)
                V.tensor_tensor(hd[:, s, CH:2 * CH], vd, hd[:, s, 0:CH], ALU.subtract).then_inc(s_dlo, 1)

            def d_out(c, s):
                for t in range(DT):
                    dve.wait_ge(s_dmm, c * DT + t + 1 + 2 * DT)
                    V.tensor_tensor(otmp[:, t % 2], bank[s * DT + t][:, :], rowv[:, :], ALU.mult).then_inc(s_dev, 1)
                    dve.wait_ge(s_dev, c * DT + t + 1 + 4)
                    V.tensor_tensor(ob[:, s, t * H:(t + 1) * H], otmp[:, t % 2], x1b[:, s, t * H:(t + 1) * H],
                                    ALU.add).then_inc(s_ob, 1)

            def d_room(pair, s):
                dve.wait_ge(s_x1i[s], pair * 16 + 16)
                dve.wait_ge(s_out[s], pair * 16 + 16)

            dve.wait_ge(s_par, 5)
            d_integer(0, 0)
            for t in range(KT):
                ch.then(V.tensor_scalar(dgS[:, :], ident, dS[:, t:t + 1], None, ALU.mult))
                dve.sem_inc(s_dg, 1)
                dve.wait_ge(s_row, t + 1)
            ch.then(V.tensor_scalar(rowv[:, :], bank[7][:, :], par(O, SC), 1.0 / (WUP * VDN), ALU.mult, ALU.mult))
            with dve.Fori(0, (DCHUNKS - 2) // 2) as i:
                for s in range(2):
                    c = i * 2 + s
                    d_integer(c + 1, 1 - s)
                    d_room(i, s)
                    d_out(c, s)
            d_integer(DCHUNKS - 1, 1)
            for s in range(2):
                d_room((DCHUNKS - 2) // 2, s)
                d_out(DCHUNKS - 2 + s, s)

        @block.scalar
        def _(act):
            A = nc.scalar
            act.wait_ge(s_zero, 2)
            act.sem_inc(xq_hi, 2)
            act.sem_inc(xq_ea, 1)
            act.sem_inc(s_y0e, 2)
            act.sem_inc(s_cve, 2)
            act.sem_inc(g_ev, 4)
            act.sem_inc(u_ev, 4)
            act.sem_inc(s_dhi, 1)
            for s in range(2):
                act.sem_inc(wt_copied[s], 1)
            A.activation(smx[:, 3:4], ones[:, 0:1], ACT.Gelu).then_inc(s_none, 1)
            act.wait_ge(s_pe, PE_AT["h1"])
            A.activation(h1T, bank[5][:, 0:P], ACT.Gelu, bias=b01[:, 0:1]).then_inc(s_act, 1)
            act.wait_ge(s_pe, PE_AT["h2"])
            A.activation(h2T, bank[6][:, 0:P], ACT.Gelu, bias=b01[:, 1:2]).then_inc(s_act, 1)
            act.wait_ge(s_ev, EV_AT["negmax"])
            A.activation(expv, bank[7][:, 0:MIX_K], ACT.Exp, bias=smx[:, 0:1], accum_out=smx[:, 1:2])\
                .then_inc(s_act, 1)

            def copy_weights(u, slot, dst):
                settle_wait(act, (hl_turned[slot], u + 2))
                A.activation(dst, bank[4 + slot][:, :].bitcast(F16).rearrange("p (a b) -> p a b", a=8), ACT.Copy)\
                    .then_inc(wt_copied[slot], 1)

            def y0_out(g, between=None):
                for t in range(GT):
                    act.wait_ge(s_y0, g * GT + t + 1)
                    if t >= 2:
                        act.wait_ge(s_z1, g * GT + t - 1)
                    A.activation(y0T[:, t % 2], bank[t % 2][:, :], ACT.Copy).then_inc(s_y0e, 1)
                    if between is not None and t in (1, 3):
                        between(t // 2)

            def gates_exp(g):
                act.wait_ge(s_d4, g + 1)
                A.activation(gate_t[:, 5, 0:GT * EXP_N], gate_t[:, 4, 0:GT * EXP_N], ACT.Exp).then_inc(s_exp, 1)

            def gmid_out(g):
                for h in range(2):
                    act.wait_ge(s_gt, g * 2 + h + 1)
                    A.activation(gmidT[0:ER, h * SUP:(h + 1) * SUP].rearrange("p a b -> p (a b)"),
                                 bank[4 + h][0:ER, :], ACT.Copy).then_inc(s_gte, 1)

            def x1_high(g, s, i):
                act.wait_ge(s_x1, g * GT + s * SUP + SUP + 2)
                ts = slice(s * SUP, (s + 1) * SUP)
                A.activation(xpair[i][OWN[i], ts, PAD:PAD + H], xres[OWN[i], ts], ACT.Copy).then_inc(s_hi0, 1)

            def conv_out(g, t):
                settle_wait(act, (s_cv, g * GT + t + 1))
                tile = g * GT + t
                bias = ctxcol[:, tile:tile + 1] if isinstance(g, int) else ctxcol[:, ds(tile, 1)]
                A.activation(pick1(y1, tile), bank[t % 2][:, :], ACT.Identity, bias=bias, scale=1.0 / KUP)\
                    .then_inc(s_cve, 1)

            act.wait_ge(s_ev, EV_AT["ctx"])
            y0_out(0)
            gates_exp(0)
            gmid_out(0)
            with act.Fori(0, GROUPS - 1) as g:
                for i in range(2):
                    x1_high(g, 0, i)
                y0_out(g + 1, lambda i: x1_high(g, 1, i))
                gates_exp(g + 1)
                for t in range(GT):
                    conv_out(g, t)
                    if t == GATED_AFTER:
                        gmid_out(g + 1)
                    if t in PAIR_AFTER:
                        s = PAIR_AFTER[t]
                        copy_weights(g, s, wgT[:, :, ds(g * 2 * P + s * P, P)])
            for s in range(2):
                for i in range(2):
                    x1_high(GROUPS - 1, s, i)
            for t in range(GT):
                conv_out(GROUPS - 1, t)
                m = TURN_AFTER.get(t)
                if m is not None:
                    copy_weights(m // 2, m % 2, wgT[:, :, m * P:(m + 1) * P])

            def x_quant(c):
                settle_wait(act, (xq_v, c + 1))
                v = y1[:, c * SUP:(c + 1) * SUP] if isinstance(c, int) else y1[:, ds(c * SUP, SUP)]
                A.activation(xq, v.rearrange("p a b -> p (a b)"), ACT.Identity, bias=par(X, ZP), scale=par(X, INV))\
                    .then_inc(xq_q, 1)

            def x_high(c, s):
                act.wait_ge(xq_v, c + 2)
                act.wait_ge(xq_t, c * SUP + SUP)
                A.activation(xhl[:, s, 0], xv[:, s], ACT.Copy).then_inc(xq_hi, 1)

            def x_copy(c):
                settle_wait(act, (xq_t, c * SUP + SUP + 2 * SUP))
                tile = c * SUP + SUP - 1
                dst = xT[:, :, tile * P:(tile + 1) * P] if isinstance(c, int) else xT[:, :, ds(tile * P, P)]
                A.activation(dst, bank[7][:, :].bitcast(F16).rearrange("p (a b) -> p a b", a=8), ACT.Copy)\
                    .then_inc(xq_ea, 1)

            def first_gate_out(c, s):
                settle_wait(act, (g_mm, c + 1))
                dst = gbuf[:, 0, c * NC:(c + 1) * NC] if isinstance(c, int) else gbuf[:, 0, ds(c * NC, NC)]
                A.activation(dst, bank[s][:, :], ACT.Copy, scale=gS[:, 0:1]).then_inc(g_ev, 1)

            act.wait_ge(s_par, 1)
            x_quant(0)
            x_high(0, 0)
            x_quant(1)
            x_high(1, 1)
            x_quant(2)
            x_copy(0)
            x_high(2, 0)
            x_quant(3)
            x_copy(1)
            with act.Fori(0, (CHUNKS - 4) // 2) as i:
                for s in range(2):
                    c = i * 2 + s + 3
                    x_high(c, 1 - s)
                    x_quant(c + 1)
                    x_copy(c - 1)
                    first_gate_out(c - 3, s)
            x_high(CHUNKS - 1, 1)
            x_copy(CHUNKS - 2)
            first_gate_out(CHUNKS - 4, 0)
            x_copy(CHUNKS - 1)
            for c in range(CHUNKS - 3, CHUNKS):
                first_gate_out(c, c % 2)

            def raw_out(pair, m, slot, c, buf, place, mm, ev, rd, stored, scale):
                if c == 0:
                    act.wait_ge(stored[slot], pair * 16 + 16)
                    act.wait_ge(rd, m + 1)
                settle_wait(act, (mm, m * CHUNKS + c + 1))
                col = scale[:, m:m + 1] if isinstance(m, int) else scale[:, ds(m, 1)]
                A.activation(buf[:, place, c * NC:(c + 1) * NC], bank[c % 4][:, :], ACT.Copy, scale=col)\
                    .then_inc(ev, 1)

            def copy_unit(m, slot):
                if slot == 0:
                    copy_weights(m + U0, 0, wuT[:, :, m * P:(m + 1) * P] if isinstance(m, int) else
                                 wuT[:, :, ds(m * P, P)])
                else:
                    copy_weights(m + U1, 1, wdT8[:, m] if isinstance(m, int) else
                                 wdT8[:, ds(m, 1)].rearrange("p a b c -> p (a b) c"))

            def gate_step(pair, slot):
                m = pair * 2 + slot
                for c in range(CHUNKS):
                    raw_out(pair, m, slot, c, gbuf, slot, g_mm, g_ev, g_rd, g_st, gS)
                    if c in UNIT_AFTER:
                        copy_unit(m - 1, UNIT_AFTER[c])

            with act.Fori(0, (MT - 1) // 2) as i:
                gate_step(i, 1)
                gate_step(i + 1, 0)

            def gate_quant(m, half):
                n = m * 2 + half
                act.wait_ge(s_gin[half], m * 16 + 16)
                act.wait_ge(s_nv, n + 1)
                A.activation(gq, graw[:, half], ACT.Identity, bias=par(G, ZP), scale=par(G, INV)).then_inc(s_gq, 1)

            def gate_sigmoid(m, half, quantise=True):
                n = m * 2 + half
                act.wait_ge(s_nv, n + 2)
                act.wait_ge(s_sq, n + 1)
                A.activation(sig, nv[:, half], ACT.Sigmoid, scale=par(G, NSC)).then_inc(s_sig, 1)
                if quantise:
                    act.wait_ge(s_sig, n + 1)
                    if not isinstance(n, int) or n > 0:
                        act.wait_ge(s_pr, n)
                    A.activation(sq, sig, ACT.Copy, scale=SIG_ONE).then_inc(s_sq, 1)

            def up_step(pair, slot, others=None):
                m = pair * 2 + slot
                for c in range(CHUNKS):
                    raw_out(pair, m, slot, c, ubuf, 1 - slot, u_mm, u_ev, u_rd, u_st, uS)
                    if others is not None:
                        for tile, half, quantise, sigmoid in others:
                            if c == quantise:
                                gate_quant(tile, half)
                            if c == sigmoid:
                                gate_sigmoid(tile, half, quantise=False)
                        continue
                    if isinstance(m, int) and m == 0:
                        if c in LAST_UNIT_AFTER:
                            copy_unit(MT - 1, LAST_UNIT_AFTER[c])
                        if c == 5:
                            act.wait_ge(s_par, 2)
                            A.activation(vmq[:, 0:1], par(G, 5), ACT.Identity, bias=par(G, ZP), scale=par(G, INV))\
                                .then_inc(s_vma, 1)
                            act.wait_ge(s_vm, 1)
                            A.activation(vm[:, 1:2], vm[:, 0:1], ACT.Sigmoid, scale=par(G, NSC)).then_inc(s_vma, 1)
                            for s in range(2):
                                act.wait_ge(g_st[s], 16 + 16 * N_SLOT[s])
                    elif c == 1:
                        gate_quant(m - 1, 1)
                    elif c == 3:
                        gate_sigmoid(m - 1, 1)
                    if c == 5:
                        gate_quant(m, 0)
                    if c == 7:
                        gate_sigmoid(m, 0)

            act.wait_ge(g_rd, 2 + MT - 1)
            up_step(0, 0)
            with act.Fori(0, (MT - 3) // 2) as i:
                up_step(i, 1)
                up_step(i + 1, 0)
            up_step((MT - 2) // 2, 1, others=((MT - 3, 1, 0, 1), (MT - 2, 0, 2, 4), (MT - 2, 1, 5, 6)))
            up_step((MT - 1) // 2, 0, others=((MT - 1, 0, 0, 1), (MT - 1, 1, 3, 5)))

            def factors(k, half, gate, up):
                n = k * 2 + half
                settle_wait(act, (s_po, n + 1))
                A.activation(qu[:, half], up, ACT.Identity, bias=par(U, ZP), scale=par(U, INV)).then_inc(s_q2u, 1)
                if isinstance(k, int) and k == 0:
                    act.wait_ge(s_par, 4)
                A.activation(qg[:, half], gate, ACT.Identity, bias=par(S, ZP), scale=par(S, NINV)).then_inc(s_q2g, 1)
                settle_wait(act, (s_q2u, n + 1))
                A.activation(vu[half], qu[:, half], ACT.Identity, bias=par(U, NZP)).then_inc(s_vu2, 1)

            act.wait_ge(s_par, 3)
            for half in range(2):
                factors(0, half, nv[:, half], ubuf[:, 1, half * HALF:(half + 1) * HALF])
            act.wait_ge(s_p9, 32)
            for half in range(2):
                factors(1, half, pin9[:, half], ubuf[:, 0, half * HALF:(half + 1) * HALF])
            for half in range(2):
                act.wait_ge(s_pinb[half], 32)
                factors(2, half, pinb[:, half], uinb[:, half])
            with act.Fori(0, (SPILLED + 1) // 2) as i:
                for half in range(2):
                    act.wait_ge(s_pin[half], i * 32 + 32)
                    factors(i * 2 + 3, half, pin[:, half], uin[:, half])
                for half in range(2):
                    act.wait_ge(s_pinb[half], i * 32 + 64)
                    factors(i * 2 + 4, half, pinb[:, half], uinb[:, half])
            for k in (MT - 2, MT - 1):
                for half in range(2):
                    act.wait_ge(s_pin[half], (SPILLED + 3) // 2 * 32 + (k - MT + 2) * 16)
                    if k == MT - 1:
                        act.wait_ge(s_p5[half], 16)
                    factors(k, half, (pin, prod)[k - MT + 2][:, half], uin[:, half])

            act.wait_ge(s_par, 5)
            with act.Fori(0, DCHUNKS // 2) as i:
                for s in range(2):
                    c = i * 2 + s
                    act.wait_ge(s_din[s], i * 16 + 16)
                    act.wait_ge(s_dv, c + 1)
                    A.activation(qd[:, 0:SPILLED * DC], pd[:, s], ACT.Identity, bias=par(O, ZP), scale=par(O, INV))\
                        .then_inc(s_dq, 1)
                    A.activation(qd[:, SPILLED * DC:].rearrange("p (m t) -> p m t", t=DC), kept[:, :, ds(c * DC, DC)],
                                 ACT.Identity, bias=par(O, ZP), scale=par(O, INV)).then_inc(s_dq, 1)
                    act.wait_ge(s_dv, c + 2)
                    act.wait_ge(s_dmm, c * DT + DT)
                    A.activation(hd[:, s, 0:CH], vd, ACT.Copy).then_inc(s_dhi, 1)

        @block.gpsimd
        def _(pool):
            G_ = nc.gpsimd
            pc = Chain(pool, pch)

            def load(dst, src, signal):
                pool.dma_start(dst, src).then_inc(signal, 16)

            load(cw[0:CHAN, :], a["L1_cond_c_weight"], s_mixn)
            mix_v = a["L0_cond_weight"].rearrange("k o i a -> (k o) (i a)").rearrange("(t p) i -> p t i", p=P)
            for j in range(BPT):
                load(mixnat[:, :, CHAN * j:CHAN * (j + 1)], mix_v, s_mixn)
            for j in range(BPT):
                load(side[CHAN * j:CHAN * (j + 1), :], a["fside_S_0"].rearrange("(p a) -> p a", a=1), s_side)

            pool.wait_ge(s_bd, BPT)
            start = pc.start()
            with pool.Fori(0, GROUPS - 1) as i:
                pc.iteration(start, i, MIX_STEPS)
                mix(pool, G_, pc, i + 1)
            pc.end(start, GROUPS - 1, MIX_STEPS)
            for which in (X, G, U, S, O):
                pool.wait_ge(s_st, which + 1)
                G_.partition_all_reduce(red[:, which, :], st[:, which, :], P, RMAX).then_inc(s_red, 1)

        @block.tensor
        def _(pe):
            T = nc.tensor
            for s in range(2):
                pe.sem_inc(hl_turned[s], 1)
            pe.sem_inc(xq_t, 2 * SUP)
            pe.sem_inc(s_dmm, 2 * DT)

            def b16(i):
                return bank[i][:, :].bitcast(F16)

            pe.wait_ge(s_load, 16 * N_SMALL)
            pe.wait_ge(s_mixn, 16 * 5)
            pe.wait_ge(s_zero, 2)
            T.transpose(bank[0][:, 0:P], cond, ident).then_inc(s_pe, 1)
            for t in range(KT):
                last = T.transpose(bank[1][:, t * AWN:(t + 1) * AWN], aw[0:AWN, t * P:(t + 1) * P],
                                   cst[0:AWN, C_ID:C_ID + AWN])
            last.then_inc(s_pe, 1)
            for t in range(4):
                last = T.transpose(bank[2][0:ER, t * P:(t + 1) * P], bnat[:, t], ident)
            last.then_inc(s_pe, 1)
            for t in range(2):
                last = T.transpose(bank[3][:, t * P:(t + 1) * P], mixnat[:, t], ident)
            last.then_inc(s_pe, 1)
            T.transpose(bank[4][:, 0:CHAN], cw[0:CHAN, :], cst[0:CHAN, C_ID:C_ID + CHAN]).then_inc(s_pe, 1)
            pe.wait_ge(s_ev, EV_AT["condT"])
            T.matmul(bank[5][:, 0:P], w0, condT, start=True, stop=True).then_inc(s_pe, 1)
            pe.wait_ge(s_act, 1)
            T.matmul(bank[6][:, 0:P], w1, h1T, start=True, stop=True).then_inc(s_pe, 1)
            pe.wait_ge(s_act, 2)
            T.matmul(bank[7][:, 0:MIX_K], h2T, w2, start=True, stop=False)
            T.matmul(bank[7][:, 0:MIX_K], ones[0:1, :], b2[0:1, :], start=False, stop=True).then_inc(s_pe, 1)
            pe.wait_ge(s_ev, EV_AT["att"])
            T.transpose(bank[0][0:MIX_K, 0:P], att, ident).then_inc(s_pe, 1)
            pe.wait_ge(s_ev, EV_AT["attT"])
            attT_v = attT[0:MIX_K, :].rearrange("k (q b) -> k b q", b=BPT)
            for b in range(BPT):
                last = T.matmul(bank[1][CHAN * b:CHAN * (b + 1), 0:TILES], biask[0:MIX_K, :], attT_v[:, b],
                                start=True, stop=True)
            last.then_inc(s_pe, 1)
            condT_v = condT.rearrange("d (t b) -> d b t", b=BPT)
            for b in range(BPT):
                last = T.matmul(bank[2][CHAN * b:CHAN * (b + 1), 0:TILES], cwT, condT_v[:, b], start=True, stop=True)
            last.then_inc(s_pe, 1)
            pe.wait_ge(s_ev, EV_AT["attexp"])
            T.matmul(bank[3][:, 0:TILES * MIX_K], cst[:, C_PICK:C_PICK + P], attexp.rearrange("p a b -> p (a b)"),
                     start=True, stop=True).then_inc(s_pe, 1)
            for t in range(KT):
                last = T.matmul(bank[4][:, 0:AWN], ones[:, :], awT[:, t], start=(t == 0), stop=(t == KT - 1))
            last.then_inc(s_pe, 1)

            def turn(wsp, u, slot):
                pe.wait_ge(hl_ready[slot], u + 1)
                pe.wait_ge(wt_copied[slot], u + 1)
                for b in range(8):
                    last = T.transpose(b16(4 + slot)[:, b * P:(b + 1) * P], wsp[:, slot, b * P:(b + 1) * P], id16[:, :])
                last.then_inc(hl_turned[slot], 1)

            pe.wait_ge(s_ev, EV_AT["ctx"])
            def y0(g, t):
                pe.wait_ge(s_y0e, g * GT + t + 1)
                for k in range(KT):
                    last = T.matmul(bank[t % 2][:, k * P:(k + 1) * P], xin[:, t, k * P:(k + 1) * P], mixbd[:, t],
                                    start=True, stop=True)
                last.then_inc(s_y0, 1)

            def z(g, t):
                pe.wait_ge(s_y0e, g * GT + t + 3)
                for k in range(KT):
                    last = T.matmul(bank[2 + t // SUP][:, (t % SUP) * AWN:(t % SUP + 1) * AWN],
                                    y0T[:, t % 2, k * P:(k + 1) * P], awT[:, k], start=(k == 0), stop=(k == KT - 1))
                last.then_inc(s_z1, 1)

            def mixed(g):
                pe.wait_ge(s_bd, g * BPT + BPT)
                pe.wait_ge(s_xin, g * 16 + 16)
                if not isinstance(g, int):
                    pe.wait_ge(s_cve, (g - 1) * GT + 2)
                    pe.wait_ge(s_ze, g * 2)
                y0(g, 0)
                for t in range(GT):
                    if t + 1 < GT:
                        y0(g, t + 1)
                    z(g, t)

            def turn_gated(g):
                if isinstance(g, int):
                    pe.wait_ge(s_gm, g + 1)
                else:
                    settle_wait(pe, (s_gm, g + 1), (wt_copied[0], g), (wt_copied[1], g))
                for h in range(2):
                    for t in range(SUP):
                        last = T.transpose(bank[4 + h][0:ER, t * P:(t + 1) * P], gmid[:, h * SUP + t], ident)
                    last.then_inc(s_gt, 1)

            def delta(g):
                for t in range(GT):
                    if t % SUP == 0:
                        pe.wait_ge(s_gte, g * 2 + t // SUP + 1)
                    pe.wait_ge(s_x1, g * GT + t + 1)
                    T.matmul(bank[6 + t % 2][:, :], gmidT[0:ER, t], bT[0:ER, 0], start=True, stop=True)\
                        .then_inc(s_dl, 1)

            def convolve(g, t):
                if t % SUP == 0:
                    pe.wait_ge(s_lo0, g * 4 + t // SUP * 2 + 2)
                pe.wait_ge(s_cve, g * GT + t + 1)
                for k in range(KTAP):
                    for i in range(2):
                        T.matmul(bank[t % 2][OWN[i], :], wbd[:, 0, k], xpair[i][:, t, k:k + H], start=(k == 0),
                                 stop=False)
                    for i in range(2):
                        last = T.matmul(bank[t % 2][OWN[i], :], wbd[OWN[i], 1, k], xpair[i][OWN[i], t, k:k + H],
                                        start=False, stop=(k == KTAP - 1))
                last.then_inc(s_cv, 1)

            mixed(0)
            pe.wait_ge(s_wbd, BPT)
            turn_gated(0)
            with pe.Fori(0, GROUPS - 1) as g:
                delta(g)
                mixed(g + 1)
                pe.wait_ge(s_y0e, g * GT + 2 * GT + 2)
                for t in range(GT):
                    convolve(g, t)
                    if t == GATED_AFTER:
                        turn_gated(g + 1)
                    if t in PAIR_AFTER:
                        pe.wait_ge(s_gte, g * 2 + 4)
                        turn(prep_a[2], g, PAIR_AFTER[t])
            delta(GROUPS - 1)
            for t in range(GT):
                convolve(GROUPS - 1, t)
                m = TURN_AFTER.get(t)
                if m is not None:
                    turn(prep_a[2], m // 2, m % 2)

            def x_turn(c, s):
                pe.wait_ge(xq_lo, c + 1)
                for t in range(SUP):
                    if t < 3:
                        pe.wait_ge(xq_ed, c * 3 + t + 1)
                    else:
                        pe.wait_ge(xq_ea, c + 1)
                    for b in range(8):
                        src = xhl[:, s, b // KT, t * H + (b % KT) * P:t * H + (b % KT + 1) * P]
                        last = T.transpose(b16(4 + t)[:, b * P:(b + 1) * P], src, id16[:, :])
                    last.then_inc(xq_t, 1)

            pe.wait_ge(wt_copied[0], U0 + 1)
            pe.wait_ge(wt_copied[1], U1 + 1)
            def product(w, m, rhs_of, dst):
                n = 0
                for k in range(KT):
                    for wh, xh in ((0, 0), (0, 1), (1, 0)):
                        blk = wh * KT + k
                        lhs = w[:, blk, m * P:(m + 1) * P] if isinstance(m, int) else w[:, blk, ds(m * P, P)]
                        last = T.matmul(dst, lhs, rhs_of(xh * KT + k), start=(n == 0), stop=(n == 3 * KT - 1))
                        n += 1
                return last

            def first_gate(c, s):
                settle_wait(pe, (xq_ed, c * 3 + 6), (xq_ea, c + 2), (g_ev, c + 3))
                product(wgT, 0, lambda b: xT[:, b, c * NC:(c + 1) * NC] if isinstance(c, int) else
                        xT[:, b, ds(c * NC, NC)], bank[s][:, :]).then_inc(g_mm, 1)

            pe.wait_ge(s_cve, GROUPS * GT + 2)
            x_turn(0, 0)
            with pe.Fori(0, (CHUNKS - 2) // 2) as i:
                for s in range(2):
                    x_turn(i * 2 + s + 1, 1 - s)
                    first_gate(i * 2 + s, s)
            x_turn(CHUNKS - 1, 1)
            first_gate(CHUNKS - 2, 0)
            first_gate(CHUNKS - 1, 1)

            def project(m, w, mm, ev, unit=None, after=UNIT_AFTER):
                for c in range(CHUNKS):
                    pe.wait_ge(ev, m * CHUNKS + c + 1)
                    product(w, m, lambda b: xT[:, b, c * NC:(c + 1) * NC], bank[c % 4][:, :]).then_inc(mm, 1)
                    if unit is not None and c in after:
                        slot = after[c]
                        turn(prep_b[2], unit + (U0, U1)[slot], slot)

            pe.wait_ge(g_ev, CHUNKS + 4)
            with pe.Fori(0, MT - 1) as i:
                project(i + 1, wgT, g_mm, g_ev, i)
            pe.wait_ge(g_ev, MT * CHUNKS + 4)
            project(0, wuT, u_mm, u_ev, MT - 1, LAST_UNIT_AFTER)
            pe.wait_ge(wt_copied[0], U0 + MT + 1)
            with pe.Fori(0, MT - 1) as i:
                project(i + 1, wuT, u_mm, u_ev)
            pe.wait_ge(wt_copied[1], U1 + MT + 1)

            for t in range(KT):
                pe.wait_ge(s_dg, t + 1)
                T.matmul(bank[7][:, t * P:(t + 1) * P], ones[:, :], dgS[:, :], start=True, stop=True)\
                    .then_inc(s_row, 1)

            def down(c, s):
                pe.wait_ge(s_dlo, c + 1)
                for t in range(DT):
                    pe.wait_ge(s_dev, c * DT + t + 1)
                    n = 0
                    for m in range(MT):
                        for vh, wh in ((0, 0), (0, 1), (1, 0)):
                            o_ = vh * CH + m * DC + t * P
                            last = T.matmul(bank[s * DT + t][:, :], hd[:, s, o_:o_ + P], wdT[:, m, wh],
                                            start=(n == 0), stop=(n == 3 * MT - 1))
                            n += 1
                    last.then_inc(s_dmm, 1)

            pe.wait_ge(u_ev, MT * CHUNKS + 4)
            with pe.Fori(0, DCHUNKS // 2) as i:
                for s in range(2):
                    down(i * 2 + s, s)


_INS = ["x", "cond_128", "fside_S_0", "L0_cond_W0", "L0_cond_b0", "L0_cond_W1", "L0_cond_b1", "L0_cond_W2",
        "L0_cond_b2", "L0_cond_weight", "L0_cond_bias_k", "L0_ffn_A", "L0_ffn_B", "L0_ffn_Wr", "L1_cond_weight",
        "L1_cond_c_weight", "L1_ffn_w_gate", "L1_ffn_w_up", "L1_ffn_w_down"]


def kernel(**inputs):
    import concourse.bacc as bacc
    from concourse.bass_utils import run_bass_kernel_spmd

    nc = bacc.Bacc("TRN2", target_bir_lowering=False, num_devices=1)
    arrays, args = {}, {}
    for name in _INS + ["consts"]:
        v = constants() if name == "consts" else np.ascontiguousarray(inputs[name])
        arrays[f"in_{name}"] = v
        args[name] = nc.dram_tensor(f"in_{name}", v.shape, mybir.dt.from_np(v.dtype), kind="ExternalInput").ap()
    result = nc.dram_tensor("out", (BATCH, CHAN, H), F32, kind="ExternalOutput").ap()
    build(nc, args, result)
    r = run_bass_kernel_spmd(nc, [arrays], core_ids=[0])
    return r.results[0]["out"]
```
